# Optimizing a Trainium2 kernel written in Bass

```python
import numpy as np
import jax
import jax.numpy as jnp

def _softmax(x, axis=-1):
    return jax.nn.softmax(x, axis=axis)

def _gelu(x):
    return jax.nn.gelu(x, approximate=True)

def _silu(x):
    return jax.nn.silu(x)

def _sigmoid(x):
    return jax.nn.sigmoid(x)

def _layernorm(x, axis=-1, eps=1e-05):
    m = jnp.mean(x, axis=axis, keepdims=True)
    v = jnp.var(x, axis=axis, keepdims=True)
    return (x - m) / jnp.sqrt(v + eps)

def _scatter_add(tgt, idx, src, axis=0):
    return tgt.at[idx].add(src)

def _segment_sum(src, seg, n):
    return jax.ops.segment_sum(src, seg, n)
kernel_name = 'mk_gnn_resnorm_d4_gnn_r8_438682'

def setup_inputs(seed: int=0):
    np.random.seed(seed)
    _w = jnp.asarray

    def _rec_inputs():
        import jax
        import jax.numpy as jnp
        _gk = jax.random.key(seed)
        x = -0.0005121 + 1.001 * jax.random.normal(jax.random.fold_in(_gk, 1), (12500, 64), jnp.float32)
        src = jax.random.randint(jax.random.fold_in(_gk, 2), (200000,), 0, 12500, jnp.int32)
        dst = jax.random.randint(jax.random.fold_in(_gk, 3), (200000,), 0, 12500, jnp.int32)
        _o = jnp.argsort(dst, stable=True)
        src = src[_o]
        dst = dst[_o]
        edge_type_9 = jax.random.randint(jax.random.fold_in(_gk, 12), (200000,), 0, 9, jnp.int32)
        edge_weight = jax.random.uniform(jax.random.fold_in(_gk, 13), (200000,), jnp.float32, 0.0, 0.999998)
        return (x, src, dst, edge_type_9, edge_weight)
    x, src, dst, edge_type_9, edge_weight = _rec_inputs()

    def _L0_gnn_setup():
        import jax, jax.numpy as jnp
        import numpy as np
        N = 6250
        E = 100000
        IN = 64
        OUT = 64

        def gcn_conv(x, w, b, row, col, ew, n):
            h = x @ w
            deg = jax.ops.segment_sum(ew, col, num_segments=n)
            dinv = jnp.where(deg > 0, jax.lax.rsqrt(deg), 0.0)
            norm = dinv[row] * ew * dinv[col]
            out = jax.ops.segment_sum(norm[:, None] * h[row], col, num_segments=n)
            return out + b
        key = jax.random.key(seed)
        ks = jax.random.split(key, 8)
        x = jax.random.normal(ks[0], (N, IN), dtype=jnp.float32)
        edge_index = jax.random.randint(ks[1], (2, E), 0, N)
        edge_attr = jax.random.uniform(ks[2], (E,), dtype=jnp.float32)

        def lin(k, i, o):
            return (jax.random.normal(k, (i, o), dtype=jnp.float32) / np.sqrt(i)).astype(jnp.float32)
        return {'x': x, 'edge_index': edge_index, 'edge_attr': edge_attr, 'w1': lin(ks[3], IN, 16), 'b1': jnp.zeros((16,), jnp.float32), 'w2': lin(ks[4], 16, 32), 'b2': jnp.zeros((32,), jnp.float32), 'w3': lin(ks[5], 32, IN), 'b3': jnp.zeros((IN,), jnp.float32), 'lw': lin(ks[6], 2 * IN, OUT), 'lb': jnp.zeros((OUT,), jnp.float32)}
    _L0_gnn_all = _L0_gnn_setup()
    _L0_gnn_in = {k: v for k, v in _L0_gnn_all.items() if k in ('w1', 'b1', 'w2', 'b2', 'w3', 'b3', 'lw', 'lb')}
    del _L0_gnn_all

    def _L1_gnn_setup():
        import jax, jax.numpy as jnp
        import numpy as np
        N_NODES = 12500
        N_EDGES = 200000
        N_FEAT = 64
        EPS = 1e-08
        key = jax.random.key(seed)
        kx, ke = jax.random.split(key)
        x = jax.random.normal(kx, (N_NODES, N_FEAT), dtype=jnp.float32)
        edge_index = jax.random.randint(ke, (2, N_EDGES), 0, N_NODES, dtype=jnp.int32)
        return {'x': x, 'edge_index': edge_index}
    _L1_gnn_all = _L1_gnn_setup()
    _L1_gnn_in = {k: v for k, v in _L1_gnn_all.items() if k in ()}
    del _L1_gnn_all

    def _L2_gnn_setup():
        import jax, jax.numpy as jnp
        import numpy as np
        NEG_SLOPE = 0.3
        BN_EPS = 1e-05
        key = jax.random.key(seed)
        k1, k2, k3, k4 = jax.random.split(key, 4)
        N, E, IN_DIM, OUT_DIM = (6250, 100000, 64, 64)
        feature = jax.random.normal(k1, (N, IN_DIM), dtype=jnp.float32)
        edge_index = jax.random.randint(k2, (2, E), 0, N, dtype=jnp.int64)
        lim = 1.0 / np.sqrt(2 * IN_DIM)
        W = jax.random.uniform(k3, (OUT_DIM, 2 * IN_DIM), minval=-lim, maxval=lim, dtype=jnp.float32)
        b = jax.random.uniform(k4, (OUT_DIM,), minval=-lim, maxval=lim, dtype=jnp.float32)
        gamma = jnp.ones((OUT_DIM,), dtype=jnp.float32)
        beta = jnp.zeros((OUT_DIM,), dtype=jnp.float32)
        return {'feature': feature, 'edge_index': edge_index, 'W': W, 'b': b, 'gamma': gamma, 'beta': beta}
    _L2_gnn_all = _L2_gnn_setup()
    _L2_gnn_in = {k: v for k, v in _L2_gnn_all.items() if k in ('W', 'b', 'gamma', 'beta')}
    del _L2_gnn_all

    def _L3_gnn_setup():
        import jax, jax.numpy as jnp
        import numpy as np
        N_NODES = 12500
        HIDDEN = 64
        N_REL = 9
        N_LAYERS = 3
        N_EDGES = 125000
        key = jax.random.key(seed)
        k1, k2, k3, k4, k5 = jax.random.split(key, 5)
        edge_index = jax.random.randint(k1, (2, N_EDGES), 0, N_NODES, dtype=jnp.int64)
        edge_type = jax.random.randint(k2, (N_EDGES,), 0, N_REL, dtype=jnp.int64)
        embeddings = jax.random.uniform(k3, (N_NODES, HIDDEN), dtype=jnp.float32)
        weights = jax.random.uniform(k4, (N_LAYERS, 2 * N_REL, HIDDEN, HIDDEN), dtype=jnp.float32)
        biases = jax.random.uniform(k5, (N_LAYERS, 2 * N_REL, HIDDEN), dtype=jnp.float32)
        return {'edge_index': edge_index, 'edge_type': edge_type, 'embeddings': embeddings, 'weights': weights, 'biases': biases}
    _L3_gnn_all = _L3_gnn_setup()
    _L3_gnn_in = {k: v for k, v in _L3_gnn_all.items() if k in ('weights', 'biases')}
    del _L3_gnn_all
    return {'x': x, 'src': src, 'dst': dst, 'edge_type_9': edge_type_9, 'edge_weight': edge_weight, 'L0_gnn_w1': _L0_gnn_in['w1'], 'L0_gnn_b1': _L0_gnn_in['b1'], 'L0_gnn_w2': _L0_gnn_in['w2'], 'L0_gnn_b2': _L0_gnn_in['b2'], 'L0_gnn_w3': _L0_gnn_in['w3'], 'L0_gnn_b3': _L0_gnn_in['b3'], 'L0_gnn_lw': _L0_gnn_in['lw'], 'L0_gnn_lb': _L0_gnn_in['lb'], 'L2_gnn_W': _L2_gnn_in['W'], 'L2_gnn_b': _L2_gnn_in['b'], 'L2_gnn_gamma': _L2_gnn_in['gamma'], 'L2_gnn_beta': _L2_gnn_in['beta'], 'L3_gnn_weights': _L3_gnn_in['weights'], 'L3_gnn_biases': _L3_gnn_in['biases']}

def reference(x, src, dst, edge_type_9, edge_weight, L0_gnn_w1, L0_gnn_b1, L0_gnn_w2, L0_gnn_b2, L0_gnn_w3, L0_gnn_b3, L0_gnn_lw, L0_gnn_lb, L2_gnn_W, L2_gnn_b, L2_gnn_gamma, L2_gnn_beta, L3_gnn_weights, L3_gnn_biases):
    import jax
    import jax.numpy as jnp

    def _L0_gnn_ref(x, edge_index, edge_attr, w1, b1, w2, b2, w3, b3, lw, lb):
        import jax, jax.numpy as jnp
        import numpy as np
        N = 6250
        E = 100000
        IN = 64
        OUT = 64

        def gcn_conv(x, w, b, row, col, ew, n):
            h = x @ w
            deg = jax.ops.segment_sum(ew, col, num_segments=n)
            dinv = jnp.where(deg > 0, jax.lax.rsqrt(deg), 0.0)
            norm = dinv[row] * ew * dinv[col]
            out = jax.ops.segment_sum(norm[:, None] * h[row], col, num_segments=n)
            return out + b
        n = x.shape[0]
        loop = jnp.arange(n)
        row = jnp.concatenate([edge_index[0], loop])
        col = jnp.concatenate([edge_index[1], loop])
        ew = jnp.concatenate([edge_attr, jnp.ones((n,), edge_attr.dtype)])
        x2 = jax.nn.relu(gcn_conv(x, w1, b1, row, col, ew, n))
        x3 = jax.nn.relu(gcn_conv(x2, w2, b2, row, col, ew, n))
        x4 = jax.nn.relu(gcn_conv(x3, w3, b3, row, col, ew, n))
        h = jnp.concatenate([x, x4], axis=1)
        return h @ lw + lb

    def _L1_gnn_ref(x, edge_index):
        import jax, jax.numpy as jnp
        import numpy as np
        N_NODES = 12500
        N_EDGES = 200000
        N_FEAT = 64
        EPS = 1e-08
        src = edge_index[0]
        tgt = edge_index[1]
        num_nodes = x.shape[0]
        messages = jnp.take(x, src, axis=0)
        ones = jnp.ones((messages.shape[0], 1), dtype=messages.dtype)
        count = jax.ops.segment_sum(ones, tgt, num_segments=num_nodes)
        sum_msgs = jax.ops.segment_sum(messages, tgt, num_segments=num_nodes)
        safe_count = jnp.maximum(count, jnp.asarray(EPS, dtype=count.dtype))
        mean = sum_msgs / safe_count
        mean_per_edge = jnp.take(mean, tgt, axis=0)
        squared_diff = jnp.square(messages - mean_per_edge)
        sum_sq = jax.ops.segment_sum(squared_diff, tgt, num_segments=num_nodes)
        variance = sum_sq / safe_count
        std_dev = jnp.sqrt(jnp.maximum(variance, jnp.zeros_like(variance)))
        std_dev = jnp.where(count <= 1, jnp.zeros_like(std_dev), std_dev)
        return std_dev

    def _L2_gnn_ref(feature, edge_index, W, b, gamma, beta):
        import jax, jax.numpy as jnp
        import numpy as np
        NEG_SLOPE = 0.3
        BN_EPS = 1e-05
        N = feature.shape[0]
        src, dst = (edge_index[0], edge_index[1])
        x_i = feature[dst]
        x_j = feature[src]
        msg_in = jnp.concatenate([x_i, x_j - x_i], axis=-1)
        h = msg_in @ W.T + b
        mean = jnp.mean(h, axis=0)
        var = jnp.var(h, axis=0)
        h = (h - mean) * jax.lax.rsqrt(var + BN_EPS) * gamma + beta
        h = jnp.where(h >= 0, h, NEG_SLOPE * h)
        summed = jax.ops.segment_sum(h, dst, num_segments=N)
        counts = jax.ops.segment_sum(jnp.ones((h.shape[0],), h.dtype), dst, num_segments=N)
        return summed / jnp.maximum(counts, 1.0)[:, None]

    def _L3_gnn_ref(edge_index, edge_type, embeddings, weights, biases):
        import jax, jax.numpy as jnp
        import numpy as np
        N_NODES = 12500
        HIDDEN = 64
        N_REL = 9
        N_LAYERS = 3
        N_EDGES = 125000
        N, E = embeddings.shape
        L = weights.shape[0]
        R = weights.shape[1] // 2
        idx0 = edge_index[0]
        idx1 = edge_index[1]
        rel0 = edge_type
        rel1 = edge_type + R
        output = embeddings
        for l in range(L):
            T = jnp.einsum('ne,reo->rno', embeddings, weights[l])
            m0 = T[rel0, idx0] + biases[l][rel0]
            m1 = T[rel1, idx1] + biases[l][rel1]
            m = jnp.concatenate([m0, m1], axis=0)
            d = jnp.concatenate([idx0, idx1], axis=0)
            s = jax.ops.segment_sum(m, d, num_segments=N)
            cnt = jax.ops.segment_sum(jnp.ones((d.shape[0],), m.dtype), d, num_segments=N)
            hidden = jnp.where(cnt[:, None] > 0, s / jnp.maximum(cnt, 1.0)[:, None], 0.0)
            if l + 1 < L:
                hidden = jax.nn.relu(hidden)
            output = hidden
        return output
    edge_index = jnp.stack([src, dst])
    x = _layernorm(x + _L0_gnn_ref(x, edge_index, edge_weight, L0_gnn_w1, L0_gnn_b1, L0_gnn_w2, L0_gnn_b2, L0_gnn_w3, L0_gnn_b3, L0_gnn_lw, L0_gnn_lb), axis=-1)
    x = _layernorm(x + _L1_gnn_ref(x, edge_index), axis=-1)
    x = _layernorm(x + _L2_gnn_ref(x, edge_index, L2_gnn_W, L2_gnn_b, L2_gnn_gamma, L2_gnn_beta), axis=-1)
    x = _layernorm(x + _L3_gnn_ref(edge_index, edge_type_9, x, L3_gnn_weights, L3_gnn_biases), axis=-1)
    return x

_drawn_inputs = setup_inputs


def setup_inputs(seed=0):
    import zlib

    import numpy as np

    out = dict(_drawn_inputs(seed))
    spreads = {'L0_gnn_b1': (0.0, 0.8),
     'L0_gnn_b2': (0.0, 0.367),
     'L0_gnn_b3': (0.0, 0.272),
     'L0_gnn_lb': (0.0, 0.1),
     'L2_gnn_gamma': (1.0, 0.2),
     'L2_gnn_beta': (0.0, 0.1)}
    factors = {'edge_weight': 8.0, 'L0_gnn_w1': 8.0, 'L2_gnn_b': 8.0}
    for name, (base, spread) in spreads.items():
        noise = np.random.default_rng([zlib.crc32(name.encode()), seed]).standard_normal(out[name].shape)
        drawn = base * np.exp(spread * noise) if base else spread * noise
        out[name] = jnp.asarray(drawn.astype(out[name].dtype))
    for name, factor in factors.items():
        out[name] = (out[name] * factor).astype(out[name].dtype)
    return out
```

```python
import concourse.bass as bass
from concourse import mybir
from contextlib import ExitStack


P = 128
N_NODES, N_EDGES, D, R = 12500, 200000, 64, 9
NB = -(-N_NODES // P)
NPAD = NB * P
QT = 8
EB = QT * P
NQ = -(-N_EDGES // EB)
NT = NQ * QT
EPAD = NT * P
QH = NQ // 2
HALVES = 2
PAD_NODE = NPAD - 1
SLOTS = 4
GROUP = 7
NGROUPS = NB // GROUP
LN_EPS = 1e-5
BN_EPS = 1e-5
COUNT_EPS = 1e-8
SLOPE = 0.3
assert NQ % (2 * SLOTS) in (0, SLOTS) and NQ % SLOTS == 0 and NB % (2 * GROUP) == 0


def gnn_kernel(nc, ins, out):
    f32, i32, bf16, f16 = mybir.dt.float32, mybir.dt.int32, mybir.dt.bfloat16, mybir.dt.float16
    ALU = mybir.AluOpType
    ACT = mybir.ActivationFunctionType
    AX = mybir.AxisListType
    root = ExitStack()
    semaphores_of = {}

    def sb(ctx, name, shape, dt=f32):
        return ctx.enter_context(nc.sbuf_tensor(name, shape, dt))

    def pb(ctx, name, shape, dt=f32):
        return ctx.enter_context(nc.psum_tensor(name, shape, dt))

    def sem(ctx, name):
        held = semaphores_of.get(id(ctx))
        if held is None:
            held = semaphores_of[id(ctx)] = []

            def release():
                nc.clear_and_free_semaphores(held)
                del semaphores_of[id(ctx)]
                with nc.Block():
                    pass
            ctx.callback(release)
        held.append(nc.alloc_semaphore(name))
        return held[-1]

    def dram(name, shape, dt=f32):
        return nc.dram_tensor(name, shape, dt).ap()

    table16 = dram("table16", (NPAD, 16))
    table16b = dram("table16b", (NPAD, 16))
    table32 = dram("table32", (NPAD, 32))
    table64 = dram("table64", (NPAD, D))
    table_q = dram("table_q", (NPAD, D))
    table_p = dram("table_p", (NPAD, D))
    prefix = {w: dram(f"prefix{w}", (EPAD, w)) for w in (25, 16, 32, 128, 64)}
    messages = dram("messages", (EPAD, D))
    node_at_edge = dram("node_at_edge", (EPAD + NPAD, D))

    with root:
        ident = sb(root, "ident", [P, P])
        anti = sb(root, "anti", [P, P])
        ones = sb(root, "ones", [P, P])
        upper = sb(root, "upper", [P, P])
        iota_row = sb(root, "iota_row", [P, P])
        iota_upper = sb(root, "iota_upper", [P, P])
        X = sb(root, "X", [P, NB, D])
        src_idx = sb(root, "src_idx", [P, NT + 2 * QT], i32)
        weight = sb(root, "weight", [P, NT])
        seg_end = sb(root, "seg_end", [P, NT])
        seg_end_first = sb(root, "seg_end_first", [P, NT])
        etype = sb(root, "etype", [P, NT])
        dst_hi = sb(root, "dst_hi", [P, NT])
        dst_lo = sb(root, "dst_lo", [P, NT])
        carry_on = sb(root, "carry_on", [P, NT])
        linked = sb(root, "linked", [P, 2 * QT])
        fix_row = sb(root, "fix_row", [P, 2 * QT], i32)
        first_dst = sb(root, "first_dst", [P, 2 * QT], i32)
        end_row = sb(root, "end_row", [P, NB], i32)
        start_row = sb(root, "start_row", [P, NB], i32)
        count = sb(root, "count", [P, NB])
        nonempty = sb(root, "nonempty", [P, NB])
        dinv = sb(root, "dinv", [P, NB])
        counts = sb(root, "counts", [P, NB, 2 * R])

        def chain_of(engine, s):
            n = [0]

            def link(instruction):
                n[0] += 1
                instruction.then_inc(s, 1)
                engine.wait_ge(s, n[0])
            return link

        turns = [sem(root, "turns_pe"), sem(root, "turns_pool")]

        def settled(engine):
            engine.sem_inc(turns[engine is nc.gpsimd], 1)

        def per_half(ap):
            return ap.rearrange("p (h q j) -> p h j q", h=HALVES, j=QT)

        with ExitStack() as c:
            iota_i = sb(c, "iota_i", [P, P], i32)
            ew_f = sb(c, "ew_f", [QH, HALVES, EB])
            src_f = sb(c, "src_f", [QH, HALVES, EB])
            dst_f = sb(c, "dst_f", [QH, HALVES, EB])
            typ_f = sb(c, "typ_f", [QH, HALVES, EB])
            prev_i = sb(c, "prev_i", [QH, HALVES], i32)
            prev_f = sb(c, "prev_f", [QH, HALVES])
            raw = ExitStack()
            src_i = sb(raw, "src_i", [QH, HALVES, EB], i32)
            dst_i = sb(raw, "dst_i", [QH, HALVES, EB], i32)
            typ_i = sb(raw, "typ_i", [QH, HALVES, EB], i32)
            s_load = sem(c, "s_load")
            s_const = sem(c, "s_const")
            s_pchain = sem(c, "s_pchain")
            s_dchain = sem(c, "s_dchain")
            s_pad = sem(c, "s_pad")
            full = N_EDGES // EB - QH
            rest = N_EDGES - (QH + full) * EB
            with nc.Block() as block:
                @block.gpsimd
                def _(pool):
                    link = chain_of(pool, s_pchain)
                    link(nc.gpsimd.iota(iota_i[:], pattern=[[1, P]], base=0, channel_multiplier=0))
                    link(nc.gpsimd.memset(ident[:], 0.0))
                    link(nc.gpsimd.memset(anti[:], 0.0))
                    link(nc.gpsimd.memset(ones[:], 1.0))
                    link(nc.gpsimd.tensor_copy(iota_row[:], iota_i[:]))
                    link(nc.gpsimd.affine_select(out=ident[:], in_=ident[:], compare_op=ALU.not_equal, fill=1.0,
                                                 base=0, pattern=[[1, P]], channel_multiplier=-1))
                    link(nc.gpsimd.affine_select(out=anti[:], in_=anti[:], compare_op=ALU.not_equal, fill=1.0,
                                                 base=-(P - 1), pattern=[[1, P]], channel_multiplier=1))
                    link(nc.gpsimd.affine_select(out=upper[:], in_=ones[:], compare_op=ALU.is_ge, fill=0.0,
                                                 base=0, pattern=[[1, P]], channel_multiplier=-1))
                    link(nc.gpsimd.affine_select(out=iota_upper[:], in_=iota_row[:], compare_op=ALU.is_ge,
                                                 fill=999.0, base=0, pattern=[[1, P]], channel_multiplier=-1))

                @block.sync
                def _(sp):
                    sp.wait_ge(s_pad, 6)
                    n = 0
                    for dst_tile, name in ((src_i, "src"), (dst_i, "dst"), (typ_i, "edge_type_9"), (ew_f, "edge_weight")):
                        a = ins[name]
                        sp.dma_start(dst_tile[:, 0, :], a[0:QH * EB].rearrange("(q e) -> q e", e=EB)).then_inc(s_load, 16)
                        sp.dma_start(dst_tile[0:full, 1, :], a[QH * EB:(QH + full) * EB].rearrange("(q e) -> q e", e=EB)).then_inc(s_load, 16)
                        sp.dma_start(dst_tile[full:full + 1, 1, 0:rest], a[(QH + full) * EB:N_EDGES].rearrange("(q e) -> q e", q=1)).then_inc(s_load, 16)
                        n += 3
                    last = ins["dst"][0:QH * EB * 2 - EB].rearrange("(q e) -> q e", e=EB)[:, EB - 1:EB]
                    with nc.allow_non_contiguous_dma(reason="one index per batch"):
                        sp.dma_start(prev_i[1:QH, 0:1], last[0:QH - 1]).then_inc(s_load, 16)
                        sp.dma_start(prev_i[0:QH, 1:2], last[QH - 1:2 * QH - 1]).then_inc(s_load, 16)
                    sp.dma_start(X[:, 0:NB - 1, :], ins["x"][0:(NB - 1) * P, :].rearrange("(h l) d -> l h d", l=P)).then_inc(s_load, 16)
                    sp.dma_start(X[0:N_NODES - (NB - 1) * P, NB - 1, :], ins["x"][(NB - 1) * P:N_NODES, :]).then_inc(s_load, 16)
                    sp.wait_ge(s_load, 16 * (n + 4))

                @block.vector
                def _(dve):
                    nc.vector.memset(src_i[:], PAD_NODE).then_inc(s_pad, 1)
                    nc.vector.memset(dst_i[:], PAD_NODE).then_inc(s_pad, 1)
                    nc.vector.memset(typ_i[:], 0).then_inc(s_pad, 1)
                    nc.vector.memset(ew_f[:], 0.0).then_inc(s_pad, 1)
                    nc.vector.memset(prev_i[:], -1).then_inc(s_pad, 1)
                    nc.vector.memset(X[:, NB - 1, :], 0.0).then_inc(s_pad, 1)
                    nc.vector.memset(src_idx[:, NT:], PAD_NODE).then_inc(s_dchain, 1)
                    dve.wait_ge(s_load, 16 * 16)
                    nc.vector.tensor_copy(src_f[:], src_i[:]).then_inc(s_dchain, 1)
                    nc.vector.tensor_copy(dst_f[:], dst_i[:]).then_inc(s_dchain, 1)
                    nc.vector.tensor_copy(typ_f[:], typ_i[:]).then_inc(s_dchain, 1)
                    nc.vector.tensor_copy(prev_f[:], prev_i[:]).then_inc(s_dchain, 1)

            raw.close()
            same = sb(c, "same", [QH, 2 * QT, P])
            rev = sb(c, "rev", [QH, 2 * QT, P])
            eval_rev = sb(c, "eval_rev", [QH, P])
            end_rev = sb(c, "end_rev", [QH, 2 * QT * P])
            is_first = sb(c, "is_first", [QH, 2 * QT, P])
            dst_t = sb(c, "dst_t", [P, NT])
            src_t = sb(c, "src_t", [P, NT])
            first_t = sb(c, "first_t", [P, NT])
            end_rev_t = sb(c, "end_rev_t", [P, NT])
            dst_ti = sb(c, "dst_ti", [P, NT], i32)
            dst_tj = sb(c, "dst_tj", [P, NT], i32)
            diag = sb(c, "diag", [QH, 2 * QT, QH])
            carry_q = sb(c, "carry_q", [QH, 2 * QT])
            tmp_q = sb(c, "tmp_q", [QH, 2 * QT])
            qbase = sb(c, "qbase", [QH, 2 * QT], i32)
            qbase_f = sb(c, "qbase_f", [QH, 2 * QT])
            ps = pb(c, "ps", [P, 4, 512])
            t_pe = sem(c, "t_pe")
            t_ev = sem(c, "t_ev")
            t_seg = sem(c, "t_seg")
            t_first = sem(c, "t_first")
            t_diag = sem(c, "t_diag")
            t_pool = sem(c, "t_pool")
            t_dve = sem(c, "t_dve")
            HJ = [(h, j0) for h in range(HALVES) for j0 in (0, 4)]

            def view4(ap3, h, j0):
                return ap3[:, h, j0:j0 + 4, :]

            with nc.Block() as block:
                @block.tensor
                def _(pe):
                    g = 0

                    def group(fill):
                        nonlocal g
                        if g >= 4:
                            pe.wait_ge(t_ev, g - 3)
                        for j in range(4):
                            last = fill(j, g % 4)
                        last.then_inc(t_pe, 1)
                        g += 1

                    def tr(src):
                        for h, j0 in HJ:
                            group(lambda j, b: nc.tensor.transpose(
                                ps[:, b, j * QH:(j + 1) * QH], src(h, j0 + j), ident[0:QH, 0:QH]))
                    for a in (src_f, dst_f, typ_f, ew_f):
                        tr(lambda h, j, a=a: a[:, h, j * P:(j + 1) * P])
                    pe.wait_ge(t_ev, 8)
                    for h, j0 in HJ:
                        group(lambda j, b: nc.tensor.matmul(
                            ps[0:QH, b, j * P:(j + 1) * P], per_half(dst_t[:])[:, h, j0 + j, :], anti[:],
                            start=True, stop=True))
                    pe.wait_ge(t_first, 1)
                    tr(lambda h, j: is_first[:, h * QT + j, :])
                    pe.wait_ge(t_seg, 1)
                    tr(lambda h, j: end_rev[:, (h * QT + j) * P:(h * QT + j + 1) * P])
                    pe.wait_ge(t_ev, 28)
                    for k in range(4):
                        pe.wait_ge(t_ev, g - 3)
                        nc.tensor.matmul(ps[:, g % 4, 0:NT // 4], anti[:], end_rev_t[:, k * (NT // 4):(k + 1) * (NT // 4)],
                                         start=True, stop=True).then_inc(t_pe, 1)
                        g += 1
                    pe.wait_ge(t_diag, 1)
                    for h, j0 in HJ:
                        group(lambda j, b: nc.tensor.matmul(
                            ps[:, b, j * QH:(j + 1) * QH], ones[0:QH, :], diag[:, h * QT + j0 + j, :],
                            start=True, stop=True))

                @block.scalar
                def _(act):
                    g = 0

                    def evict(out_ap, n, parts=P):
                        nonlocal g
                        act.wait_ge(t_pe, g + 1)
                        v = ps[0:parts, g % 4, 0:4 * n].rearrange("p (j q) -> p j q", j=4)
                        nc.scalar.copy(out_ap, v).then_inc(t_ev, 1)
                        g += 1
                    for a in (src_t, dst_t, etype, weight):
                        for h, j0 in HJ:
                            evict(view4(per_half(a[:]), h, j0), QH)
                    for h, j0 in HJ:
                        evict(rev[:, h * QT + j0:h * QT + j0 + 4, :], P, QH)
                    for a in (first_t, end_rev_t):
                        for h, j0 in HJ:
                            evict(view4(per_half(a[:]), h, j0), QH)
                    for k in range(4):
                        evict(seg_end[:, k * (NT // 4):(k + 1) * (NT // 4)].rearrange("p (j q) -> p j q", j=4), NT // 16)
                    for h, j0 in HJ:
                        evict(view4(per_half(carry_on[:]), h, j0), QH)

                @block.gpsimd
                def _(pool):
                    nc.gpsimd.iota(qbase[:].rearrange("q (h j) -> q h j", h=HALVES), pattern=[[0, HALVES], [1, QT]],
                                   base=0, channel_multiplier=EB).then_inc(t_pool, 1)

                @block.vector
                def _(dve):
                    link = chain_of(dve, t_dve)
                    dstv = dst_f[:].rearrange("q h (j e) -> q (h j) e", e=P)
                    link(nc.vector.tensor_tensor(same[:, :, 1:P], dstv[:, :, 1:P], dstv[:, :, 0:P - 1], ALU.is_equal))
                    link(nc.vector.memset(is_first[:, :, 0:1], 1.0))
                    nc.vector.tensor_scalar(is_first[:, :, 1:P], same[:, :, 1:P], -1.0, 1.0, ALU.mult, ALU.add).then_inc(t_first, 1)
                    lv = linked[0:QH, :].rearrange("q (h j) -> q h j", h=HALVES)
                    df = dst_f[:].rearrange("q h (j e) -> q h j e", e=P)
                    link(nc.vector.tensor_tensor(lv[:, :, 1:QT], df[:, :, 1:QT, 0], df[:, :, 0:QT - 1, P - 1], ALU.is_equal))
                    link(nc.vector.tensor_tensor(lv[:, :, 0], df[:, :, 0, 0], prev_f[:], ALU.is_equal))
                    link(nc.vector.tensor_copy(first_dst[0:QH, :].rearrange("q (h j) -> q h j", h=HALVES), df[:, :, :, 0]))
                    link(nc.vector.tensor_scalar(eval_rev[:], iota_row[0:QH, :], -1.0, float(P - 1), ALU.mult, ALU.add))
                    dve.wait_ge(t_ev, 20)
                    link(nc.vector.memset(same[:, :, 0:1], 0.0))
                    link(nc.vector.tensor_tensor(same[:, :, 1:P], rev[:, :, 1:P], rev[:, :, 0:P - 1], ALU.is_equal))
                    link(nc.vector.tensor_scalar(rev[:], same[:], -1.0, 1.0, ALU.mult, ALU.add))
                    link(nc.vector.tensor_tensor(rev[:], rev[:], eval_rev[:, None, :].to_broadcast([QH, 2 * QT, P]), ALU.mult))
                    nc.vector.tensor_tensor_scan(end_rev[:], same[:].rearrange("q t e -> q (t e)"),
                                                 rev[:].rearrange("q t e -> q (t e)"), 0.0, ALU.mult, ALU.add).then_inc(t_seg, 1)
                    dve.wait_ge(t_seg, 1)
                    ev = end_rev[:].rearrange("q (t e) -> q t e", e=P)[:, :, P - 1]
                    link(nc.vector.tensor_single_scalar(tmp_q[:], ev, float(P - 1), ALU.is_equal))
                    link(nc.vector.tensor_tensor(carry_q[:], tmp_q[:], linked[0:QH, :], ALU.mult))
                    for t in range(2 * QT):
                        last = nc.vector.tensor_scalar(diag[:, t, :], ident[0:QH, 0:QH], carry_q[:, t:t + 1], None, ALU.mult)
                    link(last)
                    nc.vector.memset(tmp_q[:], 0.0).then_inc(t_diag, 1)
                    dve.wait_ge(t_diag, 1)
                    dve.wait_ge(t_pool, 1)
                    link(nc.vector.tensor_copy(qbase_f[:], qbase[:]))
                    link(nc.vector.tensor_scalar_add(qbase_f[:, QT:], qbase_f[:, QT:], float(QH * EB)))
                    link(nc.vector.scalar_tensor_tensor(qbase_f[:], ev, float(QT), qbase_f[:], ALU.mult, ALU.add))
                    link(nc.vector.tensor_copy(fix_row[0:QH, :], qbase_f[:]))
                    dve.wait_ge(t_ev, 32)
                    link(nc.vector.tensor_scalar_add(seg_end_first[:], seg_end[:], 1.0))
                    link(nc.vector.tensor_tensor(seg_end_first[:], seg_end_first[:], first_t[:], ALU.mult))
                    link(nc.vector.tensor_scalar_add(seg_end_first[:], seg_end_first[:], -1.0))
                    link(nc.vector.tensor_copy(src_idx[:, 0:NT], src_t[:]))
                    link(nc.vector.tensor_copy(dst_ti[:], dst_t[:]))
                    link(nc.vector.tensor_single_scalar(dst_tj[:], dst_ti[:], 7, ALU.logical_shift_right))
                    link(nc.vector.tensor_copy(dst_hi[:], dst_tj[:]))
                    link(nc.vector.tensor_single_scalar(dst_tj[:], dst_ti[:], P - 1, ALU.bitwise_and))
                    link(nc.vector.tensor_copy(dst_lo[:], dst_tj[:]))

        with ExitStack() as c:
            lo_hot = sb(c, "lo_hot", [P, SLOTS, QT, P])
            hi_hot = sb(c, "hi_hot", [P, SLOTS, QT, 2, NB])
            hist = pb(c, "hist", [P, 2 * NB])
            h_hot = sem(c, "h_hot")
            h_pe = sem(c, "h_pe")
            with nc.Block() as block:
                @block.vector
                def _(dve):
                    def step(i, first):
                        for k in range(SLOTS):
                            if not first:
                                dve.wait_ge(h_pe, (i - 1) * SLOTS + k + 1)
                            for u in range(QT):
                                t = i * (SLOTS * QT) + k * QT + u
                                lo, hi, ew = dst_lo[:, bass.ds(t, 1)], dst_hi[:, bass.ds(t, 1)], weight[:, bass.ds(t, 1)]
                                nc.vector.tensor_scalar(lo_hot[:, k, u, :], iota_row[:], lo, None, ALU.is_equal)
                                nc.vector.tensor_scalar(hi_hot[:, k, u, 0, :], iota_row[:, 0:NB], hi, None, ALU.is_equal)
                                last = nc.vector.tensor_scalar(hi_hot[:, k, u, 1, :], iota_row[:, 0:NB], hi, ew, ALU.is_equal, ALU.mult)
                            last.then_inc(h_hot, 1)
                    step(0, True)
                    with dve.Fori(1, NQ // SLOTS) as i:
                        step(i, False)

                @block.tensor
                def _(pe):
                    def step(i, first, final):
                        for k in range(SLOTS):
                            pe.wait_ge(h_hot, i * SLOTS + k + 1)
                            for u in range(QT):
                                last = nc.tensor.matmul(hist[:], lo_hot[:, k, u, :],
                                                        hi_hot[:, k, u, :, :].rearrange("p a n -> p (a n)"),
                                                        start=first and k == 0 and u == 0,
                                                        stop=final and k == SLOTS - 1 and u == QT - 1)
                            last.then_inc(h_pe, 1)
                    step(0, True, False)
                    with pe.Fori(1, NQ // SLOTS - 1) as i:
                        step(i, False, False)
                    step(NQ // SLOTS - 1, False, True)

            incl = pb(c, "incl", [P, NB])
            totals = pb(c, "totals", [P, NB])
            cum = sb(c, "cum", [P, NB])
            end_f = sb(c, "end_f", [P, NB])
            tmp = sb(c, "tmp", [P, NB])
            tmp2 = sb(c, "tmp2", [P, NB])
            ti = sb(c, "ti", [P, NB], i32)
            tj = sb(c, "tj", [P, NB], i32)
            tk = sb(c, "tk", [P, NB], i32)
            node = sb(c, "node", [P, NB], i32)
            d_ch = sem(c, "d_ch")
            d_count = sem(c, "d_count")
            d_pe = sem(c, "d_pe")
            d_deg = sem(c, "d_deg")
            d_sqrt = sem(c, "d_sqrt")
            d_node = sem(c, "d_node")
            with nc.Block() as block:
                @block.tensor
                def _(pe):
                    pe.wait_ge(d_count, 1)
                    nc.tensor.matmul(incl[:], upper[:], count[:], start=True, stop=True)
                    nc.tensor.matmul(totals[:], ones[:], count[:], start=True, stop=True).then_inc(d_pe, 1)

                @block.scalar
                def _(act):
                    act.wait_ge(d_deg, 1)
                    nc.scalar.sqrt(tmp2[:], tmp[:]).then_inc(d_sqrt, 1)

                @block.gpsimd
                def _(pool):
                    nc.gpsimd.iota(node[:], pattern=[[P, NB]], base=EPAD, channel_multiplier=1).then_inc(d_node, 1)

                @block.vector
                def _(dve):
                    link = chain_of(dve, d_ch)
                    nc.vector.tensor_copy(count[:], hist[:, 0:NB]).then_inc(d_count, 1)
                    link(nc.vector.tensor_scalar_add(dinv[:], hist[:, NB:2 * NB], 1.0))
                    link(nc.vector.tensor_single_scalar(end_f[:], dinv[:], 0.0, ALU.is_gt))
                    nc.vector.tensor_scalar_max(tmp[:], dinv[:], 1e-30).then_inc(d_deg, 1)
                    dve.wait_ge(d_sqrt, 1)
                    link(nc.vector.reciprocal(dinv[:], tmp2[:]))
                    link(nc.vector.tensor_tensor(dinv[:], dinv[:], end_f[:], ALU.mult))
                    dve.wait_ge(d_pe, 1)
                    link(nc.vector.tensor_copy(tmp2[:], totals[:]))
                    link(nc.vector.memset(tmp[:], 1.0))
                    link(nc.vector.tensor_tensor_scan(cum[:], tmp[:], tmp2[:], 0.0, ALU.mult, ALU.add))
                    link(nc.vector.tensor_tensor(cum[:], cum[:], tmp2[:], ALU.subtract))
                    link(nc.vector.tensor_tensor(end_f[:], cum[:], incl[:], ALU.add))
                    link(nc.vector.tensor_single_scalar(nonempty[:], count[:], 0.0, ALU.is_gt))

                    def to_row(edge_f, row):
                        link(nc.vector.tensor_copy(ti[:], edge_f))
                        link(nc.vector.tensor_scalar(tj[:], ti[:], 10, 10, ALU.logical_shift_right, ALU.logical_shift_left))
                        link(nc.vector.tensor_scalar(tk[:], ti[:], P - 1, 3, ALU.bitwise_and, ALU.logical_shift_left))
                        link(nc.vector.tensor_tensor(tj[:], tj[:], tk[:], ALU.bitwise_or))
                        link(nc.vector.tensor_scalar(tk[:], ti[:], 7, QT - 1, ALU.logical_shift_right, ALU.bitwise_and))
                        link(nc.vector.tensor_tensor(row, tj[:], tk[:], ALU.bitwise_or))
                    link(nc.vector.tensor_scalar(tmp[:], end_f[:], -1.0, 0.0, ALU.add, ALU.max))
                    to_row(tmp[:], end_row[:])
                    link(nc.vector.tensor_tensor(tmp[:], end_f[:], count[:], ALU.subtract))
                    link(nc.vector.tensor_scalar_min(tmp[:], tmp[:], float(EPAD - 1)))
                    to_row(tmp[:], start_row[:])
                    link(nc.vector.tensor_copy(tmp[:], start_row[:]))
                    dve.wait_ge(d_node, 1)
                    link(nc.vector.tensor_copy(tmp2[:], node[:]))
                    link(nc.vector.tensor_tensor(tmp[:], tmp[:], tmp2[:], ALU.subtract))
                    link(nc.vector.tensor_tensor(tmp[:], tmp[:], nonempty[:], ALU.mult))
                    link(nc.vector.tensor_tensor(tmp[:], tmp[:], tmp2[:], ALU.add))
                    link(nc.vector.tensor_copy(start_row[:], tmp[:]))

        def rows_of(dram_ap):
            return dram_ap.rearrange("(h l) d -> l h d", l=P)

        def batches_of(dram_ap):
            return dram_ap.rearrange("(b e j) w -> b e (j w)", e=P, j=QT)

        def edge_pass(tag, table, gathered, width, weighted=False, with_types=False, squares=False,
                      histogram=None, zero_fill=None):
            with ExitStack() as c:
                idx = sb(c, tag + "idx", [P, SLOTS, QT], i32)
                segment_matrix = sb(c, tag + "seg", [P, SLOTS, QT, P])
                msg = sb(c, tag + "msg", [P, SLOTS, QT, width])
                summed = sb(c, tag + "sum", [P, SLOTS, QT * width])
                banks = -(-QT * width // 512)
                acc = [pb(c, tag + f"acc{k}", [P, QT * width]) for k in range(2)]
                types_too = with_types
                gathered_rows = [sem(c, tag + f"gathered{k}") for k in range(SLOTS)]
                stored = [sem(c, tag + f"stored{k}") for k in range(SLOTS)]
                idx_ready = sem(c, tag + "idx_ready")
                matrix_ready = sem(c, tag + "matrix_ready")
                msg_ready = sem(c, tag + "msg_ready")
                product_done = sem(c, tag + "product_done")
                evicted = sem(c, tag + "evicted")
                hot_ready = sem(c, tag + "hot_ready")
                hot_used = sem(c, tag + "hot_used")
                zero_set = sem(c, tag + "zero_set")
                zeroed = sem(c, tag + "zeroed")
                out_b = batches_of(prefix[width])
                iters = NQ // SLOTS
                if histogram is not None:
                    key_lo, key_hi, iota_key = histogram["lo"], histogram["hi"], histogram["iota"]
                    hot_lo = sb(c, tag + "hot_lo", [P, 2, QT, P], bf16)
                    hot_hi = sb(c, tag + "hot_hi", [P, 2, QT, NB * R], bf16)
                    hacc = [pb(c, tag + f"hacc{k}", [P, NB * R // 2]) for k in range(2)]
                if zero_fill is not None:
                    zeros = sb(c, tag + "zeros", [P, QT * D])
                with nc.Block() as block:
                    @block.gpsimd
                    def _(pool):
                        def step(i, first):
                            for k in range(SLOTS):
                                pool.wait_ge(idx_ready, i * SLOTS + k + 1)
                                if not first:
                                    pool.wait_ge(product_done, (i - 1) * SLOTS + k + 1)
                                settled(pool)
                                for u in range(QT):
                                    nc.gpsimd.indirect_dma_start(
                                        msg[:, k, u, 0:gathered], None, table,
                                        bass.IndirectOffsetOnAxis(idx[:, k, u:u + 1], 0)).then_inc(gathered_rows[k], 16)
                        step(0, True)
                        with pool.Fori(1, iters) as i:
                            step(i, False)

                    @block.scalar
                    def _(act):
                        for k in range(2):
                            nc.scalar.copy(idx[:, k, :], src_idx[:, k * QT:(k + 1) * QT]).then_inc(idx_ready, 1)

                        def step(i, first):
                            for k in range(SLOTS):
                                ahead = (k + 2) % SLOTS
                                if not (first and k < 2):
                                    act.wait_ge(gathered_rows[ahead], ((i if k < 2 else i + 1)) * (16 * QT))
                                nc.scalar.copy(idx[:, ahead, :], src_idx[:, bass.ds((i * SLOTS + k + 2) * QT, QT)]).then_inc(idx_ready, 1)
                                if squares:
                                    act.wait_ge(gathered_rows[k], (i + 1) * (16 * QT))
                                    nc.scalar.square(msg[:, k, :, gathered:2 * gathered], msg[:, k, :, 0:gathered]).then_inc(msg_ready, 1)
                                act.wait_ge(product_done, i * SLOTS + k + 1)
                                if not first:
                                    act.wait_ge(stored[k], i * 16)
                                for a in range(0, QT * width, 512):
                                    z = min(a + 512, QT * width)
                                    last = nc.scalar.copy(summed[:, k, a:z], acc[k % 2][:, a:z])
                                last.then_inc(evicted, 1)
                        step(0, True)
                        with act.Fori(1, iters) as i:
                            step(i, False)

                    @block.sync
                    def _(sp):
                        if zero_fill is not None:
                            sp.wait_ge(zero_set, 1)
                        with sp.Fori(0, iters) as i:
                            for k in range(SLOTS):
                                sp.wait_ge(evicted, i * SLOTS + k + 1)
                                sp.dma_start(out_b[i * SLOTS + k], summed[:, k, :]).then_inc(stored[k], 16)
                                if zero_fill is not None:
                                    sp.dma_start(zero_fill[i * SLOTS + k], zeros[:]).then_inc(zeroed, 16)
                        for k in range(SLOTS):
                            sp.wait_ge(stored[k], iters * 16)
                        if zero_fill is not None:
                            sp.wait_ge(zeroed, NQ * 16)

                    @block.vector
                    def _(dve):
                        if zero_fill is not None:
                            nc.vector.memset(zeros[:], 0.0).then_inc(zero_set, 1)

                        def step(i, first):
                            for k in range(SLOTS):
                                if not first:
                                    dve.wait_ge(product_done, (i - 1) * SLOTS + k + 1)
                                for u in range(QT):
                                    t = i * (SLOTS * QT) + k * QT + u
                                    end = seg_end[:, bass.ds(t, 1)]
                                    if weighted:
                                        last = nc.vector.tensor_scalar(segment_matrix[:, k, u, :], iota_upper[:], end,
                                                                       weight[:, bass.ds(t, 1)], ALU.is_le, ALU.mult)
                                    else:
                                        last = nc.vector.tensor_scalar(segment_matrix[:, k, u, :], iota_upper[:], end,
                                                                       None, ALU.is_le)
                                last.then_inc(matrix_ready, 1)
                                if types_too:
                                    t0 = i * (SLOTS * QT) + k * QT
                                    nc.vector.tensor_tensor(
                                        msg[:, k, :, gathered:gathered + R],
                                        iota_row[:, None, 0:R].to_broadcast([P, QT, R]),
                                        etype[:, bass.ds(t0, QT)][:, :, None].to_broadcast([P, QT, R]), ALU.is_equal)
                                    dve.wait_ge(gathered_rows[k], (i + 1) * (16 * QT))
                                    nc.vector.tensor_tensor(
                                        msg[:, k, :, 0:gathered], msg[:, k, :, 0:gathered],
                                        weight[:, bass.ds(t0, QT)][:, :, None].to_broadcast([P, QT, gathered]),
                                        ALU.mult).then_inc(msg_ready, 1)
                                if histogram is not None:
                                    s = k % 2
                                    if not (first and k < 2):
                                        dve.wait_ge(hot_used, i * SLOTS + k - 1)
                                    for u in range(QT):
                                        t = i * (SLOTS * QT) + k * QT + u
                                        nc.vector.tensor_scalar(hot_lo[:, s, u, :], iota_key[:, 0:P], key_lo[:, bass.ds(t, 1)], None, ALU.is_equal)
                                        last = nc.vector.tensor_scalar(hot_hi[:, s, u, :], iota_key[:], key_hi[:, bass.ds(t, 1)], None, ALU.is_equal)
                                    last.then_inc(hot_ready, 1)
                        step(0, True)
                        with dve.Fori(1, iters) as i:
                            step(i, False)

                    @block.tensor
                    def _(pe):
                        def step(i, first, final):
                            for k in range(SLOTS):
                                if histogram is not None:
                                    s = k % 2
                                    pe.wait_ge(hot_ready, i * SLOTS + k + 1)
                                    half = NB * R // 2
                                    for u in range(QT):
                                        for a in range(2):
                                            last = nc.tensor.matmul(hacc[a][:], hot_lo[:, s, u, :], hot_hi[:, s, u, a * half:(a + 1) * half],
                                                                    start=first and k == 0 and u == 0,
                                                                    stop=final and k == SLOTS - 1 and u == QT - 1)
                                    last.then_inc(hot_used, 1)
                                pe.wait_ge(matrix_ready, i * SLOTS + k + 1)
                                if types_too or squares:
                                    pe.wait_ge(msg_ready, i * SLOTS + k + 1)
                                pe.wait_ge(gathered_rows[k], (i + 1) * (16 * QT))
                                if not (first and k < 2):
                                    pe.wait_ge(evicted, i * SLOTS + k - 1)
                                for u in range(QT):
                                    last = nc.tensor.matmul(acc[k % 2][:, u * width:(u + 1) * width], segment_matrix[:, k, u, :],
                                                            msg[:, k, u, :], start=True, stop=True)
                                last.then_inc(product_done, 1)
                        step(0, True, False)
                        with pe.Fori(1, iters - 1) as i:
                            step(i, False, False)
                        step(iters - 1, False, True)
                if histogram is not None:
                    done = sem(c, tag + "hist_out")
                    with nc.Block() as block:
                        @block.vector
                        def _(dve):
                            half = NB // 2
                            for a in range(2):
                                nc.vector.tensor_copy(counts[:, a * half:(a + 1) * half, 0:R],
                                                      hacc[a][:].rearrange("p (n r) -> p n r", r=R)).then_inc(done, 1)

        def carry_stage(tag, width):
            pre = prefix[width]
            with ExitStack() as c:
                tile_last = sb(c, tag + "tile_last", [QH, HALVES, QT, width])
                totals_t = sb(c, tag + "totals_t", [width, NT])
                running = sb(c, tag + "running", [width, 1 + NT])
                fixed = sb(c, tag + "fixed", [QH, 2 * QT, width])
                ps4 = pb(c, tag + "ps4", [P, 4, 512])
                qs4 = pb(c, tag + "qs4", [P, 4, 512])
                last_loaded = sem(c, tag + "last_loaded")
                turned = sem(c, tag + "turned")
                turned_out = sem(c, tag + "turned_out")
                scanned = sem(c, tag + "scanned")
                back = sem(c, tag + "back")
                rows_there = sem(c, tag + "rows_there")
                rows_fixed = sem(c, tag + "rows_fixed")
                rows_back = sem(c, tag + "rows_back")
                HJ = [(h, j0) for h in range(HALVES) for j0 in (0, 4)]
                with nc.Block() as block:
                    @block.sync
                    def _(sp):
                        v = pre.rearrange("(h q e j) w -> q h e (j w)", h=HALVES, q=QH, e=P)
                        for h in range(HALVES):
                            sp.dma_start(tile_last[:, h, :, :].rearrange("q j w -> q (j w)"), v[:, h, P - 1, :]).then_inc(last_loaded, 16)

                    @block.tensor
                    def _(pe):
                        pe.wait_ge(last_loaded, 32)
                        for g, (h, j0) in enumerate(HJ):
                            for j in range(4):
                                last = nc.tensor.transpose(ps4[0:width, g, j * QH:(j + 1) * QH], tile_last[:, h, j0 + j, :],
                                                           ident[0:QH, 0:QH])
                            last.then_inc(turned, 1)
                        pe.wait_ge(scanned, 2)
                        rv = per_half(running[:, 0:NT])
                        for g, (h, j0) in enumerate(HJ):
                            for j in range(4):
                                last = nc.tensor.transpose(qs4[0:QH, g, j * width:(j + 1) * width], rv[:, h, j0 + j, :],
                                                           ident[0:width, 0:width])
                            last.then_inc(back, 1)

                    @block.scalar
                    def _(act):
                        for g, (h, j0) in enumerate(HJ):
                            act.wait_ge(turned, g + 1)
                            nc.scalar.copy(per_half(totals_t[:])[:, h, j0:j0 + 4, :],
                                           ps4[0:width, g, 0:4 * QH].rearrange("p (j q) -> p j q", j=4)).then_inc(turned_out, 1)

                    @block.vector
                    def _(dve):
                        nc.vector.memset(running[:, 0:1], 0.0).then_inc(scanned, 1)
                        dve.wait_ge(turned_out, 4)
                        nc.vector.tensor_tensor_scan(running[:, 1:1 + NT], carry_on[0:width, :], totals_t[:], 0.0,
                                                     ALU.mult, ALU.add).then_inc(scanned, 1)
                        dve.wait_ge(rows_there, 16 * 2 * QT)
                        for t in range(2 * QT):
                            g, j = t // 4, t % 4
                            dve.wait_ge(back, g + 1)
                            last = nc.vector.scalar_tensor_tensor(fixed[:, t, :], qs4[0:QH, g, j * width:(j + 1) * width],
                                                                  linked[0:QH, t:t + 1], fixed[:, t, :], ALU.mult, ALU.add)
                            last.then_inc(rows_fixed, 1)

                    @block.gpsimd
                    def _(pool):
                        for t in range(2 * QT):
                            nc.gpsimd.indirect_dma_start(fixed[:, t, :], None, pre,
                                                         bass.IndirectOffsetOnAxis(fix_row[0:QH, t:t + 1], 0)).then_inc(rows_there, 16)
                        pool.wait_ge(last_loaded, 32)
                        for t in range(2 * QT):
                            pool.wait_ge(rows_fixed, t + 1)
                            nc.gpsimd.indirect_dma_start(pre, bass.IndirectOffsetOnAxis(fix_row[0:QH, t:t + 1], 0),
                                                         fixed[:, t, :], None).then_inc(rows_back, 16)
                        pool.wait_ge(rows_back, 16 * 2 * QT)

        def node_gather(tag, width, agg):
            with ExitStack() as c:
                idx = sb(c, tag + "nidx", [P, 2, GROUP], i32)
                rows = sb(c, tag + "rows", [P, 2, GROUP, width])
                nidx_ready = sem(c, tag + "nidx_ready")
                got = [sem(c, tag + f"got{k}") for k in range(2)]
                taken = sem(c, tag + "taken")
                iters = NGROUPS // 2
                with nc.Block() as block:
                    @block.gpsimd
                    def _(pool):
                        def step(i, first):
                            for k in range(2):
                                pool.wait_ge(nidx_ready, 2 * i + k + 1)
                                if not first:
                                    pool.wait_ge(taken, 2 * i + k - 1)
                                settled(pool)
                                for u in range(GROUP):
                                    nc.gpsimd.indirect_dma_start(
                                        rows[:, k, u, :], None, prefix[width],
                                        bass.IndirectOffsetOnAxis(idx[:, k, u:u + 1], 0)).then_inc(got[k], 16)
                        step(0, True)
                        with pool.Fori(1, iters) as i:
                            step(i, False)

                    @block.scalar
                    def _(act):
                        def step(i, first):
                            for k in range(2):
                                if not first:
                                    act.wait_ge(got[k], i * (16 * GROUP))
                                nc.scalar.copy(idx[:, k, :], end_row[:, bass.ds((2 * i + k) * GROUP, GROUP)]).then_inc(nidx_ready, 1)
                        step(0, True)
                        with act.Fori(1, iters) as i:
                            step(i, False)

                    @block.vector
                    def _(dve):
                        with dve.Fori(0, iters) as i:
                            for k in range(2):
                                dve.wait_ge(got[k], (i + 1) * (16 * GROUP))
                                n0 = (2 * i + k) * GROUP
                                nc.vector.tensor_tensor(agg[:, bass.ds(n0, GROUP), :], rows[:, k, :, :],
                                                        nonempty[:, bass.ds(n0, GROUP)][:, :, None].to_broadcast([P, GROUP, width]),
                                                        ALU.mult).then_inc(taken, 1)

        def dense(tag, src, k_in, w, bias, n_out, dst, relu=False):
            with ExitStack() as c:
                row = sb(c, tag + "row", [P, 2, k_in])
                turned_sb = sb(c, tag + "turned_sb", [k_in, 2, P])
                pt = [pb(c, tag + f"pt{k}", [k_in, P]) for k in range(2)]
                po = [pb(c, tag + f"po{k}", [P, n_out]) for k in range(2)]
                row_ready = sem(c, tag + "row_ready")
                t_done = sem(c, tag + "t_done")
                t_out = sem(c, tag + "t_out")
                m_done = sem(c, tag + "m_done")
                m_out = sem(c, tag + "m_out")
                iters = NB // 2
                with nc.Block() as block:
                    @block.vector
                    def _(dve):
                        def copy_in(i, k, first):
                            if not first:
                                dve.wait_ge(t_done, 2 * i + k - 1)
                            nc.vector.tensor_copy(row[:, k, :], src[:, bass.ds(2 * i + k, 1), :].rearrange("p a d -> p (a d)")).then_inc(row_ready, 1)

                        def copy_t(i, k, first):
                            dve.wait_ge(t_done, 2 * i + k + 1)
                            if not first:
                                dve.wait_ge(m_done, 2 * i + k - 1)
                            nc.vector.tensor_copy(turned_sb[:, k, :], pt[k][:]).then_inc(t_out, 1)

                        def step(i, first):
                            for k in range(2):
                                copy_in(i, k, first)
                            for k in range(2):
                                copy_t(i, k, first)
                        step(0, True)
                        with dve.Fori(1, iters) as i:
                            step(i, False)

                    @block.tensor
                    def _(pe):
                        def step(i, first):
                            for k in range(2):
                                pe.wait_ge(row_ready, 2 * i + k + 1)
                                if not first:
                                    pe.wait_ge(t_out, 2 * i + k - 1)
                                settled(pe)
                                nc.tensor.transpose(pt[k][:], row[:, k, :], ident[:]).then_inc(t_done, 1)
                            for k in range(2):
                                pe.wait_ge(t_out, 2 * i + k + 1)
                                if not first:
                                    pe.wait_ge(m_out, 2 * i + k - 1)
                                last = nc.tensor.matmul(po[k][:], turned_sb[:, k, :], w, start=True, stop=bias is None)
                                if bias is not None:
                                    last = nc.tensor.matmul(po[k][:], ones[0:1, :], bias, start=False, stop=True)
                                last.then_inc(m_done, 1)
                        step(0, True)
                        with pe.Fori(1, iters) as i:
                            step(i, False)

                    @block.scalar
                    def _(act):
                        with act.Fori(0, iters) as i:
                            for k in range(2):
                                act.wait_ge(m_done, 2 * i + k + 1)
                                nc.scalar.activation(dst[:, bass.ds(2 * i + k, 1), :].rearrange("p a d -> p (a d)"), po[k][:],
                                                     ACT.Relu if relu else ACT.Copy).then_inc(m_out, 1)

        def per_node(v, width):
            return v[:, :, None].to_broadcast([P, NB, width])

        def per_column(v, width):
            return v[:, None, :].to_broadcast([P, NB, width])

        def store_table(tag, pairs):
            with ExitStack() as c:
                s = sem(c, tag + "table_stored")
                with nc.Block() as block:
                    @block.sync
                    def _(sp):
                        for table, rows in pairs:
                            sp.dma_start(rows_of(table), rows).then_inc(s, 16)
                        sp.wait_ge(s, 16 * len(pairs))

        def elementwise(tag, steps):
            with ExitStack() as c:
                s = sem(c, tag + "step_done")
                with nc.Block() as block:
                    @block.vector
                    def _(dve):
                        for n, (e, f) in enumerate(steps):
                            if e == "v":
                                if n:
                                    dve.wait_ge(s, n)
                                f().then_inc(s, 1)

                    @block.scalar
                    def _(act):
                        for n, (e, f) in enumerate(steps):
                            if e == "a":
                                if n:
                                    act.wait_ge(s, n)
                                f().then_inc(s, 1)

        V = nc.vector
        TT = V.tensor_tensor

        def layernorm_steps(y, sq, m, v, dst):
            return [
                ("v", lambda: V.reduce_sum(m, y, AX.X)),
                ("v", lambda: V.tensor_scalar_mul(m, m, 1.0 / D)),
                ("v", lambda: TT(y, y, per_node(m, D), ALU.subtract)),
                ("a", lambda: nc.scalar.square(sq, y)),
                ("v", lambda: V.reduce_sum(v, sq, AX.X)),
                ("v", lambda: V.tensor_scalar(v, v, 1.0 / D, LN_EPS, ALU.mult, ALU.add)),
                ("a", lambda: nc.scalar.sqrt(v, v)),
                ("v", lambda: V.reciprocal(m, v)),
                ("v", lambda: TT(dst, y, per_node(m, D), ALU.mult)),
            ]

        w1 = sb(root, "w1", [D, 16])
        w2 = sb(root, "w2", [16, 32])
        w3 = sb(root, "w3", [32, D])
        lw = sb(root, "lw", [2 * D, D])
        lb = sb(root, "lb", [1, D])
        b2 = sb(root, "b2", [1, 32])
        b3 = sb(root, "b3", [1, D])
        b1row = sb(root, "b1row", [P, 16])
        w2_raw = sb(root, "w2_raw", [D, 2, D])
        w_src = sb(root, "w_src", [D, D])
        w_dst = sb(root, "w_dst", [D, D])
        bn_b = sb(root, "bn_b", [1, D])
        gamma = sb(root, "gamma", [1, D])
        beta = sb(root, "beta", [1, D])
        w_rel = sb(root, "w_rel", [D, 2 * R, D])
        b_rel = sb(root, "b_rel", [1, 2 * R * D])
        with ExitStack() as c:
            wl = sem(c, "wl")
            wt = sem(c, "wt")
            wv = sem(c, "wv")
            psw = pb(c, "psw", [D, 2, D])
            loads = [(w1[:], ins["L0_gnn_w1"]), (w2[:], ins["L0_gnn_w2"]), (w3[:], ins["L0_gnn_w3"]), (lw[:], ins["L0_gnn_lw"]),
                     (lb[:], ins["L0_gnn_lb"][None, :]), (b2[:], ins["L0_gnn_b2"][None, :]), (b3[:], ins["L0_gnn_b3"][None, :]),
                     (b1row[:], ins["L0_gnn_b1"][None, :].to_broadcast([P, 16])),
                     (w2_raw[:], ins["L2_gnn_W"].rearrange("o (a i) -> o a i", a=2)),
                     (bn_b[:], ins["L2_gnn_b"][None, :]), (gamma[:], ins["L2_gnn_gamma"][None, :]), (beta[:], ins["L2_gnn_beta"][None, :]),
                     (w_rel[:], ins["L3_gnn_weights"][2].rearrange("r i o -> i r o")),
                     (b_rel[:], ins["L3_gnn_biases"][2:3].rearrange("l r o -> l (r o)"))]
            with nc.Block() as block:
                @block.sync
                def _(sp):
                    for a, b in loads:
                        sp.dma_start(a, b).then_inc(wl, 16)
                    sp.wait_ge(wl, 16 * len(loads))

                @block.tensor
                def _(pe):
                    pe.wait_ge(wl, 16 * len(loads))
                    nc.tensor.transpose(psw[:, 0, :], w2_raw[:, 0, :], ident[0:D, 0:D])
                    nc.tensor.transpose(psw[:, 1, :], w2_raw[:, 1, :], ident[0:D, 0:D]).then_inc(wt, 1)

                @block.vector
                def _(dve):
                    dve.wait_ge(wt, 1)
                    nc.vector.tensor_copy(w_src[:], psw[:, 1, :]).then_inc(wv, 1)
                    dve.wait_ge(wv, 1)
                    nc.vector.tensor_tensor(w_dst[:], psw[:, 0, :], w_src[:], ALU.subtract).then_inc(wv, 1)

        L0 = ExitStack()
        h16 = sb(L0, "h16", [P, NB, 16])
        dense("h1", X, D, w1[:], None, 16, h16)
        elementwise("h1s", [("v", lambda: TT(h16[:], h16[:], per_node(dinv, 16), ALU.mult))])
        store_table("t1", [(table16, h16[:])])
        edge_pass("p1", table16, 16, 25, with_types=True, zero_fill=batches_of(node_at_edge[0:EPAD, :]))
        carry_stage("c1", 25)
        with ExitStack() as c:
            agg = sb(c, "agg1", [P, NB, 25])
            node_gather("n1", 25, agg)
            a16 = agg[:, :, 0:16]
            elementwise("x2", [
                ("v", lambda: V.tensor_copy(counts[:, :, R:2 * R], agg[:, :, 16:25])),
                ("v", lambda: TT(a16, a16, h16[:], ALU.add)),
                ("v", lambda: TT(a16, a16, per_node(dinv, 16), ALU.mult)),
                ("v", lambda: TT(a16, a16, per_column(b1row, 16), ALU.add)),
                ("v", lambda: V.tensor_scalar_max(a16, a16, 0.0)),
                ("v", lambda: TT(h16[:], a16, per_node(dinv, 16), ALU.mult)),
            ])
        store_table("t2", [(table16b, h16[:])])
        with ExitStack() as c:
            key_lo = sb(c, "key_lo", [P, NT])
            key_hi = sb(c, "key_hi", [P, NT])
            ki = sb(c, "ki", [P, NT], i32)
            iota_ki = sb(c, "iota_ki", [P, NB * R], i32)
            iota_key = sb(c, "iota_key", [P, NB * R], f16)
            made = sem(c, "made_iota")
            with nc.Block() as block:
                @block.gpsimd
                def _(pool):
                    nc.gpsimd.iota(iota_ki[:], pattern=[[1, NB * R]], base=0, channel_multiplier=0).then_inc(made, 1)
            elementwise("keys", [
                ("v", lambda: V.tensor_copy(iota_key[:], iota_ki[:])),
                ("v", lambda: V.tensor_single_scalar(ki[:], src_idx[:, 0:NT], 7, ALU.logical_shift_right)),
                ("v", lambda: V.tensor_copy(key_hi[:], ki[:])),
                ("v", lambda: V.scalar_tensor_tensor(key_hi[:], key_hi[:], float(R), etype[:], ALU.mult, ALU.add)),
                ("v", lambda: V.tensor_single_scalar(ki[:], src_idx[:, 0:NT], P - 1, ALU.bitwise_and)),
                ("v", lambda: V.tensor_copy(key_lo[:], ki[:])),
            ])
            edge_pass("p2", table16b, 16, 16, weighted=True,
                      histogram={"lo": key_lo, "hi": key_hi, "iota": iota_key})
        carry_stage("c2", 16)
        h32 = sb(L0, "h32", [P, NB, 32])
        with ExitStack() as c:
            agg = sb(c, "agg2", [P, NB, 16])
            node_gather("n2", 16, agg)
            elementwise("y2", [
                ("v", lambda: TT(agg[:], agg[:], h16[:], ALU.add)),
                ("v", lambda: TT(agg[:], agg[:], per_node(dinv, 16), ALU.mult)),
            ])
            dense("x3", agg, 16, w2[:], b2[:], 32, h32, relu=True)
            elementwise("x3s", [("v", lambda: TT(h32[:], h32[:], per_node(dinv, 32), ALU.mult))])
        store_table("t3", [(table32, h32[:])])
        edge_pass("p3", table32, 32, 32, weighted=True)
        carry_stage("c3", 32)
        with ExitStack() as c:
            agg = sb(c, "agg3", [P, NB, 32])
            node_gather("n3", 32, agg)
            elementwise("y3", [
                ("v", lambda: TT(agg[:], agg[:], h32[:], ALU.add)),
                ("v", lambda: TT(agg[:], agg[:], per_node(dinv, 32), ALU.mult)),
            ])
            xx = sb(c, "xx", [P, NB, 2 * D])
            dense("x4", agg, 32, w3[:], b3[:], D, xx[:, :, D:2 * D], relu=True)
            elementwise("xcp", [("v", lambda: V.tensor_copy(xx[:, :, 0:D], X[:]))])
            y = sb(c, "y0", [P, NB, D])
            dense("o0", xx, 2 * D, lw[:], lb[:], D, y)
            m = sb(c, "m0", [P, NB])
            v = sb(c, "v0", [P, NB])
            elementwise("ln0", [("v", lambda: TT(y[:], y[:], X[:], ALU.add))]
                        + layernorm_steps(y[:], xx[:, :, 0:D], m[:], v[:], X[:]))
        L0.close()
        store_table("t4", [(table64, X[:])])

        edge_pass("p4", table64, D, 2 * D, squares=True)
        carry_stage("c4", 2 * D)
        with ExitStack() as c:
            agg = sb(c, "agg4", [P, NB, 2 * D])
            node_gather("n4", 2 * D, agg)
            m = sb(c, "m1", [P, NB])
            v = sb(c, "v1", [P, NB])
            s1, s2 = agg[:, :, 0:D], agg[:, :, D:2 * D]
            sq = sb(c, "sq1", [P, NB, D])
            elementwise("std", [
                ("v", lambda: V.tensor_scalar_max(m[:], count[:], COUNT_EPS)),
                ("v", lambda: V.reciprocal(m[:], m[:])),
                ("v", lambda: TT(s1, s1, per_node(m, D), ALU.mult)),
                ("v", lambda: TT(s2, s2, per_node(m, D), ALU.mult)),
                ("v", lambda: TT(s1, s1, s1, ALU.mult)),
                ("v", lambda: TT(s2, s2, s1, ALU.subtract)),
                ("v", lambda: V.tensor_scalar_max(s2, s2, 0.0)),
                ("a", lambda: nc.scalar.sqrt(s1, s2)),
                ("v", lambda: V.tensor_single_scalar(v[:], count[:], 1.0, ALU.is_gt)),
                ("v", lambda: TT(s1, s1, per_node(v, D), ALU.mult)),
                ("v", lambda: TT(s1, s1, X[:], ALU.add)),
            ] + layernorm_steps(s1, sq[:], m[:], v[:], X[:]))

        with ExitStack() as c:
            q_rows = sb(c, "q_rows", [P, NB, D])
            p_rows = sb(c, "p_rows", [P, NB, D])
            dense("dq", X, D, w_src[:], None, D, q_rows)
            dense("dp", X, D, w_dst[:], bn_b[:], D, p_rows)
            store_table("t5", [(table_q, q_rows[:]), (table_p, p_rows[:])])
            slot = sb(c, "slot", [P, 2, GROUP, D])
            sidx = sb(c, "sidx", [P, 2, GROUP], i32)
            heads = sb(c, "heads", [QH, HALVES, QT * D])
            ready = sem(c, "sc_ready")
            idxs = sem(c, "sc_idx")
            out_s = [sem(c, f"sc_out{k}") for k in range(2)]
            head_got = sem(c, "head_got")
            head_put = sem(c, "head_put")
            with nc.Block() as block:
                @block.vector
                def _(dve):
                    def step(i, first):
                        for k in range(2):
                            if not first:
                                dve.wait_ge(out_s[k], i * (16 * GROUP))
                            nc.vector.tensor_copy(slot[:, k, :, :], p_rows[:, bass.ds((2 * i + k) * GROUP, GROUP), :]).then_inc(ready, 1)
                    step(0, True)
                    with dve.Fori(1, NGROUPS // 2) as i:
                        step(i, False)

                @block.scalar
                def _(act):
                    def step(i, first):
                        for k in range(2):
                            if not first:
                                act.wait_ge(out_s[k], i * (16 * GROUP))
                            nc.scalar.copy(sidx[:, k, :], start_row[:, bass.ds((2 * i + k) * GROUP, GROUP)]).then_inc(idxs, 1)
                    step(0, True)
                    with act.Fori(1, NGROUPS // 2) as i:
                        step(i, False)

                @block.gpsimd
                def _(pool):
                    with pool.Fori(0, NGROUPS // 2) as i:
                        for k in range(2):
                            pool.wait_ge(ready, 2 * i + k + 1)
                            pool.wait_ge(idxs, 2 * i + k + 1)
                            settled(pool)
                            for u in range(GROUP):
                                nc.gpsimd.indirect_dma_start(node_at_edge, bass.IndirectOffsetOnAxis(sidx[:, k, u:u + 1], 0),
                                                             slot[:, k, u, :], None).then_inc(out_s[k], 16)
                    for t in range(2 * QT):
                        nc.gpsimd.indirect_dma_start(heads[:, t // QT, (t % QT) * D:(t % QT + 1) * D], None, table_p,
                                                     bass.IndirectOffsetOnAxis(first_dst[0:QH, t:t + 1], 0)).then_inc(head_got, 16)

                @block.sync
                def _(sp):
                    for k in range(2):
                        sp.wait_ge(out_s[k], (NGROUPS // 2) * 16 * GROUP)
                    sp.wait_ge(head_got, 16 * 2 * QT)
                    v = node_at_edge[0:EPAD, :].rearrange("(h q e j) w -> q h e (j w)", h=HALVES, q=QH, e=P)
                    for h in range(HALVES):
                        sp.dma_start(v[:, h, 0, :], heads[:, h, :]).then_inc(head_put, 16)
                    sp.wait_ge(head_put, 32)

        stat_ctx = ExitStack()
        scale_b = sb(stat_ctx, "scale_b", [P, D])
        shift_b = sb(stat_ctx, "shift_b", [P, D])
        with ExitStack() as c:
            idx = sb(c, "e_idx", [P, SLOTS, QT], i32)
            spread = sb(c, "spread", [P, SLOTS, QT, P])
            msg = sb(c, "e_msg", [P, SLOTS, QT, D])
            at_edge = sb(c, "at_edge", [P, SLOTS, QT, D])
            hid = sb(c, "hid", [P, SLOTS, QT, D])
            hid_sq = sb(c, "hid_sq", [P, SLOTS, QT, D])
            acc = [pb(c, f"e_acc{k}", [P, QT * D]) for k in range(2)]
            moment = [pb(c, f"moment{k}", [1, QT * D]) for k in range(2)]
            got = [sem(c, f"e_got{k}") for k in range(SLOTS)]
            loaded = [sem(c, f"e_loaded{k}") for k in range(SLOTS)]
            stored = [sem(c, f"e_stored{k}") for k in range(SLOTS)]
            idx_ready = sem(c, "e_idx_ready")
            matrix_ready = sem(c, "e_matrix_ready")
            spread_done = sem(c, "e_spread_done")
            hid_ready = sem(c, "e_hid_ready")
            sq_ready = sem(c, "e_sq_ready")
            moments_done = sem(c, "e_moments_done")
            iters = NQ // SLOTS
            in_b = batches_of(node_at_edge[0:EPAD, :])
            out_b = batches_of(messages)
            last_tiles = [min(P, max(0, N_EDGES - ((NQ - 1) * EB + u * P))) for u in range(QT)]
            with nc.Block() as block:
                @block.gpsimd
                def _(pool):
                    def step(i, first):
                        for k in range(SLOTS):
                            pool.wait_ge(idx_ready, i * SLOTS + k + 1)
                            if not first:
                                pool.wait_ge(hid_ready, (i - 1) * SLOTS + k + 1)
                            settled(pool)
                            for u in range(QT):
                                nc.gpsimd.indirect_dma_start(msg[:, k, u, :], None, table_q,
                                                             bass.IndirectOffsetOnAxis(idx[:, k, u:u + 1], 0)).then_inc(got[k], 16)
                    step(0, True)
                    with pool.Fori(1, iters) as i:
                        step(i, False)

                @block.sync
                def _(sp):
                    for k in range(2):
                        sp.dma_start(at_edge[:, k, :, :].rearrange("p j d -> p (j d)"), in_b[k]).then_inc(loaded[k], 16)

                    def step(i, first, final):
                        for k in range(SLOTS):
                            ahead = (k + 2) % SLOTS
                            if not (final and k >= 2):
                                if not (first and k < 2):
                                    sp.wait_ge(spread_done, i * SLOTS + k - 1)
                                sp.dma_start(at_edge[:, ahead, :, :].rearrange("p j d -> p (j d)"), in_b[i * SLOTS + k + 2]).then_inc(loaded[ahead], 16)
                            sp.wait_ge(hid_ready, i * SLOTS + k + 1)
                            sp.dma_start(out_b[i * SLOTS + k], hid[:, k, :, :].rearrange("p j d -> p (j d)")).then_inc(stored[k], 16)
                    step(0, True, False)
                    with sp.Fori(1, iters - 1) as i:
                        step(i, False, False)
                    step(iters - 1, False, True)
                    for k in range(SLOTS):
                        sp.wait_ge(stored[k], iters * 16)

                @block.scalar
                def _(act):
                    for k in range(2):
                        nc.scalar.copy(idx[:, k, :], src_idx[:, k * QT:(k + 1) * QT]).then_inc(idx_ready, 1)

                    def step(i, first):
                        for k in range(SLOTS):
                            ahead = (k + 2) % SLOTS
                            if not (first and k < 2):
                                act.wait_ge(got[ahead], (i if k < 2 else i + 1) * (16 * QT))
                            nc.scalar.copy(idx[:, ahead, :], src_idx[:, bass.ds((i * SLOTS + k + 2) * QT, QT)]).then_inc(idx_ready, 1)
                            act.wait_ge(hid_ready, i * SLOTS + k + 1)
                            if not first:
                                act.wait_ge(moments_done, (i - 1) * SLOTS + k + 1)
                            nc.scalar.square(hid_sq[:, k, :, :], hid[:, k, :, :]).then_inc(sq_ready, 1)
                    step(0, True)
                    with act.Fori(1, iters) as i:
                        step(i, False)

                @block.vector
                def _(dve):
                    def step(i, first):
                        for k in range(SLOTS):
                            if not first:
                                dve.wait_ge(spread_done, (i - 1) * SLOTS + k + 1)
                            for u in range(QT):
                                t = i * (SLOTS * QT) + k * QT + u
                                last = nc.vector.tensor_scalar(spread[:, k, u, :], iota_upper[:], seg_end_first[:, bass.ds(t, 1)], None, ALU.is_le)
                            last.then_inc(matrix_ready, 1)
                            dve.wait_ge(spread_done, i * SLOTS + k + 1)
                            dve.wait_ge(got[k], (i + 1) * (16 * QT))
                            if not first:
                                dve.wait_ge(stored[k], i * 16)
                                dve.wait_ge(moments_done, (i - 1) * SLOTS + k + 1)
                            nc.vector.tensor_tensor(hid[:, k, :, :].rearrange("p j d -> p (j d)"), acc[k % 2][:],
                                                    msg[:, k, :, :].rearrange("p j d -> p (j d)"), ALU.add).then_inc(hid_ready, 1)
                    step(0, True)
                    with dve.Fori(1, iters) as i:
                        step(i, False)

                @block.tensor
                def _(pe):
                    def step(i, first, final):
                        for k in range(SLOTS):
                            pe.wait_ge(matrix_ready, i * SLOTS + k + 1)
                            pe.wait_ge(loaded[k], (i + 1) * 16)
                            if not (first and k < 2):
                                pe.wait_ge(hid_ready, i * SLOTS + k - 1)
                            for u in range(QT):
                                last = nc.tensor.matmul(acc[k % 2][:, u * D:(u + 1) * D], spread[:, k, u, :], at_edge[:, k, u, :], start=True, stop=True)
                            last.then_inc(spread_done, 1)
                            pe.wait_ge(sq_ready, i * SLOTS + k + 1)
                            begin = first and k == 0
                            if final and k == SLOTS - 1:
                                for m_ps, a in ((moment[0], hid), (moment[1], hid_sq)):
                                    for u in range(QT):
                                        n = last_tiles[u]
                                        if n:
                                            stop = u == QT - 1 or not last_tiles[u + 1]
                                            last = nc.tensor.matmul(m_ps[:, u * D:(u + 1) * D], ones[0:n, 0:1], a[0:n, k, u, :], start=False, stop=stop)
                            else:
                                for m_ps, a in ((moment[0], hid), (moment[1], hid_sq)):
                                    last = nc.tensor.matmul(m_ps[:], ones[:, 0:1], a[:, k, :, :].rearrange("p j d -> p (j d)"), start=begin, stop=False)
                            last.then_inc(moments_done, 1)
                    step(0, True, False)
                    with pe.Fori(1, iters - 1) as i:
                        step(i, False, False)
                    step(iters - 1, False, True)

            mu = sb(c, "mu", [1, D])
            va = sb(c, "va", [1, D])
            tq = sb(c, "tq", [1, D])
            bc = pb(c, "bc", [P, 2, D])
            s_st = sem(c, "s_st")
            s_bc = sem(c, "s_bc")
            s_bo = sem(c, "s_bo")
            elementwise("bn", [
                ("v", lambda: V.reduce_sum(mu[:], moment[0][:].rearrange("p (j d) -> p d j", j=QT), AX.X)),
                ("v", lambda: V.reduce_sum(va[:], moment[1][:].rearrange("p (j d) -> p d j", j=QT), AX.X)),
                ("v", lambda: V.tensor_scalar_mul(mu[:], mu[:], 1.0 / N_EDGES)),
                ("v", lambda: TT(tq[:], mu[:], mu[:], ALU.mult)),
                ("v", lambda: V.scalar_tensor_tensor(va[:], va[:], 1.0 / N_EDGES, tq[:], ALU.mult, ALU.subtract)),
                ("v", lambda: V.tensor_scalar(va[:], va[:], 0.0, BN_EPS, ALU.max, ALU.add)),
                ("a", lambda: nc.scalar.sqrt(va[:], va[:])),
                ("v", lambda: V.reciprocal(tq[:], va[:])),
                ("v", lambda: TT(tq[:], tq[:], gamma[:], ALU.mult)),
                ("v", lambda: TT(mu[:], mu[:], tq[:], ALU.mult)),
                ("v", lambda: TT(mu[:], beta[:], mu[:], ALU.subtract)),
            ])
            with nc.Block() as block:
                @block.tensor
                def _(pe):
                    nc.tensor.matmul(bc[:, 0, :], ones[0:1, :], tq[:], start=True, stop=True)
                    nc.tensor.matmul(bc[:, 1, :], ones[0:1, :], mu[:], start=True, stop=True).then_inc(s_bc, 1)

                @block.vector
                def _(dve):
                    dve.wait_ge(s_bc, 1)
                    nc.vector.tensor_copy(scale_b[:], bc[:, 0, :]).then_inc(s_bo, 1)
                    nc.vector.tensor_copy(shift_b[:], bc[:, 1, :]).then_inc(s_bo, 1)

        with ExitStack() as c:
            seg = sb(c, "f_seg", [P, SLOTS, QT, P])
            hid = sb(c, "f_hid", [P, SLOTS, QT, D])
            act_h = sb(c, "f_act", [P, SLOTS, QT, D])
            tmp_h = sb(c, "f_tmp", [P, QT, D])
            summed = sb(c, "f_sum", [P, SLOTS, QT * D])
            acc = [pb(c, f"f_acc{k}", [P, QT * D]) for k in range(2)]
            loaded = [sem(c, f"f_loaded{k}") for k in range(SLOTS)]
            stored = [sem(c, f"f_stored{k}") for k in range(SLOTS)]
            matrix_ready = sem(c, "f_matrix_ready")
            leaky_ready = sem(c, "f_leaky_ready")
            product_done = sem(c, "f_product_done")
            evicted = sem(c, "f_evicted")
            ch = sem(c, "f_chain")
            ch2 = sem(c, "f_chain2")
            iters = NQ // SLOTS
            in_b = batches_of(messages)
            out_b = batches_of(prefix[D])
            with nc.Block() as block:
                @block.sync
                def _(sp):
                    def load(b, k):
                        sp.dma_start(hid[:, k, :, :].rearrange("p j d -> p (j d)"), in_b[b]).then_inc(loaded[k], 16)
                    for k in range(SLOTS):
                        load(k, k)
                    with sp.Fori(1, iters) as i:
                        for k in range(SLOTS):
                            sp.wait_ge(leaky_ready, (i - 1) * SLOTS + k + 1)
                            load(i * SLOTS + k, k)

                @block.gpsimd
                def _(pool):
                    with pool.Fori(0, iters) as i:
                        for k in range(SLOTS):
                            pool.wait_ge(evicted, i * SLOTS + k + 1)
                            pool.dma_start(out_b[i * SLOTS + k], summed[:, k, :]).then_inc(stored[k], 16)
                    for k in range(SLOTS):
                        pool.wait_ge(stored[k], iters * 16)

                @block.scalar
                def _(act):
                    def step(i, first):
                        for k in range(SLOTS):
                            act.wait_ge(product_done, i * SLOTS + k + 1)
                            if not first:
                                act.wait_ge(stored[k], i * 16)
                            nc.scalar.copy(summed[:, k, :], acc[k % 2][:]).then_inc(evicted, 1)
                    step(0, True)
                    with act.Fori(1, iters) as i:
                        step(i, False)

                @block.vector
                def _(dve):
                    def step(i, first):
                        for k in range(SLOTS):
                            b = i * SLOTS + k
                            dve.wait_ge(loaded[k], (i + 1) * 16)
                            nc.vector.tensor_tensor(hid[:, k, :, :], hid[:, k, :, :],
                                                    scale_b[:, None, :].to_broadcast([P, QT, D]), ALU.mult).then_inc(ch, 1)
                            if not first:
                                dve.wait_ge(product_done, (i - 1) * SLOTS + k + 1)
                            for u in range(QT):
                                t = i * (SLOTS * QT) + k * QT + u
                                last = nc.vector.tensor_scalar(seg[:, k, u, :], iota_upper[:], seg_end[:, bass.ds(t, 1)], None, ALU.is_le)
                            last.then_inc(matrix_ready, 1)
                            dve.wait_ge(ch, b + 1)
                            nc.vector.tensor_tensor(tmp_h[:], hid[:, k, :, :],
                                                    shift_b[:, None, :].to_broadcast([P, QT, D]), ALU.add).then_inc(ch2, 1)
                            dve.wait_ge(ch2, b + 1)
                            nc.vector.scalar_tensor_tensor(act_h[:, k, :, :], tmp_h[:], SLOPE, tmp_h[:], ALU.mult, ALU.max).then_inc(leaky_ready, 1)
                    step(0, True)
                    with dve.Fori(1, iters) as i:
                        step(i, False)

                @block.tensor
                def _(pe):
                    def step(i, first):
                        for k in range(SLOTS):
                            pe.wait_ge(matrix_ready, i * SLOTS + k + 1)
                            pe.wait_ge(leaky_ready, i * SLOTS + k + 1)
                            if not (first and k < 2):
                                pe.wait_ge(evicted, i * SLOTS + k - 1)
                            for u in range(QT):
                                last = nc.tensor.matmul(acc[k % 2][:, u * D:(u + 1) * D], seg[:, k, u, :], act_h[:, k, u, :], start=True, stop=True)
                            last.then_inc(product_done, 1)
                    step(0, True)
                    with pe.Fori(1, iters) as i:
                        step(i, False)
        stat_ctx.close()
        carry_stage("c5", D)
        with ExitStack() as c:
            agg = sb(c, "agg5", [P, NB, D])
            node_gather("n5", D, agg)
            m = sb(c, "m2", [P, NB])
            v = sb(c, "v2", [P, NB])
            sq = sb(c, "sq2", [P, NB, D])
            elementwise("ln2", [
                ("v", lambda: V.tensor_scalar_max(m[:], count[:], 1.0)),
                ("v", lambda: V.reciprocal(m[:], m[:])),
                ("v", lambda: TT(agg[:], agg[:], per_node(m, D), ALU.mult)),
                ("v", lambda: TT(agg[:], agg[:], X[:], ALU.add)),
            ] + layernorm_steps(agg[:], sq[:], m[:], v[:], X[:]))

        with ExitStack() as c:
            y = sb(c, "y3r", [P, NB, D])
            row = sb(c, "r_row", [P, 2, D])
            turned_sb = sb(c, "r_turned", [D, 2, P])
            prod = sb(c, "r_prod", [P, 2, 2 * R, D])
            pt = [pb(c, f"r_pt{k}", [D, P]) for k in range(2)]
            T3 = 2 * R * D // 3
            po = [[pb(c, f"r_po{k}_{a}", [P, T3]) for a in range(3)] for k in range(2)]
            row_ready = sem(c, "r_row_ready")
            t_done = sem(c, "r_t_done")
            t_out = sem(c, "r_t_out")
            m_done = sem(c, "r_m_done")
            m_out = sem(c, "r_m_out")
            iters = NB // 2
            with nc.Block() as block:
                @block.scalar
                def _(act):
                    def step(i, first):
                        for k in range(2):
                            if not first:
                                act.wait_ge(t_done, 2 * i + k - 1)
                            nc.scalar.copy(row[:, k, :], X[:, bass.ds(2 * i + k, 1), :].rearrange("p a d -> p (a d)")).then_inc(row_ready, 1)
                        for k in range(2):
                            act.wait_ge(t_done, 2 * i + k + 1)
                            if not first:
                                act.wait_ge(m_done, 2 * i + k - 1)
                            nc.scalar.copy(turned_sb[:, k, :], pt[k][:]).then_inc(t_out, 1)
                    step(0, True)
                    with act.Fori(1, iters) as i:
                        step(i, False)

                @block.tensor
                def _(pe):
                    def step(i, first):
                        for k in range(2):
                            pe.wait_ge(row_ready, 2 * i + k + 1)
                            if not first:
                                pe.wait_ge(t_out, 2 * i + k - 1)
                            settled(pe)
                            nc.tensor.transpose(pt[k][:], row[:, k, :], ident[:]).then_inc(t_done, 1)
                        for k in range(2):
                            pe.wait_ge(t_out, 2 * i + k + 1)
                            if not first:
                                pe.wait_ge(m_out, 2 * i + k - 1)
                            for a in range(3):
                                nc.tensor.matmul(po[k][a][:], turned_sb[:, k, :],
                                                 w_rel[:].rearrange("i r o -> i (r o)")[:, a * T3:(a + 1) * T3], start=True, stop=False)
                                last = nc.tensor.matmul(po[k][a][:], ones[0:1, :], b_rel[:, a * T3:(a + 1) * T3], start=False, stop=True)
                            last.then_inc(m_done, 1)
                    step(0, True)
                    with pe.Fori(1, iters) as i:
                        step(i, False)

                @block.vector
                def _(dve):
                    with dve.Fori(0, iters) as i:
                        for k in range(2):
                            dve.wait_ge(m_done, 2 * i + k + 1)
                            n = 2 * i + k
                            for a in range(3):
                                r3 = 2 * R // 3
                                cv = counts[:, bass.ds(n, 1), a * r3:(a + 1) * r3].rearrange("p a r -> p (a r)")[:, :, None].to_broadcast([P, r3, D])
                                last = nc.vector.tensor_tensor(prod[:, k, a * r3:(a + 1) * r3, :], po[k][a][:].rearrange("p (r o) -> p r o", o=D), cv, ALU.mult)
                            last.then_inc(m_out, 1)
                            dve.wait_ge(m_out, n + 1)
                            nc.vector.reduce_sum(y[:, bass.ds(n, 1), :].rearrange("p a d -> p (a d)"), prod[:, k, :, :].rearrange("p r o -> p o r"), AX.X)
            m = sb(c, "m3", [P, NB])
            v = sb(c, "v3", [P, NB])
            sq = sb(c, "sq3", [P, NB, D])
            elementwise("ln3", [
                ("v", lambda: V.reduce_sum(m[:], counts[:], AX.X)),
                ("v", lambda: V.tensor_single_scalar(v[:], m[:], 0.0, ALU.is_gt)),
                ("v", lambda: V.tensor_scalar_max(m[:], m[:], 1.0)),
                ("v", lambda: V.reciprocal(m[:], m[:])),
                ("v", lambda: TT(m[:], m[:], v[:], ALU.mult)),
                ("v", lambda: TT(y[:], y[:], per_node(m, D), ALU.mult)),
                ("v", lambda: TT(y[:], y[:], X[:], ALU.add)),
            ] + layernorm_steps(y[:], sq[:], m[:], v[:], X[:]))
            written = sem(c, "written")
            with nc.Block() as block:
                @block.sync
                def _(sp):
                    sp.dma_start(out[0:(NB - 1) * P, :].rearrange("(h l) d -> l h d", l=P), X[:, 0:NB - 1, :]).then_inc(written, 16)
                    sp.dma_start(out[(NB - 1) * P:N_NODES, :], X[0:N_NODES - (NB - 1) * P, NB - 1, :]).then_inc(written, 16)
                    sp.wait_ge(written, 32)


_INS = ["x", "src", "dst", "edge_type_9", "edge_weight", "L0_gnn_w1", "L0_gnn_b1", "L0_gnn_w2", "L0_gnn_b2", "L0_gnn_w3",
        "L0_gnn_b3", "L0_gnn_lw", "L0_gnn_lb", "L2_gnn_W", "L2_gnn_b", "L2_gnn_gamma", "L2_gnn_beta", "L3_gnn_weights",
        "L3_gnn_biases"]


def kernel(**inputs):
    import numpy as np
    import concourse.bacc as bacc
    from concourse.bass_utils import run_bass_kernel_spmd

    nc = bacc.Bacc("TRN2", target_bir_lowering=False, num_devices=1)
    arrays, args = {}, {}
    for name in _INS:
        a = np.ascontiguousarray(inputs[name])
        arrays[f"in_{name}"] = a
        args[name] = nc.dram_tensor(f"in_{name}", a.shape, mybir.dt.from_np(a.dtype), kind="ExternalInput").ap()
    out = nc.dram_tensor("out_0", (N_NODES, D), mybir.dt.float32, kind="ExternalOutput").ap()
    gnn_kernel(nc, args, out)
    r = run_bass_kernel_spmd(nc, [arrays], core_ids=[0])
    return r.results[0]["out_0"]
```

```python
import concourse.bass as bass
from concourse import mybir
from contextlib import ExitStack


P = 128
N_NODES, N_EDGES, D, R = 12500, 200000, 64, 9
NB = -(-N_NODES // P)
NPAD = NB * P
QT = 8
EB = QT * P
NQ = -(-N_EDGES // EB)
NT = NQ * QT
EPAD = NT * P
QH = NQ // 2
HALVES = 2
PAD_NODE = NPAD - 1
SLOTS = 4
GROUP = 7
NGROUPS = NB // GROUP
LN_EPS = 1e-5
BN_EPS = 1e-5
COUNT_EPS = 1e-8
SLOPE = 0.3
assert NQ % (2 * SLOTS) in (0, SLOTS) and NQ % SLOTS == 0 and NB % (2 * GROUP) == 0


def gnn_kernel(nc, ins, out):
    f32, i32, bf16, f16 = mybir.dt.float32, mybir.dt.int32, mybir.dt.bfloat16, mybir.dt.float16
    ALU = mybir.AluOpType
    ACT = mybir.ActivationFunctionType
    AX = mybir.AxisListType
    root = ExitStack()
    semaphores_of = {}

    def sb(ctx, name, shape, dt=f32):
        return ctx.enter_context(nc.sbuf_tensor(name, shape, dt))

    def pb(ctx, name, shape, dt=f32):
        return ctx.enter_context(nc.psum_tensor(name, shape, dt))

    def sem(ctx, name):
        held = semaphores_of.get(id(ctx))
        if held is None:
            held = semaphores_of[id(ctx)] = []

            def release():
                nc.clear_and_free_semaphores(held)
                del semaphores_of[id(ctx)]
                with nc.Block():
                    pass
            ctx.callback(release)
        held.append(nc.alloc_semaphore(name))
        return held[-1]

    def dram(name, shape, dt=f32):
        return nc.dram_tensor(name, shape, dt).ap()

    table16 = dram("table16", (NPAD, 16))
    table16b = dram("table16b", (NPAD, 16))
    table32 = dram("table32", (NPAD, 32))
    table64 = dram("table64", (NPAD, D))
    table_q = dram("table_q", (NPAD, D))
    table_p = dram("table_p", (NPAD, D))
    windows = dram("windows", (NT + 1, 2 * P))
    prefix = {w: dram(f"prefix{w}", (EPAD, w)) for w in (25, 16, 32, 128, 64)}
    messages = dram("messages", (EPAD, D))
    node_at_edge = dram("node_at_edge", (EPAD + NPAD, D))

    with root:
        ident = sb(root, "ident", [P, P])
        anti = sb(root, "anti", [P, P])
        ones = sb(root, "ones", [P, P])
        upper = sb(root, "upper", [P, P])
        iota_row = sb(root, "iota_row", [P, P])
        iota_upper = sb(root, "iota_upper", [P, P])
        X = sb(root, "X", [P, NB, D])
        src_idx = sb(root, "src_idx", [P, NT + 2 * QT], i32)
        weight = sb(root, "weight", [P, NT])
        seg_end = sb(root, "seg_end", [P, NT])
        seg_end_first = sb(root, "seg_end_first", [P, NT])
        etype = sb(root, "etype", [P, NT])
        carry_on = sb(root, "carry_on", [P, NT])
        linked = sb(root, "linked", [P, 2 * QT])
        node_f = sb(root, "node_f", [P, NB])
        h16 = sb(root, "h16", [P, NB, 16])
        fix_row = sb(root, "fix_row", [P, 2 * QT], i32)
        first_dst = sb(root, "first_dst", [P, 2 * QT], i32)
        end_row = sb(root, "end_row", [P, NB], i32)
        start_row = sb(root, "start_row", [P, NB], i32)
        count = sb(root, "count", [P, NB])
        several = sb(root, "several", [P, NB])
        nonempty = sb(root, "nonempty", [P, NB])
        dinv = sb(root, "dinv", [P, NB])
        counts = sb(root, "counts", [P, NB, 2 * R])

        def chain_of(engine, s):
            n = [0]

            def link(instruction):
                n[0] += 1
                instruction.then_inc(s, 1)
                engine.wait_ge(s, n[0])
            return link

        turns = [sem(root, "turns_pe"), sem(root, "turns_pool")]

        def settled(engine):
            engine.sem_inc(turns[engine is nc.gpsimd], 1)

        def per_half(ap):
            return ap.rearrange("p (h q j) -> p h j q", h=HALVES, j=QT)

        w_first = sb(root, "w_first", [D + 1, 16 + D])
        w2a = sb(root, "w2a", [33, 32])
        w3a = sb(root, "w3a", [33, D])
        lw_low = sb(root, "lw_low", [D, D])
        b1row = sb(root, "b1row", [P, 16])
        w_qp = sb(root, "w_qp", [D, 2 * D])
        bn_b = sb(root, "bn_b", [1, D])
        gamma = sb(root, "gamma", [1, D])
        beta = sb(root, "beta", [1, D])
        w_rel = sb(root, "w_rel", [D + 1, 2 * R, D])
        bias_sgn = sb(root, "bias_sgn", [1, D])
        lhs65 = sb(root, "lhs65", [D + 1, 2, GROUP * P])
        lhs33 = sb(root, "lhs33", [33, 2, GROUP * P])
        zeroed_weights = [w_first[:], w2a[:], lhs33[:]]
        unit_rows = [lhs65[D:D + 1, :, :], lhs33[32:33, :, :]]

        def loads(w2_raw):
            lw = ins["L0_gnn_lw"]
            return [(w_first[0:D, 0:16], ins["L0_gnn_w1"]), (w_first[0:D, 16:16 + D], lw[0:D, :]),
                    (w_first[D:D + 1, 16:16 + D], ins["L0_gnn_lb"][None, :]),
                    (w2a[0:16, :], ins["L0_gnn_w2"]), (w2a[32:33, :], ins["L0_gnn_b2"][None, :]),
                    (w3a[0:32, :], ins["L0_gnn_w3"]), (w3a[32:33, :], ins["L0_gnn_b3"][None, :]),
                    (lw_low[:], lw[D:2 * D, :]),
                    (b1row[:], ins["L0_gnn_b1"][None, :].to_broadcast([P, 16])),
                    (w2_raw[:], ins["L2_gnn_W"].rearrange("o (a i) -> o a i", a=2)),
                    (bn_b[:], ins["L2_gnn_b"][None, :]), (gamma[:], ins["L2_gnn_gamma"][None, :]),
                    (beta[:], ins["L2_gnn_beta"][None, :]),
                    (w_rel[0:D, :, :], ins["L3_gnn_weights"][2].rearrange("r i o -> i r o")),
                    (w_rel[D:D + 1, :, :], ins["L3_gnn_biases"][2:3])]

        def skewed(engine, parts, first_at=2):
            lag = max(n for n, _ in parts)
            begin = 2 * ((max(lag + first_at, 2) + 1) // 2)
            steps = NGROUPS - begin

            def step(s, i, k):
                for n, f in parts:
                    g = s - n
                    if not isinstance(s, int):
                        f(g, i + (k - n) // 2, (k - n) % 2, False)
                    elif 0 <= g < NGROUPS:
                        f(g, g // 2, g % 2, g < first_at)
            for s in range(begin):
                step(s, s // 2, s % 2)
            with engine.Fori(begin // 2, NGROUPS // 2) as i:
                for k in range(2):
                    step(2 * i + k, i, k)
            for s in range(NGROUPS, NGROUPS + lag):
                step(s, s // 2, s % 2)

        V = nc.vector
        TT = nc.vector.tensor_tensor

        edges_ctx = ExitStack()
        iota_i = sb(edges_ctx, "iota_i", [P, P], i32)
        node_i = sb(edges_ctx, "node_i", [P, NB], i32)
        ew_f = sb(edges_ctx, "ew_f", [QH, HALVES, EB])
        src_f = sb(edges_ctx, "src_f", [QH, HALVES, EB])
        dst_f = sb(edges_ctx, "dst_f", [QH, HALVES, EB])
        typ_f = sb(edges_ctx, "typ_f", [QH, HALVES, EB])
        below = sb(edges_ctx, "below", [P, P])
        corner = sb(edges_ctx, "corner", [P, P])
        prev_f = sb(edges_ctx, "prev_f", [QH, HALVES])
        next_f = sb(edges_ctx, "next_f", [QH, HALVES])
        tau = sb(edges_ctx, "tau", [P, NB])
        tau_i = sb(edges_ctx, "tau_i", [P, NB], i32)
        qbase = sb(edges_ctx, "qbase", [QH, 2 * QT], i32)
        full = N_EDGES // EB - QH
        rest = N_EDGES - (QH + full) * EB
        inner = ExitStack()
        src_i = sb(inner, "src_i", [QH, HALVES, EB], i32)
        dst_i = sb(inner, "dst_i", [QH, HALVES, EB], i32)
        typ_i = sb(inner, "typ_i", [QH, HALVES, EB], i32)
        prev_i = sb(inner, "prev_i", [QH, HALVES], i32)
        next_i = sb(inner, "next_i", [QH, HALVES], i32)
        w2_raw = sb(inner, "w2_raw", [D, 2, D])
        head = sb(inner, "head", [QH, HALVES, EB])
        same = sb(inner, "q_same", [QH, HALVES, EB])
        running_w = sb(inner, "running_w", [QH, HALVES, EB])
        tile_end = sb(inner, "tile_end", [QH, 2 * QT], i32)
        tile_lo = sb(inner, "tile_lo", [QH, 2 * QT])
        tile_hi = sb(inner, "tile_hi", [QH, 2 * QT])
        bits = sb(inner, "bits", [QH, 2 * QT], i32)
        lo_hot = sb(inner, "lo_hot", [QH, 2 * QT, P])
        hi_hot = sb(inner, "hi_hot", [QH, 2 * QT, NB])
        tiles_at = sb(inner, "tiles_at", [P, NB])
        all_q = sb(inner, "all_q", [P, NB])
        run_q = sb(inner, "run_q", [P, NB])
        link_q = sb(inner, "link_q", [QH, HALVES])
        chain_q = sb(inner, "chain_q", [QH, HALVES])
        last_q = sb(inner, "last_q", [QH, HALVES])
        row_q = sb(inner, "row_q", [1, 2 * NQ])
        run_row = sb(inner, "run_row", [1, 1 + NQ])
        carry_in = sb(inner, "carry_in", [QH, HALVES])
        far = sb(inner, "far", [1, 2 * P])
        sgn = sb(inner, "sgn", [1, D])
        s_pad = sem(inner, "s_pad")
        s_dst = sem(inner, "s_dst")
        s_ew = sem(inner, "s_ew")
        s_rest = sem(inner, "s_rest")
        s_wts = sem(inner, "s_wts")
        s_const = sem(inner, "s_const")
        s_dve = sem(inner, "s_dve")
        s_hot = sem(inner, "s_hot")
        s_tiles = sem(inner, "s_tiles")
        s_cum = sem(inner, "s_cum")
        s_rowq = sem(inner, "s_rowq")
        s_colq = sem(inner, "s_colq")
        s_scan = sem(inner, "s_scan")
        s_dstwin = sem(inner, "s_dstwin")
        s_prewin = sem(inner, "s_prewin")
        s_win = sem(inner, "s_win")
        s_wraw = sem(inner, "s_wraw")
        s_sgn = sem(inner, "s_sgn")
        hist = pb(inner, "tile_hist", [P, NB])
        incl = pb(inner, "incl", [P, NB])
        totals = pb(inner, "totals", [P, NB])
        psq = pb(inner, "psq", [1, 2 * NQ])
        psc = pb(inner, "psc", [QH, HALVES])
        psw = pb(inner, "psw", [D, 3, D])

        def edge_rows(a):
            return [(lambda t: t[:, 0, :], a[0:QH * EB].rearrange("(q e) -> q e", e=EB)),
                    (lambda t: t[0:full, 1, :], a[QH * EB:(QH + full) * EB].rearrange("(q e) -> q e", e=EB)),
                    (lambda t: t[full:full + 1, 1, 0:rest], a[(QH + full) * EB:N_EDGES].rearrange("(q e) -> q e", q=1))]

        CONSTANTS = 16

        with nc.Block() as block:
            @block.gpsimd
            def _(pool):
                link = chain_of(pool, s_const)
                G = nc.gpsimd
                link(G.iota(iota_i[:], pattern=[[1, P]], base=0, channel_multiplier=0))
                link(G.tensor_copy(iota_row[:], iota_i[:]))
                link(G.memset(ones[:], 1.0))
                link(G.memset(ident[:], 0.0))
                link(G.memset(anti[:], 0.0))
                link(G.affine_select(out=ident[:], in_=ident[:], compare_op=ALU.not_equal, fill=1.0,
                                     base=0, pattern=[[1, P]], channel_multiplier=-1))
                link(G.affine_select(out=upper[:], in_=ones[:], compare_op=ALU.is_ge, fill=0.0,
                                     base=0, pattern=[[1, P]], channel_multiplier=-1))
                link(G.affine_select(out=anti[:], in_=anti[:], compare_op=ALU.not_equal, fill=1.0,
                                     base=-(P - 1), pattern=[[1, P]], channel_multiplier=1))
                link(G.affine_select(out=iota_upper[:], in_=iota_row[:], compare_op=ALU.is_ge,
                                     fill=999.0, base=0, pattern=[[1, P]], channel_multiplier=-1))
                link(G.memset(below[:], 0.0))
                link(G.memset(corner[:], 0.0))
                link(G.affine_select(out=below[:], in_=below[:], compare_op=ALU.not_equal, fill=1.0,
                                     base=-1, pattern=[[1, P]], channel_multiplier=-1))
                link(G.affine_select(out=corner[:], in_=corner[:], compare_op=ALU.not_equal, fill=1.0,
                                     base=P - 1, pattern=[[P, P]], channel_multiplier=-1))
                link(G.iota(node_i[:], pattern=[[P, NB]], base=0, channel_multiplier=1))
                link(G.tensor_copy(node_f[:], node_i[:]))
                link(G.iota(qbase[:].rearrange("q (h j) -> q h j", h=HALVES), pattern=[[0, HALVES], [1, QT]],
                            base=0, channel_multiplier=EB))

            @block.sync
            def _(sp):
                sp.wait_ge(s_pad, 1)
                for part, a in edge_rows(ins["dst"]):
                    sp.dma_start(part(dst_i), a).then_inc(s_dst, 16)
                sp.wait_ge(s_pad, 4)
                last = ins["dst"][0:(2 * QH - 1) * EB].rearrange("(q e) -> q e", e=EB)
                with nc.allow_non_contiguous_dma(reason="one index per batch"):
                    sp.dma_start(prev_i[1:QH, 0:1], last[0:QH - 1, EB - 1:EB]).then_inc(s_dst, 16)
                    sp.dma_start(prev_i[0:QH, 1:2], last[QH - 1:2 * QH - 1, EB - 1:EB]).then_inc(s_dst, 16)
                    sp.dma_start(next_i[0:QH, 0:1], last[1:QH + 1, 0:1]).then_inc(s_dst, 16)
                    sp.dma_start(next_i[0:QH - 2, 1:2], last[QH + 1:2 * QH - 1, 0:1]).then_inc(s_dst, 16)
                    sp.dma_start(next_i[QH - 2:QH - 1, 1:2], ins["dst"][(2 * QH - 1) * EB:(2 * QH - 1) * EB + 1][None, :]).then_inc(s_dst, 16)
                sp.wait_ge(s_pad, 5)
                for part, a in edge_rows(ins["edge_weight"]):
                    sp.dma_start(part(ew_f), a).then_inc(s_ew, 16)
                sp.wait_ge(s_dstwin, 1)
                def windows_out(src, col):
                    for h in range(HALVES):
                        rows = windows[h * QH * QT:(h + 1) * QH * QT, :].rearrange("(q j) c -> q j c", j=QT)
                        rows1 = windows[h * QH * QT + 1:(h + 1) * QH * QT + 1, :].rearrange("(q j) c -> q j c", j=QT)
                        v = src[:, h, :].rearrange("q (j e) -> q j e", e=P)
                        sp.dma_start(rows[:, :, col + 1:col + P], v[:, :, 0:P - 1]).then_inc(s_win, 16)
                        sp.dma_start(rows1[:, :, col:col + 1], v[:, :, P - 1:P]).then_inc(s_win, 16)
                with nc.allow_non_contiguous_dma(reason="a column of the windows"):
                    windows_out(dst_f, 0)
                    sp.dma_start(windows[0:1, 0:1], far[0:1, 0:1]).then_inc(s_win, 16)
                    sp.dma_start(windows[0:1, P:P + 1], far[0:1, P:P + 1]).then_inc(s_win, 16)
                    sp.dma_start(windows[NT:NT + 1, 1:P], far[0:1, 1:P]).then_inc(s_win, 16)
                    sp.dma_start(windows[NT:NT + 1, P + 1:2 * P], far[0:1, P + 1:2 * P]).then_inc(s_win, 16)
                    sp.wait_ge(s_prewin, 1)
                    windows_out(running_w, P)
                sp.wait_ge(s_win, 16 * 12)

            @block.scalar
            def _(act):
                act.wait_ge(s_pad, 2)
                act.dma_start(X[:, 0:NB - 1, :], ins["x"][0:(NB - 1) * P, :].rearrange("(h l) d -> l h d", l=P)).then_inc(s_rest, 16)
                act.dma_start(X[0:N_NODES - (NB - 1) * P, NB - 1, :], ins["x"][(NB - 1) * P:N_NODES, :]).then_inc(s_rest, 16)
                act.wait_ge(s_pad, 7)
                for t, name in ((src_i, "src"), (typ_i, "edge_type_9")):
                    for part, a in edge_rows(ins[name]):
                        act.dma_start(part(t), a).then_inc(s_rest, 16)
                for a, b in loads(w2_raw):
                    act.dma_start(a, b).then_inc(s_wts, 16)
                act.wait_ge(s_rest, 16 * 8)
                act.wait_ge(s_wts, 16 * len(loads(w2_raw)))
                nc.scalar.copy(src_f[:], src_i[:])
                nc.scalar.copy(typ_f[:], typ_i[:])

            @block.tensor
            def _(pe):
                pe.wait_ge(s_hot, 1)
                for t in range(2 * QT):
                    last = nc.tensor.matmul(hist[:], lo_hot[:, t, :], hi_hot[:, t, :], start=t == 0, stop=t == 2 * QT - 1)
                last.then_inc(s_tiles, 1)
                pe.wait_ge(s_const, CONSTANTS)
                pe.wait_ge(s_rowq, 1)
                for n, v in enumerate((last_q, chain_q)):
                    for h in range(HALVES):
                        last = nc.tensor.matmul(psq[0:1, n * NQ + h * QH:n * NQ + (h + 1) * QH], v[:, h:h + 1], ident[0:QH, 0:QH],
                                                start=True, stop=True)
                last.then_inc(s_colq, 1)
                pe.wait_ge(s_scan, 1)
                for h in range(HALVES):
                    last = nc.tensor.matmul(psc[:, h:h + 1], run_row[0:1, h * QH:(h + 1) * QH], ones[0:1, 0:1], start=True, stop=True)
                last.then_inc(s_colq, 1)
                pe.wait_ge(s_cum, 1)
                nc.tensor.matmul(incl[:], upper[:], tiles_at[:], start=True, stop=True)
                nc.tensor.matmul(totals[:], ones[:], tiles_at[:], start=True, stop=True).then_inc(s_tiles, 1)
                pe.wait_ge(s_wts, 16 * len(loads(w2_raw)))
                pe.wait_ge(s_sgn, 1)
                nc.tensor.transpose(psw[:, 0, :], w2_raw[:, 0, :], ident[0:D, 0:D])
                nc.tensor.transpose(psw[:, 1, :], w2_raw[:, 1, :], ident[0:D, 0:D])
                nc.tensor.matmul(psw[:, 2, :], ones[0:1, 0:D], sgn[:], start=True, stop=True).then_inc(s_wraw, 1)

            @block.vector
            def _(dve):
                link = chain_of(dve, s_dve)
                V.memset(dst_i[:], PAD_NODE).then_inc(s_pad, 1)
                V.memset(X[:, NB - 1, :], 0.0).then_inc(s_pad, 1)
                V.memset(prev_i[:], -1).then_inc(s_pad, 1)
                V.memset(next_i[:], PAD_NODE).then_inc(s_pad, 1)
                V.memset(ew_f[:], 0.0).then_inc(s_pad, 1)
                for t in zeroed_weights:
                    link(V.memset(t, 0.0))
                for t in unit_rows:
                    link(V.memset(t, 1.0))
                V.memset(src_i[:], PAD_NODE).then_inc(s_pad, 1)
                V.memset(typ_i[:], 0).then_inc(s_pad, 1)
                V.memset(src_idx[:, NT:], PAD_NODE).then_inc(s_pad, 1)
                link(V.memset(far[0:1, 1:P], 99999.0))
                link(V.memset(far[0:1, P:2 * P], 0.0))
                link(V.memset(far[0:1, 0:1], -1.0))
                dve.wait_ge(s_dst, 16 * 8)
                link(V.tensor_copy(next_f[:], next_i[:]))
                link(V.tensor_copy(prev_f[:], prev_i[:]))
                V.tensor_copy(dst_f[:], dst_i[:]).then_inc(s_dstwin, 1)
                dve.wait_ge(s_dstwin, 1)
                ends = dst_i[:].rearrange("q h (j e) -> q (h j) e", e=P)[:, :, P - 1]
                link(V.tensor_single_scalar(bits[:], ends, 7, ALU.logical_shift_right))
                link(V.tensor_copy(tile_hi[:], bits[:]))
                link(V.tensor_single_scalar(bits[:], ends, P - 1, ALU.bitwise_and))
                link(V.tensor_copy(tile_lo[:], bits[:]))
                dve.wait_ge(s_const, 2)
                link(TT(lo_hot[:], iota_row[0:QH, None, :].to_broadcast([QH, 2 * QT, P]),
                        tile_lo[:, :, None].to_broadcast([QH, 2 * QT, P]), ALU.is_equal))
                TT(hi_hot[:], iota_row[0:QH, None, 0:NB].to_broadcast([QH, 2 * QT, NB]),
                   tile_hi[:, :, None].to_broadcast([QH, 2 * QT, NB]), ALU.is_equal).then_inc(s_hot, 1)
                dve.wait_ge(s_hot, 1)
                link(V.memset(same[:, :, 0:1], 0.0))
                link(TT(same[:, :, 1:EB], dst_f[:, :, 1:EB], dst_f[:, :, 0:EB - 1], ALU.is_equal))
                dve.wait_ge(s_ew, 48)
                link(V.tensor_tensor_scan(running_w[:].rearrange("q h e -> q (h e)"), same[:].rearrange("q h e -> q (h e)"),
                                          ew_f[:].rearrange("q h e -> q (h e)"), 0.0, ALU.mult, ALU.add))
                link(TT(link_q[:], dst_f[:, :, 0], prev_f[:], ALU.is_equal))
                link(TT(chain_q[:], dst_f[:, :, 0], dst_f[:, :, EB - 1], ALU.is_equal))
                link(TT(chain_q[:], chain_q[:], link_q[:], ALU.mult))
                V.tensor_copy(last_q[:], running_w[:, :, EB - 1]).then_inc(s_rowq, 1)
                dve.wait_ge(s_colq, 1)
                link(V.tensor_copy(row_q[:], psq[:]))
                link(V.memset(run_row[:, 0:1], 0.0))
                V.tensor_tensor_scan(run_row[:, 1:1 + NQ], row_q[:, NQ:2 * NQ], row_q[:, 0:NQ], 0.0, ALU.mult, ALU.add).then_inc(s_scan, 1)
                for h in range(HALVES):
                    link(V.tensor_scalar(head[:, h, :], dst_f[:, h, :], dst_f[:, h, 0:1], None, ALU.is_equal))
                dve.wait_ge(s_tiles, 1)
                V.tensor_copy(tiles_at[:], hist[:]).then_inc(s_cum, 1)
                dve.wait_ge(s_colq, 2)
                link(TT(carry_in[:], psc[:], link_q[:], ALU.mult))
                for h in range(HALVES):
                    link(V.scalar_tensor_tensor(running_w[:, h, :], head[:, h, :], carry_in[:, h:h + 1], running_w[:, h, :],
                                                ALU.mult, ALU.add))
                link(TT(same[:, :, 0:EB - 1], dst_f[:, :, 1:EB], dst_f[:, :, 0:EB - 1], ALU.not_equal))
                link(TT(same[:, :, EB - 1], dst_f[:, :, EB - 1], next_f[:], ALU.not_equal))
                TT(running_w[:], running_w[:], same[:], ALU.mult).then_inc(s_prewin, 1)
                dve.wait_ge(s_tiles, 2)
                link(V.tensor_copy(all_q[:], totals[:]))
                link(V.memset(run_q[:], 1.0))
                link(V.tensor_tensor_scan(tau[:], run_q[:], all_q[:], 0.0, ALU.mult, ALU.add))
                link(TT(tau[:], tau[:], all_q[:], ALU.subtract))
                link(TT(tau[:], tau[:], incl[:], ALU.add))
                link(V.tensor_copy(tau_i[:], tau[:]))
                dve.wait_ge(s_wts, 16 * len(loads(w2_raw)))
                link(V.tensor_scalar(sgn[:], gamma[:], 0.0, 2.0, ALU.is_ge, ALU.mult))
                V.tensor_scalar_add(sgn[:], sgn[:], -1.0).then_inc(s_sgn, 1)
                dve.wait_ge(s_sgn, 1)
                dve.wait_ge(s_wraw, 1)
                link(TT(bias_sgn[:], bn_b[:], sgn[:], ALU.mult))
                link(V.tensor_copy(w_qp[:, D:2 * D], psw[:, 2, :]))
                link(TT(w_qp[:, 0:D], w_qp[:, D:2 * D], psw[:, 1, :], ALU.mult))
                link(TT(w_qp[:, D:2 * D], w_qp[:, D:2 * D], psw[:, 0, :], ALU.mult))
                link(TT(w_qp[:, D:2 * D], w_qp[:, D:2 * D], w_qp[:, 0:D], ALU.subtract))
                dve.wait_ge(s_const, CONSTANTS)
                link(TT(w_first[0:D, 16:16 + D], w_first[0:D, 16:16 + D], ident[0:D, 0:D], ALU.add))
        inner.close()

        c = ExitStack()
        same = sb(c, "same", [QH, 2 * QT, P])
        rev = sb(c, "rev", [QH, 2 * QT, P])
        eval_rev = sb(c, "eval_rev", [QH, P])
        end_rev = sb(c, "end_rev", [QH, 2 * QT * P])
        is_first = sb(c, "is_first", [QH, 2 * QT, P])
        dst_t = sb(c, "dst_t", [P, NT])
        first_t = sb(c, "first_t", [P, NT])
        end_rev_t = dst_t
        diag = is_first[:].rearrange("q t e -> q (t e)")[:, 0:2 * QT * QH].rearrange("q (t m) -> q t m", m=QH)
        carry_q = sb(c, "carry_q", [QH, 2 * QT])
        tmp_q = sb(c, "tmp_q", [QH, 2 * QT])
        qbase_f = sb(c, "qbase_f", [QH, 2 * QT])
        widx = sb(c, "widx", [P, 2, GROUP], i32)
        window = sb(c, "window", [P, 2, GROUP, 2 * P])
        cmp = sb(c, "cmp", [P, GROUP, P])
        upto = sb(c, "upto", [P, NB])
        deg = sb(c, "deg", [P, NB])
        xs = sb(c, "xs", [P, 2, GROUP, D])
        ps = pb(c, "ps", [P, 4, 512])
        pt = pb(c, "xw_pt", [D, 8 * P])
        po = pb(c, "xw_po", [P, 8, P])
        t_pe = sem(c, "t_pe")
        t_ev = sem(c, "t_ev")
        t_seg = sem(c, "t_seg")
        t_first = sem(c, "t_first")
        t_diag = sem(c, "t_diag")
        t_dve = sem(c, "t_dve")
        w_idx = sem(c, "w_idx")
        w_got = [sem(c, f"w_got{k}") for k in range(2)]
        w_taken = sem(c, "w_taken")
        w_chain = sem(c, "w_chain")
        x_in = sem(c, "x_in")
        x_turned = sem(c, "x_turned")
        x_evicted = sem(c, "x_evicted")
        x_done = sem(c, "x_done")
        x_out = sem(c, "x_out")
        HJ = [(h, j0) for h in range(HALVES) for j0 in (0, 4)]

        def view4(ap3, h, j0):
            return ap3[:, h, j0:j0 + 4, :]

        with nc.Block() as block:
            @block.tensor
            def _(pe):
                g = 0

                def group(fill):
                    nonlocal g
                    if g >= 4:
                        pe.wait_ge(t_ev, g - 3)
                    for j in range(4):
                        last = fill(j, g % 4)
                    last.then_inc(t_pe, 1)
                    g += 1

                def tr(src):
                    for h, j0 in HJ:
                        group(lambda j, b: nc.tensor.transpose(
                            ps[:, b, j * QH:(j + 1) * QH], src(h, j0 + j), ident[0:QH, 0:QH]))
                tr(lambda h, j: dst_f[:, h, j * P:(j + 1) * P])
                pe.wait_ge(t_ev, 4)
                for h, j0 in HJ:
                    group(lambda j, b: nc.tensor.matmul(
                        ps[0:QH, b, j * P:(j + 1) * P], per_half(dst_t[:])[:, h, j0 + j, :], anti[:],
                        start=True, stop=True))
                for a in (src_f, typ_f, ew_f):
                    tr(lambda h, j, a=a: a[:, h, j * P:(j + 1) * P])
                pe.wait_ge(t_first, 1)
                tr(lambda h, j: is_first[:, h * QT + j, :])
                pe.wait_ge(t_seg, 1)
                tr(lambda h, j: end_rev[:, (h * QT + j) * P:(h * QT + j + 1) * P])
                pe.wait_ge(t_ev, 28)
                for k in range(4):
                    pe.wait_ge(t_ev, g - 3)
                    nc.tensor.matmul(ps[:, g % 4, 0:NT // 4], anti[:], end_rev_t[:, k * (NT // 4):(k + 1) * (NT // 4)],
                                     start=True, stop=True).then_inc(t_pe, 1)
                    g += 1
                pe.wait_ge(t_diag, 1)
                for h, j0 in HJ:
                    group(lambda j, b: nc.tensor.matmul(
                        ps[:, b, j * QH:(j + 1) * QH], ones[0:QH, :], diag[:, h * QT + j0 + j, :],
                        start=True, stop=True))

                def turn(g, i, k, first):
                    pe.wait_ge(x_in, g + 1)
                    if not first:
                        pe.wait_ge(x_evicted, g)
                    settled(pe)
                    for b in range(GROUP):
                        last = nc.tensor.transpose(pt[:, b * P:(b + 1) * P], xs[:, k, b, :], ident[:])
                    last.then_inc(x_turned, 1)
                    pe.wait_ge(x_evicted, g + 1)
                    if not first:
                        pe.wait_ge(x_out, g)
                    for b in range(GROUP):
                        last = nc.tensor.matmul(po[:, b, 0:16 + D], lhs65[:, k, b * P:(b + 1) * P], w_first[:], start=True, stop=True)
                    last.then_inc(x_done, 1)
                skewed(pe, [(0, turn)], first_at=1)

            @block.scalar
            def _(act):
                g = 0

                def evict(out_ap, n, parts=P):
                    nonlocal g
                    act.wait_ge(t_pe, g + 1)
                    v = ps[0:parts, g % 4, 0:4 * n].rearrange("p (j q) -> p j q", j=4)
                    nc.scalar.copy(out_ap, v).then_inc(t_ev, 1)
                    g += 1
                for h, j0 in HJ:
                    evict(view4(per_half(dst_t[:]), h, j0), QH)
                for h, j0 in HJ:
                    evict(rev[:, h * QT + j0:h * QT + j0 + 4, :], P, QH)
                for a in (src_idx[:, 0:NT], etype[:], weight[:], first_t[:], end_rev_t[:]):
                    for h, j0 in HJ:
                        evict(view4(per_half(a), h, j0), QH)
                for k in range(4):
                    evict(seg_end[:, k * (NT // 4):(k + 1) * (NT // 4)].rearrange("p (j q) -> p j q", j=4), NT // 16)
                for h, j0 in HJ:
                    evict(view4(per_half(carry_on[:]), h, j0), QH)

                def step(g, i, k, first):
                    if not first:
                        act.wait_ge(x_turned, g - 1)
                    nc.scalar.copy(xs[:, k, :, :], X[:, bass.ds(g * GROUP, GROUP), :]).then_inc(x_in, 1)
                    act.wait_ge(x_turned, g + 1)
                    if not first:
                        act.wait_ge(x_done, g - 1)
                    nc.scalar.copy(lhs65[0:D, k, :], pt[:, 0:GROUP * P]).then_inc(x_evicted, 1)
                    act.wait_ge(x_done, g + 1)
                    nc.scalar.copy(h16[:, bass.ds(g * GROUP, GROUP), :], po[:, 0:GROUP, 0:16])
                    nc.scalar.copy(X[:, bass.ds(g * GROUP, GROUP), :], po[:, 0:GROUP, 16:16 + D]).then_inc(x_out, 1)
                skewed(act, [(0, step)])

            @block.gpsimd
            def _(pool):
                def step(g, i, k, first):
                    if not first:
                        pool.wait_ge(w_taken, g - 1)
                    nc.gpsimd.tensor_copy(widx[:, k, :], tau_i[:, bass.ds(g * GROUP, GROUP)]).then_inc(w_idx, 1)
                    pool.wait_ge(w_idx, g + 1)
                    settled(pool)
                    for u in range(GROUP):
                        nc.gpsimd.indirect_dma_start(window[:, k, u, :], None, windows,
                                                     bass.IndirectOffsetOnAxis(widx[:, k, u:u + 1], 0)).then_inc(w_got[k], 16)
                skewed(pool, [(0, step)])

            @block.vector
            def _(dve):
                link = chain_of(dve, t_dve)
                dstv = dst_f[:].rearrange("q h (j e) -> q (h j) e", e=P)
                link(TT(same[:, :, 1:P], dstv[:, :, 1:P], dstv[:, :, 0:P - 1], ALU.is_equal))
                link(V.memset(is_first[:, :, 0:1], 1.0))
                V.tensor_scalar(is_first[:, :, 1:P], same[:, :, 1:P], -1.0, 1.0, ALU.mult, ALU.add).then_inc(t_first, 1)
                lv = linked[0:QH, :].rearrange("q (h j) -> q h j", h=HALVES)
                df = dst_f[:].rearrange("q h (j e) -> q h j e", e=P)
                link(TT(lv[:, :, 1:QT], df[:, :, 1:QT, 0], df[:, :, 0:QT - 1, P - 1], ALU.is_equal))
                link(TT(lv[:, :, 0], df[:, :, 0, 0], prev_f[:], ALU.is_equal))
                link(V.tensor_copy(first_dst[0:QH, :].rearrange("q (h j) -> q h j", h=HALVES), df[:, :, :, 0]))
                link(V.tensor_scalar(eval_rev[:], iota_row[0:QH, :], -1.0, float(P - 1), ALU.mult, ALU.add))
                dve.wait_ge(t_first, 1)
                dve.wait_ge(t_ev, 8)
                link(V.memset(same[:, :, 0:1], 0.0))
                link(TT(same[:, :, 1:P], rev[:, :, 1:P], rev[:, :, 0:P - 1], ALU.is_equal))
                link(V.tensor_scalar(rev[:], same[:], -1.0, 1.0, ALU.mult, ALU.add))
                link(TT(rev[:], rev[:], eval_rev[:, None, :].to_broadcast([QH, 2 * QT, P]), ALU.mult))
                V.tensor_tensor_scan(end_rev[:], same[:].rearrange("q t e -> q (t e)"),
                                     rev[:].rearrange("q t e -> q (t e)"), 0.0, ALU.mult, ALU.add).then_inc(t_seg, 1)
                dve.wait_ge(t_seg, 1)
                ev = end_rev[:].rearrange("q (t e) -> q t e", e=P)[:, :, P - 1]
                link(V.tensor_single_scalar(tmp_q[:], ev, float(P - 1), ALU.is_equal))
                link(TT(carry_q[:], tmp_q[:], linked[0:QH, :], ALU.mult))
                dve.wait_ge(t_ev, 24)
                link(TT(diag, ident[0:QH, None, 0:QH].to_broadcast([QH, 2 * QT, QH]),
                        carry_q[:, :, None].to_broadcast([QH, 2 * QT, QH]), ALU.mult))
                V.tensor_copy(qbase_f[:], qbase[:]).then_inc(t_diag, 1)
                dve.wait_ge(t_diag, 1)
                link(V.tensor_scalar_add(qbase_f[:, QT:], qbase_f[:, QT:], float(QH * EB)))
                link(V.scalar_tensor_tensor(qbase_f[:], ev, float(QT), qbase_f[:], ALU.mult, ALU.add))
                link(V.tensor_copy(fix_row[0:QH, :], qbase_f[:]))
                dve.wait_ge(t_ev, 32)
                link(V.tensor_scalar_add(seg_end_first[:], seg_end[:], 1.0))
                link(TT(seg_end_first[:], seg_end_first[:], first_t[:], ALU.mult))
                link(V.tensor_scalar_add(seg_end_first[:], seg_end_first[:], -1.0))

                def step(g, i, k, first):
                    dve.wait_ge(w_got[k], (i + 1) * (16 * GROUP))
                    nodes = node_f[:, bass.ds(g * GROUP, GROUP)][:, :, None].to_broadcast([P, GROUP, P])
                    TT(cmp[:], window[:, k, :, 0:P], nodes, ALU.is_equal).then_inc(w_chain, 1)
                    dve.wait_ge(w_chain, g * 3 + 1)
                    TT(window[:, k, :, P:2 * P], cmp[:], window[:, k, :, P:2 * P], ALU.mult).then_inc(w_chain, 1)
                    TT(window[:, k, :, 0:P], window[:, k, :, 0:P], nodes, ALU.is_le).then_inc(w_chain, 1)
                    dve.wait_ge(w_chain, g * 3 + 3)
                    V.reduce_sum(upto[:, bass.ds(g * GROUP, GROUP)], window[:, k, :, 0:P], AX.X)
                    V.reduce_sum(deg[:, bass.ds(g * GROUP, GROUP)], window[:, k, :, P:2 * P], AX.X).then_inc(w_taken, 1)
                    dve.wait_ge(w_taken, g + 1)
                skewed(dve, [(0, step)])

        shifted = po[:, 0, 0:NB]
        end_buf = sb(c, "end_buf", [P, 1 + NB])
        end_f = end_buf[:, 1:1 + NB]
        tmp = sb(c, "tmp", [P, NB])
        tmp2 = sb(c, "tmp2", [P, NB])
        pos = sb(c, "pos", [P, NB])
        ti = sb(c, "ti", [P, NB], i32)
        tj = sb(c, "tj", [P, NB], i32)
        tk = sb(c, "tk", [P, NB], i32)
        d_ch = sem(c, "d_ch")
        d_end = sem(c, "d_end")
        d_pe = sem(c, "d_pe")
        d_deg = sem(c, "d_deg")
        d_sqrt = sem(c, "d_sqrt")
        d_h = sem(c, "d_h")
        d_out = sem(c, "d_out")
        with nc.Block() as block:
            @block.tensor
            def _(pe):
                pe.wait_ge(d_end, 1)
                nc.tensor.matmul(shifted, below[:], end_f, start=True, stop=False)
                nc.tensor.matmul(shifted, corner[:], end_buf[:, 0:NB], start=False, stop=True).then_inc(d_pe, 1)

            @block.scalar
            def _(act):
                act.wait_ge(d_deg, 1)
                nc.scalar.sqrt(tmp2[:], tmp[:]).then_inc(d_sqrt, 1)

            @block.sync
            def _(sp):
                sp.wait_ge(d_h, 1)
                sp.dma_start(table16.rearrange("(h l) d -> l h d", l=P), h16[:]).then_inc(d_out, 16)
                sp.wait_ge(d_out, 16)

            @block.vector
            def _(dve):
                link = chain_of(dve, d_ch)
                link(V.tensor_scalar_add(dinv[:], deg[:], 1.0))
                link(V.tensor_single_scalar(pos[:], dinv[:], 0.0, ALU.is_gt))
                V.tensor_scalar_max(tmp[:], dinv[:], 1e-30).then_inc(d_deg, 1)
                link(V.memset(end_buf[:, 0:1], 0.0))
                link(V.scalar_tensor_tensor(end_f, tau[:], float(P), upto[:], ALU.mult, ALU.add))
                V.tensor_scalar_add(end_f, end_f, -1.0).then_inc(d_end, 1)
                dve.wait_ge(d_end, 1)
                dve.wait_ge(d_sqrt, 1)
                link(V.reciprocal(dinv[:], tmp2[:]))
                link(TT(dinv[:], dinv[:], pos[:], ALU.mult))
                TT(h16[:], h16[:], dinv[:, :, None].to_broadcast([P, NB, 16]), ALU.mult).then_inc(d_h, 1)
                dve.wait_ge(d_pe, 1)
                link(TT(count[:], end_f, shifted, ALU.subtract))
                link(V.tensor_single_scalar(nonempty[:], count[:], 0.0, ALU.is_gt))
                link(V.tensor_single_scalar(several[:], count[:], 1.0, ALU.is_gt))
                dve.wait_ge(d_h, 1)

                def to_row(edge_f, row):
                    link(V.tensor_copy(ti[:], edge_f))
                    link(V.tensor_scalar(tj[:], ti[:], 10, 10, ALU.logical_shift_right, ALU.logical_shift_left))
                    link(V.tensor_scalar(tk[:], ti[:], P - 1, 3, ALU.bitwise_and, ALU.logical_shift_left))
                    link(TT(tj[:], tj[:], tk[:], ALU.bitwise_or))
                    link(V.tensor_scalar(tk[:], ti[:], 7, QT - 1, ALU.logical_shift_right, ALU.bitwise_and))
                    link(TT(row, tj[:], tk[:], ALU.bitwise_or))
                link(V.tensor_scalar(tmp[:], end_f, -1.0, 0.0, ALU.add, ALU.max))
                to_row(tmp[:], end_row[:])
                link(V.tensor_scalar_min(tmp[:], shifted[:], float(EPAD - 1)))
                to_row(tmp[:], start_row[:])
                link(V.tensor_copy(tmp[:], start_row[:]))
                link(V.tensor_scalar_add(tmp2[:], node_f[:], float(EPAD)))
                link(TT(tmp[:], tmp[:], tmp2[:], ALU.subtract))
                link(TT(tmp[:], tmp[:], nonempty[:], ALU.mult))
                link(TT(tmp[:], tmp[:], tmp2[:], ALU.add))
                link(V.tensor_copy(start_row[:], tmp[:]))
        c.close()
        edges_ctx.close()

        def rows_of(dram_ap):
            return dram_ap.rearrange("(h l) d -> l h d", l=P)

        def batches_of(dram_ap):
            return dram_ap.rearrange("(b e j) w -> b e (j w)", e=P, j=QT)

        def edge_pass(tag, table, gathered, width, weighted=False, with_types=False, squares=False,
                      histogram=None, zero_fill=None):
            with ExitStack() as c:
                idx = sb(c, tag + "idx", [P, SLOTS, QT], i32)
                segment_matrix = sb(c, tag + "seg", [P, SLOTS, QT, P])
                msg = sb(c, tag + "msg", [P, SLOTS, QT, width])
                summed = sb(c, tag + "sum", [P, SLOTS, QT * width])
                banks = -(-QT * width // 512)
                acc = [pb(c, tag + f"acc{k}", [P, QT * width]) for k in range(2)]
                types_too = with_types
                gathered_rows = [sem(c, tag + f"gathered{k}") for k in range(SLOTS)]
                stored = [sem(c, tag + f"stored{k}") for k in range(SLOTS)]
                idx_ready = sem(c, tag + "idx_ready")
                matrix_ready = sem(c, tag + "matrix_ready")
                msg_ready = sem(c, tag + "msg_ready")
                product_done = sem(c, tag + "product_done")
                evicted = sem(c, tag + "evicted")
                hot_ready = sem(c, tag + "hot_ready")
                hot_used = sem(c, tag + "hot_used")
                zero_set = sem(c, tag + "zero_set")
                zeroed = sem(c, tag + "zeroed")
                out_b = batches_of(prefix[width])
                iters = NQ // SLOTS
                if histogram is not None:
                    key_lo, key_hi, iota_key = histogram["lo"], histogram["hi"], histogram["iota"]
                    hot_lo = sb(c, tag + "hot_lo", [P, 2, QT, P], bf16)
                    hot_hi = sb(c, tag + "hot_hi", [P, 2, QT, NB * R], bf16)
                    hacc = [pb(c, tag + f"hacc{k}", [P, NB * R // 2]) for k in range(2)]
                if zero_fill is not None:
                    zeros = sb(c, tag + "zeros", [P, QT * D])
                with nc.Block() as block:
                    @block.gpsimd
                    def _(pool):
                        def step(i, first):
                            for k in range(SLOTS):
                                pool.wait_ge(idx_ready, i * SLOTS + k + 1)
                                if not first:
                                    pool.wait_ge(product_done, (i - 1) * SLOTS + k + 1)
                                settled(pool)
                                for u in range(QT):
                                    nc.gpsimd.indirect_dma_start(
                                        msg[:, k, u, 0:gathered], None, table,
                                        bass.IndirectOffsetOnAxis(idx[:, k, u:u + 1], 0)).then_inc(gathered_rows[k], 16)
                        step(0, True)
                        with pool.Fori(1, iters) as i:
                            step(i, False)

                    @block.scalar
                    def _(act):
                        for k in range(2):
                            nc.scalar.copy(idx[:, k, :], src_idx[:, k * QT:(k + 1) * QT]).then_inc(idx_ready, 1)

                        def step(i, first):
                            for k in range(SLOTS):
                                ahead = (k + 2) % SLOTS
                                if not (first and k < 2):
                                    act.wait_ge(gathered_rows[ahead], ((i if k < 2 else i + 1)) * (16 * QT))
                                nc.scalar.copy(idx[:, ahead, :], src_idx[:, bass.ds((i * SLOTS + k + 2) * QT, QT)]).then_inc(idx_ready, 1)
                                if squares:
                                    act.wait_ge(gathered_rows[k], (i + 1) * (16 * QT))
                                    nc.scalar.square(msg[:, k, :, gathered:2 * gathered], msg[:, k, :, 0:gathered]).then_inc(msg_ready, 1)
                                act.wait_ge(product_done, i * SLOTS + k + 1)
                                if not first:
                                    act.wait_ge(stored[k], i * 16)
                                for a in range(0, QT * width, 512):
                                    z = min(a + 512, QT * width)
                                    last = nc.scalar.copy(summed[:, k, a:z], acc[k % 2][:, a:z])
                                last.then_inc(evicted, 1)
                        step(0, True)
                        with act.Fori(1, iters) as i:
                            step(i, False)

                    @block.sync
                    def _(sp):
                        if zero_fill is not None:
                            sp.wait_ge(zero_set, 1)
                        with sp.Fori(0, iters) as i:
                            for k in range(SLOTS):
                                sp.wait_ge(evicted, i * SLOTS + k + 1)
                                sp.dma_start(out_b[i * SLOTS + k], summed[:, k, :]).then_inc(stored[k], 16)
                                if zero_fill is not None:
                                    sp.dma_start(zero_fill[i * SLOTS + k], zeros[:]).then_inc(zeroed, 16)
                        for k in range(SLOTS):
                            sp.wait_ge(stored[k], iters * 16)
                        if zero_fill is not None:
                            sp.wait_ge(zeroed, NQ * 16)

                    @block.vector
                    def _(dve):
                        if zero_fill is not None:
                            nc.vector.memset(zeros[:], 0.0).then_inc(zero_set, 1)

                        def step(i, first):
                            for k in range(SLOTS):
                                if not first:
                                    dve.wait_ge(product_done, (i - 1) * SLOTS + k + 1)
                                for u in range(QT):
                                    t = i * (SLOTS * QT) + k * QT + u
                                    end = seg_end[:, bass.ds(t, 1)]
                                    if weighted:
                                        last = nc.vector.tensor_scalar(segment_matrix[:, k, u, :], iota_upper[:], end,
                                                                       weight[:, bass.ds(t, 1)], ALU.is_le, ALU.mult)
                                    else:
                                        last = nc.vector.tensor_scalar(segment_matrix[:, k, u, :], iota_upper[:], end,
                                                                       None, ALU.is_le)
                                last.then_inc(matrix_ready, 1)
                                if types_too:
                                    t0 = i * (SLOTS * QT) + k * QT
                                    nc.vector.tensor_tensor(
                                        msg[:, k, :, gathered:gathered + R],
                                        iota_row[:, None, 0:R].to_broadcast([P, QT, R]),
                                        etype[:, bass.ds(t0, QT)][:, :, None].to_broadcast([P, QT, R]), ALU.is_equal)
                                    dve.wait_ge(gathered_rows[k], (i + 1) * (16 * QT))
                                    nc.vector.tensor_tensor(
                                        msg[:, k, :, 0:gathered], msg[:, k, :, 0:gathered],
                                        weight[:, bass.ds(t0, QT)][:, :, None].to_broadcast([P, QT, gathered]),
                                        ALU.mult).then_inc(msg_ready, 1)
                                if histogram is not None:
                                    s = k % 2
                                    if not (first and k < 2):
                                        dve.wait_ge(hot_used, i * SLOTS + k - 1)
                                    for u in range(QT):
                                        t = i * (SLOTS * QT) + k * QT + u
                                        nc.vector.tensor_scalar(hot_lo[:, s, u, :], iota_key[:, 0:P], key_lo[:, bass.ds(t, 1)], None, ALU.is_equal)
                                        last = nc.vector.tensor_scalar(hot_hi[:, s, u, :], iota_key[:], key_hi[:, bass.ds(t, 1)], None, ALU.is_equal)
                                    last.then_inc(hot_ready, 1)
                        step(0, True)
                        with dve.Fori(1, iters) as i:
                            step(i, False)

                    @block.tensor
                    def _(pe):
                        def step(i, first, final):
                            for k in range(SLOTS):
                                if histogram is not None:
                                    s = k % 2
                                    pe.wait_ge(hot_ready, i * SLOTS + k + 1)
                                    half = NB * R // 2
                                    for u in range(QT):
                                        for a in range(2):
                                            last = nc.tensor.matmul(hacc[a][:], hot_lo[:, s, u, :], hot_hi[:, s, u, a * half:(a + 1) * half],
                                                                    start=first and k == 0 and u == 0,
                                                                    stop=final and k == SLOTS - 1 and u == QT - 1)
                                    last.then_inc(hot_used, 1)
                                pe.wait_ge(matrix_ready, i * SLOTS + k + 1)
                                if types_too or squares:
                                    pe.wait_ge(msg_ready, i * SLOTS + k + 1)
                                pe.wait_ge(gathered_rows[k], (i + 1) * (16 * QT))
                                if not (first and k < 2):
                                    pe.wait_ge(evicted, i * SLOTS + k - 1)
                                for u in range(QT):
                                    last = nc.tensor.matmul(acc[k % 2][:, u * width:(u + 1) * width], segment_matrix[:, k, u, :],
                                                            msg[:, k, u, :], start=True, stop=True)
                                last.then_inc(product_done, 1)
                        step(0, True, False)
                        with pe.Fori(1, iters - 1) as i:
                            step(i, False, False)
                        step(iters - 1, False, True)
                if histogram is not None:
                    done = sem(c, tag + "hist_out")
                    with nc.Block() as block:
                        @block.vector
                        def _(dve):
                            half = NB // 2
                            for a in range(2):
                                nc.vector.tensor_copy(counts[:, a * half:(a + 1) * half, 0:R],
                                                      hacc[a][:].rearrange("p (n r) -> p n r", r=R)).then_inc(done, 1)

        def carry_stage(tag, width):
            pre = prefix[width]
            with ExitStack() as c:
                tile_last = sb(c, tag + "tile_last", [QH, HALVES, QT, width])
                totals_t = sb(c, tag + "totals_t", [width, NT])
                running = sb(c, tag + "running", [width, 1 + NT])
                carried = sb(c, tag + "carried", [QH, 2 * QT, width])
                ps4 = pb(c, tag + "ps4", [P, 4, 512])
                qs4 = pb(c, tag + "qs4", [P, 4, 512])
                last_loaded = sem(c, tag + "last_loaded")
                turned = sem(c, tag + "turned")
                turned_out = sem(c, tag + "turned_out")
                scanned = sem(c, tag + "scanned")
                back = sem(c, tag + "back")
                carried_ready = sem(c, tag + "carried_ready")
                rows_back = sem(c, tag + "rows_back")
                HJ = [(h, j0) for h in range(HALVES) for j0 in (0, 4)]
                with nc.Block() as block:
                    @block.sync
                    def _(sp):
                        v = pre.rearrange("(h q e j) w -> q h e (j w)", h=HALVES, q=QH, e=P)
                        for h in range(HALVES):
                            sp.dma_start(tile_last[:, h, :, :].rearrange("q j w -> q (j w)"), v[:, h, P - 1, :]).then_inc(last_loaded, 16)

                    @block.tensor
                    def _(pe):
                        pe.wait_ge(last_loaded, 32)
                        for g, (h, j0) in enumerate(HJ):
                            for j in range(4):
                                last = nc.tensor.transpose(ps4[0:width, g, j * QH:(j + 1) * QH], tile_last[:, h, j0 + j, :],
                                                           ident[0:QH, 0:QH])
                            last.then_inc(turned, 1)
                        pe.wait_ge(scanned, 2)
                        rv = per_half(running[:, 0:NT])
                        for g, (h, j0) in enumerate(HJ):
                            for j in range(4):
                                last = nc.tensor.transpose(qs4[0:QH, g, j * width:(j + 1) * width], rv[:, h, j0 + j, :],
                                                           ident[0:width, 0:width])
                            last.then_inc(back, 1)

                    @block.scalar
                    def _(act):
                        for g, (h, j0) in enumerate(HJ):
                            act.wait_ge(turned, g + 1)
                            nc.scalar.copy(per_half(totals_t[:])[:, h, j0:j0 + 4, :],
                                           ps4[0:width, g, 0:4 * QH].rearrange("p (j q) -> p j q", j=4)).then_inc(turned_out, 1)

                    @block.vector
                    def _(dve):
                        V.memset(running[:, 0:1], 0.0).then_inc(scanned, 1)
                        dve.wait_ge(turned_out, 4)
                        V.tensor_tensor_scan(running[:, 1:1 + NT], carry_on[0:width, :], totals_t[:], 0.0,
                                             ALU.mult, ALU.add).then_inc(scanned, 1)
                        for g in range(4):
                            dve.wait_ge(back, g + 1)
                            TT(carried[:, 4 * g:4 * g + 4, :], qs4[0:QH, g, 0:4 * width].rearrange("q (j w) -> q j w", j=4),
                               linked[0:QH, 4 * g:4 * g + 4][:, :, None].to_broadcast([QH, 4, width]), ALU.mult).then_inc(carried_ready, 1)

                    @block.gpsimd
                    def _(pool):
                        for t in range(2 * QT):
                            pool.wait_ge(carried_ready, t // 4 + 1)
                            nc.gpsimd.indirect_dma_start(pre, bass.IndirectOffsetOnAxis(fix_row[0:QH, t:t + 1], 0),
                                                         carried[:, t, :], None, compute_op=ALU.add).then_inc(rows_back, 16)
                        pool.wait_ge(rows_back, 16 * 2 * QT)

        def gather_part(pool, width, idx, rows, copied, got, taken):
            def part(g, i, k, first):
                if not first:
                    pool.wait_ge(taken, g - 1)
                nc.gpsimd.tensor_copy(idx[:, k, :], end_row[:, bass.ds(g * GROUP, GROUP)]).then_inc(copied, 1)
                pool.wait_ge(copied, g + 1)
                settled(pool)
                for u in range(GROUP):
                    nc.gpsimd.indirect_dma_start(rows[:, k, u, :], None, prefix[width],
                                                 bass.IndirectOffsetOnAxis(idx[:, k, u:u + 1], 0)).then_inc(got[k], 16)
            return part

        def of_group(v, g, width=None):
            a = v[:, bass.ds(g * GROUP, GROUP)]
            return a if width is None else a[:, :, None].to_broadcast([P, GROUP, width])

        def rows_of_group(v, g):
            return v[:, bass.ds(g * GROUP, GROUP), :]

        def every_block(v, width):
            return v[:, None, :].to_broadcast([P, GROUP, width])

        class Chain:

            def __init__(self, engine, s, length):
                self.engine, self.s, self.length = engine, s, length

            def group(self, g):
                self.base, self.n = g * self.length, 0

            def __call__(self, instruction):
                self.n += 1
                assert self.n <= self.length
                instruction.then_inc(self.s, 1)
                self.engine.wait_ge(self.s, self.base + self.n)

        def elementwise(tag, steps):
            with ExitStack() as c:
                s = sem(c, tag + "step_done")
                with nc.Block() as block:
                    @block.vector
                    def _(dve):
                        for n, (e, f) in enumerate(steps):
                            if e == "v":
                                if n:
                                    dve.wait_ge(s, n)
                                f().then_inc(s, 1)

                    @block.scalar
                    def _(act):
                        for n, (e, f) in enumerate(steps):
                            if e == "a":
                                if n:
                                    act.wait_ge(s, n)
                                f().then_inc(s, 1)

        def layernorm(dve, ch, s_var, s_root, g, y, sq, m, v, root_v, dst, done):
            ch(V.reduce_sum(m, y, AX.X))
            ch(V.tensor_scalar_mul(m, m, 1.0 / D))
            ch(TT(y, y, m[:, :, None].to_broadcast([P, GROUP, D]), ALU.subtract))
            ch(TT(sq, y, y, ALU.mult))
            ch(V.reduce_sum(v, sq, AX.X))
            V.tensor_scalar(v, v, 1.0 / D, LN_EPS, ALU.mult, ALU.add).then_inc(s_var, 1)
            dve.wait_ge(s_root, g + 1)
            ch(V.reciprocal(m, root_v))
            TT(dst, y, m[:, :, None].to_broadcast([P, GROUP, D]), ALU.mult).then_inc(done, 1)

        LN_LINKS = 6

        def layernorm_root(act, s_var, s_root, g, v, root_v):
            act.wait_ge(s_var, g + 1)
            nc.scalar.sqrt(root_v, v).then_inc(s_root, 1)

        def turn_blocks(out_ps, src):
            for b in range(GROUP):
                last = nc.tensor.transpose(out_ps[:, b * P:(b + 1) * P], src[:, b, :], ident[:])
            return last

        def node_tools(c, tag, width):
            idx = sb(c, tag + "idx", [P, 2, GROUP], i32)
            rows = sb(c, tag + "rows", [P, 2, GROUP, width])
            copied = sem(c, tag + "copied")
            got = [sem(c, tag + f"got{k}") for k in range(2)]
            taken = sem(c, tag + "taken")
            return idx, rows, copied, got, taken

        edge_pass("p1", table16, 16, 25, with_types=True, zero_fill=batches_of(node_at_edge[0:EPAD, :]))
        carry_stage("c1", 25)
        with ExitStack() as c:
            idx, rows, copied, got, taken = node_tools(c, "n1", 25)
            y = sb(c, "n1y", [P, 2, GROUP, 16])
            chain = sem(c, "n1chain")
            ready = sem(c, "n1ready")
            stored = sem(c, "n1stored")
            with nc.Block() as block:
                @block.gpsimd
                def _(pool):
                    skewed(pool, [(0, gather_part(pool, 25, idx, rows, copied, got, taken))])

                @block.vector
                def _(dve):
                    ch = Chain(dve, chain, 5)

                    def part(g, i, k, first):
                        ch.group(g)
                        dve.wait_ge(got[k], (i + 1) * (16 * GROUP))
                        ya = y[:, k, :, :]
                        TT(rows_of_group(counts, g)[:, :, R:2 * R], rows[:, k, :, 16:25], of_group(nonempty, g, R), ALU.mult)
                        ch(TT(ya, rows[:, k, :, 0:16], of_group(nonempty, g, 16), ALU.mult))
                        ch(TT(ya, ya, rows_of_group(h16, g), ALU.add))
                        ch(TT(ya, ya, of_group(dinv, g, 16), ALU.mult))
                        ch(TT(ya, ya, every_block(b1row, 16), ALU.add))
                        ch(V.tensor_scalar_max(ya, ya, 0.0))
                        TT(rows_of_group(h16, g), ya, of_group(dinv, g, 16), ALU.mult).then_inc(taken, 1)
                    skewed(dve, [(0, part)])

                @block.sync
                def _(sp):
                    def part(g, i, k, first):
                        sp.wait_ge(taken, g + 1)
                        sp.dma_start(rows_of(table16b)[:, bass.ds(g * GROUP, GROUP), :], rows_of_group(h16, g)).then_inc(stored, 16)
                    skewed(sp, [(0, part)])
                    sp.wait_ge(stored, 16 * NGROUPS)
        with ExitStack() as c:
            key_lo = sb(c, "key_lo", [P, NT])
            key_hi = sb(c, "key_hi", [P, NT])
            ki = sb(c, "ki", [P, NT], i32)
            iota_ki = sb(c, "iota_ki", [P, NB * R], i32)
            iota_key = sb(c, "iota_key", [P, NB * R], f16)
            made = sem(c, "made_iota")
            with nc.Block() as block:
                @block.gpsimd
                def _(pool):
                    nc.gpsimd.iota(iota_ki[:], pattern=[[1, NB * R]], base=0, channel_multiplier=0).then_inc(made, 1)
            elementwise("keys", [
                ("v", lambda: V.tensor_copy(iota_key[:], iota_ki[:])),
                ("v", lambda: V.tensor_single_scalar(ki[:], src_idx[:, 0:NT], 7, ALU.logical_shift_right)),
                ("v", lambda: V.tensor_copy(key_hi[:], ki[:])),
                ("v", lambda: V.scalar_tensor_tensor(key_hi[:], key_hi[:], float(R), etype[:], ALU.mult, ALU.add)),
                ("v", lambda: V.tensor_single_scalar(ki[:], src_idx[:, 0:NT], P - 1, ALU.bitwise_and)),
                ("v", lambda: V.tensor_copy(key_lo[:], ki[:])),
            ])
            edge_pass("p2", table16b, 16, 16, weighted=True,
                      histogram={"lo": key_lo, "hi": key_hi, "iota": iota_key})
        carry_stage("c2", 16)
        L0 = ExitStack()
        h32 = sb(L0, "h32", [P, NB, 32])
        with ExitStack() as c:
            idx, rows, copied, got, taken = node_tools(c, "n2", 16)
            y = sb(c, "n2y", [P, 2, GROUP, 16])
            z = sb(c, "n2z", [P, 2, GROUP, 32])
            pt = pb(c, "n2pt", [16, 8 * P])
            po = pb(c, "n2po", [P, GROUP, 32])
            chain, ready, turned, evicted, product, relued, final, stored = [
                sem(c, "n2" + n) for n in ("chain", "ready", "turned", "evicted", "product", "relued", "final", "stored")]
            with nc.Block() as block:
                @block.gpsimd
                def _(pool):
                    skewed(pool, [(0, gather_part(pool, 16, idx, rows, copied, got, taken))])

                @block.vector
                def _(dve):
                    ch = Chain(dve, chain, 1)

                    def front(g, i, k, first):
                        ch.group(g)
                        dve.wait_ge(got[k], (i + 1) * (16 * GROUP))
                        if not first:
                            dve.wait_ge(turned, g - 1)
                        ya = y[:, k, :, :]
                        TT(ya, rows[:, k, :, :], of_group(nonempty, g, 16), ALU.mult).then_inc(taken, 1)
                        dve.wait_ge(taken, g + 1)
                        ch(TT(ya, ya, rows_of_group(h16, g), ALU.add))
                        TT(ya, ya, of_group(dinv, g, 16), ALU.mult).then_inc(ready, 1)

                    def back(g, i, k, first):
                        dve.wait_ge(relued, g + 1)
                        TT(rows_of_group(h32, g), z[:, k, :, :], of_group(dinv, g, 32), ALU.mult).then_inc(final, 1)
                    skewed(dve, [(0, front), (1, back)])

                @block.tensor
                def _(pe):
                    def part(g, i, k, first):
                        pe.wait_ge(ready, g + 1)
                        if not first:
                            pe.wait_ge(evicted, g)
                        settled(pe)
                        turn_blocks(pt, y[:, k, :, :]).then_inc(turned, 1)
                        pe.wait_ge(evicted, g + 1)
                        if not first:
                            pe.wait_ge(relued, g)
                        for b in range(GROUP):
                            last = nc.tensor.matmul(po[:, b, :], lhs33[:, k, b * P:(b + 1) * P], w2a[:], start=True, stop=True)
                        last.then_inc(product, 1)
                    skewed(pe, [(0, part)], first_at=1)

                @block.scalar
                def _(act):
                    def part(g, i, k, first):
                        act.wait_ge(turned, g + 1)
                        if not first:
                            act.wait_ge(product, g - 1)
                        nc.scalar.copy(lhs33[0:16, k, :], pt[:, 0:GROUP * P]).then_inc(evicted, 1)
                        act.wait_ge(product, g + 1)
                        if not first:
                            act.wait_ge(final, g - 1)
                        nc.scalar.activation(z[:, k, :, :], po[:], ACT.Relu).then_inc(relued, 1)
                    skewed(act, [(0, part)])

                @block.sync
                def _(sp):
                    def part(g, i, k, first):
                        sp.wait_ge(final, g + 1)
                        sp.dma_start(rows_of(table32)[:, bass.ds(g * GROUP, GROUP), :], rows_of_group(h32, g)).then_inc(stored, 16)
                    skewed(sp, [(0, part)])
                    sp.wait_ge(stored, 16 * NGROUPS)
        edge_pass("p3", table32, 32, 32, weighted=True)
        carry_stage("c3", 32)
        with ExitStack() as c:
            idx, rows, copied, got, taken = node_tools(c, "n3", 32)
            y = sb(c, "n3y", [P, 2, GROUP, 32])
            x4 = sb(c, "n3x4", [P, 2, GROUP, D])
            x4t = sb(c, "n3x4t", [D, 2, GROUP * P])
            r = sb(c, "n3r", [P, GROUP, D])
            sq = sb(c, "n3sq", [P, GROUP, D])
            m = sb(c, "n3m", [P, GROUP])
            v = sb(c, "n3v", [P, GROUP])
            rv = sb(c, "n3rv", [P, GROUP])
            pt = pb(c, "n3pt", [32, 8 * P])
            pt2 = pb(c, "n3pt2", [D, 8 * P])
            po = pb(c, "n3po", [P, GROUP, D])
            po2 = pb(c, "n3po2", [P, GROUP, D])
            chain, chain2, ready, turned, evicted, product, relued, turned2, evicted2, product2, summed, var, rooted, final, stored = [
                sem(c, "n3" + n) for n in ("chain", "chain2", "ready", "turned", "evicted", "product", "relued", "turned2",
                                           "evicted2", "product2", "summed", "var", "rooted", "final", "stored")]
            with nc.Block() as block:
                @block.gpsimd
                def _(pool):
                    skewed(pool, [(0, gather_part(pool, 32, idx, rows, copied, got, taken))])

                @block.vector
                def _(dve):
                    ch = Chain(dve, chain, 1)
                    ch2 = Chain(dve, chain2, LN_LINKS)

                    def front(g, i, k, first):
                        ch.group(g)
                        dve.wait_ge(got[k], (i + 1) * (16 * GROUP))
                        if not first:
                            dve.wait_ge(turned, g - 1)
                        ya = y[:, k, :, :]
                        TT(ya, rows[:, k, :, :], of_group(nonempty, g, 32), ALU.mult).then_inc(taken, 1)
                        dve.wait_ge(taken, g + 1)
                        ch(TT(ya, ya, rows_of_group(h32, g), ALU.add))
                        TT(ya, ya, of_group(dinv, g, 32), ALU.mult).then_inc(ready, 1)

                    def back(g, i, k, first):
                        dve.wait_ge(product2, g + 1)
                        TT(r[:], po2[:], rows_of_group(X, g), ALU.add).then_inc(summed, 1)
                        dve.wait_ge(summed, g + 1)
                        ch2.group(g)
                        layernorm(dve, ch2, var, rooted, g, r[:], sq[:], m[:], v[:], rv[:], rows_of_group(X, g), final)
                        dve.wait_ge(final, g + 1)
                    skewed(dve, [(0, front), (1, back)])

                @block.tensor
                def _(pe):
                    def part(g, i, k, first):
                        pe.wait_ge(ready, g + 1)
                        if not first:
                            pe.wait_ge(evicted, g)
                        settled(pe)
                        turn_blocks(pt, y[:, k, :, :]).then_inc(turned, 1)
                        pe.wait_ge(evicted, g + 1)
                        if not first:
                            pe.wait_ge(relued, g)
                        for b in range(GROUP):
                            last = nc.tensor.matmul(po[:, b, :], lhs33[:, k, b * P:(b + 1) * P], w3a[:], start=True, stop=True)
                        last.then_inc(product, 1)
                        pe.wait_ge(relued, g + 1)
                        if not first:
                            pe.wait_ge(evicted2, g)
                        settled(pe)
                        turn_blocks(pt2, x4[:, k, :, :]).then_inc(turned2, 1)
                        pe.wait_ge(evicted2, g + 1)
                        if not first:
                            pe.wait_ge(summed, g)
                        for b in range(GROUP):
                            last = nc.tensor.matmul(po2[:, b, :], x4t[:, k, b * P:(b + 1) * P], lw_low[:], start=True, stop=True)
                        last.then_inc(product2, 1)
                    skewed(pe, [(0, part)], first_at=1)

                @block.scalar
                def _(act):
                    def front(g, i, k, first):
                        act.wait_ge(turned, g + 1)
                        if not first:
                            act.wait_ge(product, g - 1)
                        nc.scalar.copy(lhs33[0:32, k, :], pt[:, 0:GROUP * P]).then_inc(evicted, 1)
                        act.wait_ge(product, g + 1)
                        if not first:
                            act.wait_ge(turned2, g - 1)
                        nc.scalar.activation(x4[:, k, :, :], po[:], ACT.Relu).then_inc(relued, 1)
                        act.wait_ge(turned2, g + 1)
                        if not first:
                            act.wait_ge(product2, g - 1)
                        nc.scalar.copy(x4t[:, k, :], pt2[:, 0:GROUP * P]).then_inc(evicted2, 1)

                    def back(g, i, k, first):
                        layernorm_root(act, var, rooted, g, v[:], rv[:])
                    skewed(act, [(0, front), (1, back)])

                @block.sync
                def _(sp):
                    def part(g, i, k, first):
                        sp.wait_ge(final, g + 1)
                        sp.dma_start(rows_of(table64)[:, bass.ds(g * GROUP, GROUP), :], rows_of_group(X, g)).then_inc(stored, 16)
                    skewed(sp, [(0, part)])
                    sp.wait_ge(stored, 16 * NGROUPS)
        L0.close()

        edge_pass("p4", table64, D, 2 * D, squares=True)
        carry_stage("c4", 2 * D)
        with ExitStack() as c:
            idx, rows, copied, got, taken = node_tools(c, "n4", 2 * D)
            inv = sb(c, "n4inv", [P, NB])
            t = sb(c, "n4t", [P, 2, GROUP, 2 * D])
            mean_sq = sb(c, "n4mean_sq", [P, GROUP, D])
            dev = sb(c, "n4dev", [P, 2, GROUP, D])
            sq = sb(c, "n4sq", [P, GROUP, D])
            m = sb(c, "n4m", [P, GROUP])
            v = sb(c, "n4v", [P, GROUP])
            rv = sb(c, "n4rv", [P, GROUP])
            xs = sb(c, "n4xs", [P, 2, GROUP, D])
            xt = sb(c, "n4xt", [D, 2, GROUP * P])
            qs = sb(c, "n4qs", [P, 2, GROUP, D])
            p_s = sb(c, "n4ps", [P, 2, GROUP, D])
            sidx = sb(c, "n4sidx", [P, 2, GROUP], i32)
            bias_b = sb(c, "n4bias", [P, D])
            heads = sb(c, "heads", [QH, HALVES, QT * D])
            pt = pb(c, "n4pt", [D, 8 * P])
            po_q = pb(c, "n4po_q", [P, 8, D])
            po_p = pb(c, "n4po_p", [P, 8, D])
            pbias = pb(c, "n4pbias", [P, D])
            chain, chain2, var0, dev_ready, var, rooted, final, turned, evicted, product, q_out, p_out, kept, copied2 = [
                sem(c, "n4" + n) for n in ("chain", "chain2", "var0", "dev_ready", "var", "rooted", "final", "turned", "evicted",
                                           "product", "q_out", "p_out", "kept", "copied2")]
            made, bias_in = sem(c, "n4made"), sem(c, "n4bias_in")
            q_stored = [sem(c, f"n4q_stored{k}") for k in range(2)]
            p_stored = [sem(c, f"n4p_stored{k}") for k in range(2)]
            scattered = [sem(c, f"n4scattered{k}") for k in range(2)]
            head_got = sem(c, "head_got")
            head_put = sem(c, "head_put")
            with nc.Block() as block:
                @block.gpsimd
                def _(pool):
                    def scatter(g, i, k, first):
                        if not first:
                            pool.wait_ge(scattered[k], i * (16 * GROUP))
                        nc.gpsimd.tensor_copy(sidx[:, k, :], start_row[:, bass.ds(g * GROUP, GROUP)]).then_inc(copied2, 1)
                        pool.wait_ge(copied2, g + 1)
                        pool.wait_ge(p_out, g + 1)
                        settled(pool)
                        for u in range(GROUP):
                            nc.gpsimd.indirect_dma_start(node_at_edge, bass.IndirectOffsetOnAxis(sidx[:, k, u:u + 1], 0),
                                                         p_s[:, k, u, :], None).then_inc(scattered[k], 16)
                    skewed(pool, [(0, gather_part(pool, 2 * D, idx, rows, copied, got, taken)), (2, scatter)])
                    for k in range(2):
                        pool.wait_ge(p_stored[k], 16 * (NGROUPS // 2))
                    for h in range(2 * QT):
                        nc.gpsimd.indirect_dma_start(heads[:, h // QT, (h % QT) * D:(h % QT + 1) * D], None, table_p,
                                                     bass.IndirectOffsetOnAxis(first_dst[0:QH, h:h + 1], 0)).then_inc(head_got, 16)

                @block.vector
                def _(dve):
                    V.tensor_scalar_max(inv[:], count[:], COUNT_EPS).then_inc(made, 1)
                    dve.wait_ge(made, 1)
                    V.reciprocal(inv[:], inv[:]).then_inc(made, 1)
                    dve.wait_ge(made, 2)
                    TT(inv[:], inv[:], nonempty[:], ALU.mult).then_inc(made, 1)
                    dve.wait_ge(made, 3)
                    dve.wait_ge(bias_in, 1)
                    V.tensor_copy(bias_b[:], pbias[:]).then_inc(made, 1)
                    dve.wait_ge(made, 4)
                    ch = Chain(dve, chain, 2)
                    ch2 = Chain(dve, chain2, LN_LINKS + 2)

                    def front(g, i, k, first):
                        ch.group(g)
                        dve.wait_ge(got[k], (i + 1) * (16 * GROUP))
                        ta = t[:, k, :, :]
                        TT(ta, rows[:, k, :, :], of_group(inv, g, 2 * D), ALU.mult).then_inc(taken, 1)
                        dve.wait_ge(taken, g + 1)
                        ch(TT(mean_sq[:], ta[:, :, 0:D], ta[:, :, 0:D], ALU.mult))
                        ch(TT(mean_sq[:], ta[:, :, D:2 * D], mean_sq[:], ALU.subtract))
                        V.tensor_scalar_max(dev[:, k, :, :], mean_sq[:], 0.0).then_inc(var0, 1)
                        dve.wait_ge(var0, g + 1)

                    def back(g, i, k, first):
                        ch2.group(g)
                        dve.wait_ge(dev_ready, g + 1)
                        if not first:
                            dve.wait_ge(turned, g - 1)
                            dve.wait_ge(kept, g - 1)
                        y = dev[:, k, :, :]
                        ch2(TT(y, y, of_group(several, g, D), ALU.mult))
                        ch2(TT(y, y, rows_of_group(X, g), ALU.add))
                        layernorm(dve, ch2, var, rooted, g, y, sq[:], m[:], v[:], rv[:], xs[:, k, :, :], final)
                        dve.wait_ge(product, g + 1)
                        if not first:
                            dve.wait_ge(p_stored[k], i * 16)
                            dve.wait_ge(scattered[k], i * (16 * GROUP))
                        TT(p_s[:, k, :, :], po_p[:, 0:GROUP, :], every_block(bias_b, D), ALU.add).then_inc(p_out, 1)
                    skewed(dve, [(0, front), (1, back)])

                @block.tensor
                def _(pe):
                    nc.tensor.matmul(pbias[:], ones[0:1, :], bias_sgn[:], start=True, stop=True).then_inc(bias_in, 1)

                    def part(g, i, k, first):
                        pe.wait_ge(final, g + 1)
                        if not first:
                            pe.wait_ge(evicted, g)
                        settled(pe)
                        turn_blocks(pt, xs[:, k, :, :]).then_inc(turned, 1)
                        pe.wait_ge(evicted, g + 1)
                        if not first:
                            pe.wait_ge(q_out, g)
                            pe.wait_ge(p_out, g)
                        for b in range(GROUP):
                            nc.tensor.matmul(po_q[:, b, :], xt[:, k, b * P:(b + 1) * P], w_qp[:, 0:D], start=True, stop=True)
                            last = nc.tensor.matmul(po_p[:, b, :], xt[:, k, b * P:(b + 1) * P], w_qp[:, D:2 * D], start=True, stop=True)
                        last.then_inc(product, 1)
                    skewed(pe, [(0, part)], first_at=1)

                @block.scalar
                def _(act):
                    def front(g, i, k, first):
                        act.wait_ge(var0, g + 1)
                        nc.scalar.sqrt(dev[:, k, :, :], dev[:, k, :, :]).then_inc(dev_ready, 1)

                    def back(g, i, k, first):
                        layernorm_root(act, var, rooted, g, v[:], rv[:])
                        act.wait_ge(turned, g + 1)
                        if not first:
                            act.wait_ge(product, g - 1)
                        nc.scalar.copy(xt[:, k, :], pt[:, 0:GROUP * P]).then_inc(evicted, 1)
                        act.wait_ge(final, g + 1)
                        nc.scalar.copy(rows_of_group(X, g), xs[:, k, :, :]).then_inc(kept, 1)
                        act.wait_ge(product, g + 1)
                        if not first:
                            act.wait_ge(q_stored[k], i * 16)
                        nc.scalar.copy(qs[:, k, :, :], po_q[:, 0:GROUP, :]).then_inc(q_out, 1)
                    skewed(act, [(0, front), (1, back)])

                @block.sync
                def _(sp):
                    def part(g, i, k, first):
                        sp.wait_ge(q_out, g + 1)
                        sp.dma_start(rows_of(table_q)[:, bass.ds(g * GROUP, GROUP), :], qs[:, k, :, :]).then_inc(q_stored[k], 16)
                        sp.wait_ge(p_out, g + 1)
                        sp.dma_start(rows_of(table_p)[:, bass.ds(g * GROUP, GROUP), :], p_s[:, k, :, :]).then_inc(p_stored[k], 16)
                    skewed(sp, [(0, part)])
                    for k in range(2):
                        sp.wait_ge(q_stored[k], 16 * (NGROUPS // 2))
                        sp.wait_ge(scattered[k], (NGROUPS // 2) * 16 * GROUP)
                    sp.wait_ge(head_got, 16 * 2 * QT)
                    hv = node_at_edge[0:EPAD, :].rearrange("(h q e j) w -> q h e (j w)", h=HALVES, q=QH, e=P)
                    for h in range(HALVES):
                        sp.dma_start(hv[:, h, 0, :], heads[:, h, :]).then_inc(head_put, 16)
                    sp.wait_ge(head_put, 32)

        stat_ctx = ExitStack()
        scale_b = sb(stat_ctx, "scale_b", [P, D])
        shift_b = sb(stat_ctx, "shift_b", [P, D])
        with ExitStack() as c:
            idx = sb(c, "e_idx", [P, SLOTS, QT], i32)
            spread = sb(c, "spread", [P, SLOTS, QT, P])
            msg = sb(c, "e_msg", [P, SLOTS, QT, D])
            at_edge = sb(c, "at_edge", [P, SLOTS, QT, D])
            hid = sb(c, "hid", [P, SLOTS, QT, D])
            hid_sq = sb(c, "hid_sq", [P, SLOTS, QT, D])
            acc = [pb(c, f"e_acc{k}", [P, QT * D]) for k in range(2)]
            moment = [pb(c, f"moment{k}", [1, QT * D]) for k in range(2)]
            got = [sem(c, f"e_got{k}") for k in range(SLOTS)]
            loaded = [sem(c, f"e_loaded{k}") for k in range(SLOTS)]
            stored = [sem(c, f"e_stored{k}") for k in range(SLOTS)]
            idx_ready = sem(c, "e_idx_ready")
            matrix_ready = sem(c, "e_matrix_ready")
            spread_done = sem(c, "e_spread_done")
            hid_ready = sem(c, "e_hid_ready")
            sq_ready = sem(c, "e_sq_ready")
            moments_done = sem(c, "e_moments_done")
            iters = NQ // SLOTS
            in_b = batches_of(node_at_edge[0:EPAD, :])
            out_b = batches_of(messages)
            last_tiles = [min(P, max(0, N_EDGES - ((NQ - 1) * EB + u * P))) for u in range(QT)]
            with nc.Block() as block:
                @block.gpsimd
                def _(pool):
                    def step(i, first):
                        for k in range(SLOTS):
                            pool.wait_ge(idx_ready, i * SLOTS + k + 1)
                            if not first:
                                pool.wait_ge(hid_ready, (i - 1) * SLOTS + k + 1)
                            settled(pool)
                            for u in range(QT):
                                nc.gpsimd.indirect_dma_start(msg[:, k, u, :], None, table_q,
                                                             bass.IndirectOffsetOnAxis(idx[:, k, u:u + 1], 0)).then_inc(got[k], 16)
                    step(0, True)
                    with pool.Fori(1, iters) as i:
                        step(i, False)

                @block.sync
                def _(sp):
                    for k in range(2):
                        sp.dma_start(at_edge[:, k, :, :].rearrange("p j d -> p (j d)"), in_b[k]).then_inc(loaded[k], 16)

                    def step(i, first, final):
                        for k in range(SLOTS):
                            ahead = (k + 2) % SLOTS
                            if not (final and k >= 2):
                                if not (first and k < 2):
                                    sp.wait_ge(spread_done, i * SLOTS + k - 1)
                                sp.dma_start(at_edge[:, ahead, :, :].rearrange("p j d -> p (j d)"), in_b[i * SLOTS + k + 2]).then_inc(loaded[ahead], 16)
                            sp.wait_ge(hid_ready, i * SLOTS + k + 1)
                            sp.dma_start(out_b[i * SLOTS + k], hid[:, k, :, :].rearrange("p j d -> p (j d)")).then_inc(stored[k], 16)
                    step(0, True, False)
                    with sp.Fori(1, iters - 1) as i:
                        step(i, False, False)
                    step(iters - 1, False, True)
                    for k in range(SLOTS):
                        sp.wait_ge(stored[k], iters * 16)

                @block.scalar
                def _(act):
                    for k in range(2):
                        nc.scalar.copy(idx[:, k, :], src_idx[:, k * QT:(k + 1) * QT]).then_inc(idx_ready, 1)

                    def step(i, first):
                        for k in range(SLOTS):
                            ahead = (k + 2) % SLOTS
                            if not (first and k < 2):
                                act.wait_ge(got[ahead], (i if k < 2 else i + 1) * (16 * QT))
                            nc.scalar.copy(idx[:, ahead, :], src_idx[:, bass.ds((i * SLOTS + k + 2) * QT, QT)]).then_inc(idx_ready, 1)
                            act.wait_ge(hid_ready, i * SLOTS + k + 1)
                            if not first:
                                act.wait_ge(moments_done, (i - 1) * SLOTS + k + 1)
                            nc.scalar.square(hid_sq[:, k, :, :], hid[:, k, :, :]).then_inc(sq_ready, 1)
                    step(0, True)
                    with act.Fori(1, iters) as i:
                        step(i, False)

                @block.vector
                def _(dve):
                    def step(i, first):
                        for k in range(SLOTS):
                            if not first:
                                dve.wait_ge(spread_done, (i - 1) * SLOTS + k + 1)
                            for u in range(QT):
                                t = i * (SLOTS * QT) + k * QT + u
                                last = nc.vector.tensor_scalar(spread[:, k, u, :], iota_upper[:], seg_end_first[:, bass.ds(t, 1)], None, ALU.is_le)
                            last.then_inc(matrix_ready, 1)
                            dve.wait_ge(spread_done, i * SLOTS + k + 1)
                            dve.wait_ge(got[k], (i + 1) * (16 * QT))
                            if not first:
                                dve.wait_ge(stored[k], i * 16)
                                dve.wait_ge(moments_done, (i - 1) * SLOTS + k + 1)
                            nc.vector.tensor_tensor(hid[:, k, :, :].rearrange("p j d -> p (j d)"), acc[k % 2][:],
                                                    msg[:, k, :, :].rearrange("p j d -> p (j d)"), ALU.add).then_inc(hid_ready, 1)
                    step(0, True)
                    with dve.Fori(1, iters) as i:
                        step(i, False)

                @block.tensor
                def _(pe):
                    def step(i, first, final):
                        for k in range(SLOTS):
                            pe.wait_ge(matrix_ready, i * SLOTS + k + 1)
                            pe.wait_ge(loaded[k], (i + 1) * 16)
                            if not (first and k < 2):
                                pe.wait_ge(hid_ready, i * SLOTS + k - 1)
                            for u in range(QT):
                                last = nc.tensor.matmul(acc[k % 2][:, u * D:(u + 1) * D], spread[:, k, u, :], at_edge[:, k, u, :], start=True, stop=True)
                            last.then_inc(spread_done, 1)
                            pe.wait_ge(sq_ready, i * SLOTS + k + 1)
                            begin = first and k == 0
                            if final and k == SLOTS - 1:
                                for m_ps, a in ((moment[0], hid), (moment[1], hid_sq)):
                                    for u in range(QT):
                                        n = last_tiles[u]
                                        if n:
                                            stop = u == QT - 1 or not last_tiles[u + 1]
                                            last = nc.tensor.matmul(m_ps[:, u * D:(u + 1) * D], ones[0:n, 0:1], a[0:n, k, u, :], start=False, stop=stop)
                            else:
                                for m_ps, a in ((moment[0], hid), (moment[1], hid_sq)):
                                    last = nc.tensor.matmul(m_ps[:], ones[:, 0:1], a[:, k, :, :].rearrange("p j d -> p (j d)"), start=begin, stop=False)
                            last.then_inc(moments_done, 1)
                    step(0, True, False)
                    with pe.Fori(1, iters - 1) as i:
                        step(i, False, False)
                    step(iters - 1, False, True)

            mu = sb(c, "mu", [1, D])
            va = sb(c, "va", [1, D])
            tq = sb(c, "tq", [1, D])
            bc = pb(c, "bc", [P, 2, D])
            s_st = sem(c, "s_st")
            s_bc = sem(c, "s_bc")
            s_bo = sem(c, "s_bo")
            tb = sb(c, "tb", [1, D])
            elementwise("bn", [
                ("v", lambda: V.reduce_sum(mu[:], moment[0][:].rearrange("p (j d) -> p d j", j=QT), AX.X)),
                ("v", lambda: V.reduce_sum(va[:], moment[1][:].rearrange("p (j d) -> p d j", j=QT), AX.X)),
                ("v", lambda: V.tensor_scalar_mul(mu[:], mu[:], 1.0 / N_EDGES)),
                ("v", lambda: TT(tq[:], mu[:], mu[:], ALU.mult)),
                ("v", lambda: V.scalar_tensor_tensor(va[:], va[:], 1.0 / N_EDGES, tq[:], ALU.mult, ALU.subtract)),
                ("v", lambda: V.tensor_scalar(va[:], va[:], 0.0, BN_EPS, ALU.max, ALU.add)),
                ("a", lambda: nc.scalar.sqrt(va[:], va[:])),
                ("v", lambda: V.reciprocal(tq[:], va[:])),
                ("v", lambda: V.tensor_scalar_mul(va[:], gamma[:], -1.0)),
                ("v", lambda: TT(va[:], va[:], gamma[:], ALU.max)),
                ("v", lambda: TT(tq[:], tq[:], va[:], ALU.mult)),
                ("v", lambda: V.tensor_scalar_max(tq[:], tq[:], 1e-20)),
                ("v", lambda: V.reciprocal(va[:], tq[:])),
                ("v", lambda: TT(tb[:], beta[:], va[:], ALU.mult)),
                ("v", lambda: TT(mu[:], tb[:], mu[:], ALU.subtract)),
            ])
            with nc.Block() as block:
                @block.tensor
                def _(pe):
                    nc.tensor.matmul(bc[:, 0, :], ones[0:1, :], tq[:], start=True, stop=True)
                    nc.tensor.matmul(bc[:, 1, :], ones[0:1, :], mu[:], start=True, stop=True).then_inc(s_bc, 1)

                @block.vector
                def _(dve):
                    dve.wait_ge(s_bc, 1)
                    nc.vector.tensor_copy(scale_b[:], bc[:, 0, :]).then_inc(s_bo, 1)
                    nc.vector.tensor_copy(shift_b[:], bc[:, 1, :]).then_inc(s_bo, 1)

        with ExitStack() as c:
            seg = sb(c, "f_seg", [P, SLOTS, QT, P])
            hid = sb(c, "f_hid", [P, SLOTS, QT, D])
            moved = sb(c, "f_moved", [P, SLOTS, QT, D])
            act_h = sb(c, "f_act", [P, SLOTS, QT, D])
            summed = sb(c, "f_sum", [P, SLOTS, QT * D])
            acc = [pb(c, f"f_acc{k}", [P, QT * D]) for k in range(2)]
            loaded = [sem(c, f"f_loaded{k}") for k in range(SLOTS)]
            stored = [sem(c, f"f_stored{k}") for k in range(SLOTS)]
            matrix_ready = sem(c, "f_matrix_ready")
            moved_ready = sem(c, "f_moved_ready")
            leaky_ready = sem(c, "f_leaky_ready")
            product_done = sem(c, "f_product_done")
            evicted = sem(c, "f_evicted")
            iters = NQ // SLOTS
            in_b = batches_of(messages)
            out_b = batches_of(prefix[D])
            with nc.Block() as block:
                @block.sync
                def _(sp):
                    def load(b, k):
                        sp.dma_start(hid[:, k, :, :].rearrange("p j d -> p (j d)"), in_b[b]).then_inc(loaded[k], 16)
                    for k in range(SLOTS):
                        load(k, k)

                    def step(i, final):
                        for k in range(SLOTS):
                            if not final:
                                sp.wait_ge(moved_ready, i * SLOTS + k + 1)
                                load((i + 1) * SLOTS + k, k)
                            sp.wait_ge(evicted, i * SLOTS + k + 1)
                            sp.dma_start(out_b[i * SLOTS + k], summed[:, k, :]).then_inc(stored[k], 16)
                    with sp.Fori(0, iters - 1) as i:
                        step(i, False)
                    step(iters - 1, True)
                    for k in range(SLOTS):
                        sp.wait_ge(stored[k], iters * 16)

                @block.gpsimd
                def _(pool):
                    def step(i, first):
                        for k in range(SLOTS):
                            pool.wait_ge(loaded[k], (i + 1) * 16)
                            if not first:
                                pool.wait_ge(leaky_ready, (i - 1) * SLOTS + k + 1)
                            nc.gpsimd.tensor_tensor(moved[:, k, :, :], hid[:, k, :, :],
                                                    shift_b[:, None, :].to_broadcast([P, QT, D]), ALU.add).then_inc(moved_ready, 1)
                    step(0, True)
                    with pool.Fori(1, iters) as i:
                        step(i, False)

                @block.scalar
                def _(act):
                    def step(i, first):
                        for k in range(SLOTS):
                            act.wait_ge(product_done, i * SLOTS + k + 1)
                            if not first:
                                act.wait_ge(stored[k], i * 16)
                            nc.scalar.copy(summed[:, k, :], acc[k % 2][:]).then_inc(evicted, 1)
                    step(0, True)
                    with act.Fori(1, iters) as i:
                        step(i, False)

                @block.vector
                def _(dve):
                    def step(i, first):
                        for k in range(SLOTS):
                            if not first:
                                dve.wait_ge(product_done, (i - 1) * SLOTS + k + 1)
                            for u in range(QT):
                                t = i * (SLOTS * QT) + k * QT + u
                                last = V.tensor_scalar(seg[:, k, u, :], iota_upper[:], seg_end[:, bass.ds(t, 1)], None, ALU.is_le)
                            last.then_inc(matrix_ready, 1)
                            dve.wait_ge(moved_ready, i * SLOTS + k + 1)
                            V.scalar_tensor_tensor(act_h[:, k, :, :], moved[:, k, :, :], SLOPE, moved[:, k, :, :], ALU.mult, ALU.max).then_inc(leaky_ready, 1)
                    step(0, True)
                    with dve.Fori(1, iters) as i:
                        step(i, False)

                @block.tensor
                def _(pe):
                    def step(i, first):
                        for k in range(SLOTS):
                            pe.wait_ge(matrix_ready, i * SLOTS + k + 1)
                            pe.wait_ge(leaky_ready, i * SLOTS + k + 1)
                            if not (first and k < 2):
                                pe.wait_ge(evicted, i * SLOTS + k - 1)
                            for u in range(QT):
                                last = nc.tensor.matmul(acc[k % 2][:, u * D:(u + 1) * D], seg[:, k, u, :], act_h[:, k, u, :], start=True, stop=True)
                            last.then_inc(product_done, 1)
                    step(0, True)
                    with pe.Fori(1, iters) as i:
                        step(i, False)
        carry_stage("c5", D)

        with ExitStack() as c:
            idx, rows, copied, got, taken = node_tools(c, "n5", D)
            inv = sb(c, "n5inv", [P, NB])
            inv_rel = sb(c, "n5inv_rel", [P, NB])
            some = sb(c, "n5some", [P, NB])
            y = sb(c, "n5y", [P, GROUP, D])
            y2 = sb(c, "n5y2", [P, 2, GROUP, D])
            sq = sb(c, "n5sq", [P, GROUP, D])
            m = sb(c, "n5m", [P, GROUP])
            v = sb(c, "n5v", [P, GROUP])
            rv = sb(c, "n5rv", [P, GROUP])
            v_b = sb(c, "n5v_b", [P, GROUP])
            rv_b = sb(c, "n5rv_b", [P, GROUP])
            xs = sb(c, "n5xs", [P, 2, GROUP, D])
            prod = sb(c, "n5prod", [P, 2, 2 * R, D])
            halved = sb(c, "n5halved", [P, 2, R, D])
            outs = sb(c, "n5outs", [P, 2, GROUP, D])
            group_counts = sb(c, "n5counts", [P, 2, GROUP, 2 * R])
            THIRD = 2 * R // 3
            pt = pb(c, "n5pt", [D, 8 * P])
            po = [pb(c, f"n5po{k}", [P, 3, 512]) for k in range(2)]
            chain, chain2, chain3, var, rooted, final, var_b, rooted_b, turned, evicted, product, mult_v, mult_a, added, relations, written = [
                sem(c, "n5" + n) for n in ("chain", "chain2", "chain3", "var", "rooted", "final", "var_b", "rooted_b", "turned",
                                           "evicted", "product", "mult_v", "mult_a", "added", "relations", "written")]
            made = sem(c, "n5made")
            counted = sem(c, "n5counted")
            final_b = sem(c, "n5final_b")
            out_stored = [sem(c, f"n5out_stored{k}") for k in range(2)]
            with nc.Block() as block:
                @block.gpsimd
                def _(pool):
                    def adds(g, i, k, first):
                        for b in range(GROUP):
                            s = (k + b) % 2
                            n = g * GROUP + b
                            pool.wait_ge(mult_v, n + 1)
                            pool.wait_ge(mult_a, n + 1)
                            if not (first and b < 2):
                                pool.wait_ge(relations, n - 1)
                            nc.gpsimd.tensor_tensor(halved[:, s, :, :], prod[:, s, 0:R, :], prod[:, s, R:2 * R, :], ALU.add).then_inc(added, 1)
                    skewed(pool, [(0, gather_part(pool, D, idx, rows, copied, got, taken)), (1, lambda g, i, k, f: adds(g, i, k, isinstance(g, int) and g == 0))])

                @block.vector
                def _(dve):
                    mk = chain_of(dve, made)
                    mk(V.tensor_scalar_max(inv[:], count[:], 1.0))
                    mk(V.reciprocal(inv[:], inv[:]))
                    mk(TT(inv[:], inv[:], nonempty[:], ALU.mult))
                    mk(V.reduce_sum(inv_rel[:], counts[:], AX.X))
                    mk(V.tensor_single_scalar(some[:], inv_rel[:], 0.0, ALU.is_gt))
                    mk(V.tensor_scalar_max(inv_rel[:], inv_rel[:], 1.0))
                    mk(V.reciprocal(inv_rel[:], inv_rel[:]))
                    mk(TT(inv_rel[:], inv_rel[:], some[:], ALU.mult))
                    ch = Chain(dve, chain, 2 + LN_LINKS)
                    ch3 = Chain(dve, chain3, 2 + LN_LINKS)

                    def front(g, i, k, first):
                        ch.group(g)
                        dve.wait_ge(got[k], (i + 1) * (16 * GROUP))
                        TT(y[:], rows[:, k, :, :], of_group(inv, g, D), ALU.mult).then_inc(taken, 1)
                        dve.wait_ge(taken, g + 1)
                        ch(TT(y[:], y[:], every_block(scale_b, D), ALU.mult))
                        ch(TT(y[:], y[:], rows_of_group(X, g), ALU.add))
                        layernorm(dve, ch, var, rooted, g, y[:], sq[:], m[:], v[:], rv[:], xs[:, k, :, :], final)
                        dve.wait_ge(final, g + 1)

                    def back(g, i, k, first):
                        ch3.group(g)
                        r_first = isinstance(g, int) and g == 0

                        def reduce(b):
                            s = (k + b) % 2
                            dve.wait_ge(added, g * GROUP + b + 1)
                            V.reduce_sum(y2[:, k, b, :], halved[:, s, :, :].rearrange("p r o -> p o r"), AX.X).then_inc(relations, 1)
                        for b in range(GROUP):
                            s = (k + b) % 2
                            n = g * GROUP + b
                            dve.wait_ge(product, n + 1)
                            if not (r_first and b < 2):
                                dve.wait_ge(added, n - 1)
                            TT(prod[:, s, 0:2 * THIRD, :].rearrange("p (a r) o -> p a r o", a=2),
                               po[s][:, 0:2, 0:THIRD * D].rearrange("p a (r o) -> p a r o", o=D),
                               counts[:, bass.ds(n, 1), 0:2 * THIRD].rearrange("p z (a r) -> p (z a) r", a=2)[:, :, :, None].to_broadcast([P, 2, THIRD, D]),
                               ALU.mult).then_inc(mult_v, 1)
                            if b > 0:
                                reduce(b - 1)
                        reduce(GROUP - 1)
                        dve.wait_ge(relations, (g + 1) * GROUP)
                        ya = y2[:, k, :, :]
                        ch3(TT(ya, ya, of_group(inv_rel, g, D), ALU.mult))
                        ch3(TT(ya, ya, xs[:, k, :, :], ALU.add))
                        if not first:
                            dve.wait_ge(out_stored[k], i * 16)
                        layernorm(dve, ch3, var_b, rooted_b, g, ya, sq[:], m[:], v_b[:], rv_b[:], outs[:, k, :, :], final_b)
                        dve.wait_ge(final_b, g + 1)
                    skewed(dve, [(0, front), (1, back)])

                @block.tensor
                def _(pe):
                    def part(g, i, k, first):
                        pe.wait_ge(final, g + 1)
                        if not first:
                            pe.wait_ge(evicted, g)
                        settled(pe)
                        turn_blocks(pt, xs[:, k, :, :]).then_inc(turned, 1)
                        pe.wait_ge(evicted, g + 1)
                        for b in range(GROUP):
                            s = (k + b) % 2
                            n = g * GROUP + b
                            if not (first and b < 2):
                                pe.wait_ge(mult_v, n - 1)
                                pe.wait_ge(mult_a, n - 1)
                            for a in range(3):
                                last = nc.tensor.matmul(po[s][:, a, 0:THIRD * D], lhs65[:, k, b * P:(b + 1) * P],
                                                        w_rel[:, a * THIRD:(a + 1) * THIRD, :].rearrange("i r o -> i (r o)"), start=True, stop=True)
                            last.then_inc(product, 1)
                    skewed(pe, [(0, part)], first_at=1)

                @block.scalar
                def _(act):
                    def root_of(g, i, k, first):
                        layernorm_root(act, var, rooted, g, v[:], rv[:])

                    def turned_rows(g, i, k, first):
                        act.wait_ge(turned, g + 1)
                        if not first:
                            act.wait_ge(product, (g - 1) * GROUP)
                        nc.scalar.copy(lhs65[0:D, k, :], pt[:, 0:GROUP * P]).then_inc(evicted, 1)
                        if not first:
                            act.wait_ge(mult_a, (g - 1) * GROUP)
                        nc.scalar.copy(group_counts[:, k, :, :], rows_of_group(counts, g)).then_inc(counted, 1)

                    def products(g, i, k, first):
                        r_first = isinstance(g, int) and g == 0
                        act.wait_ge(counted, g + 1)
                        for b in range(GROUP):
                            s = (k + b) % 2
                            n = g * GROUP + b
                            act.wait_ge(product, n + 1)
                            if not (r_first and b < 2):
                                act.wait_ge(added, n - 1)
                            for r in range(THIRD):
                                last = nc.scalar.activation(prod[:, s, 2 * THIRD + r, :], po[s][:, 2, r * D:(r + 1) * D], ACT.Copy,
                                                            scale=group_counts[:, k, b, 2 * THIRD + r:2 * THIRD + r + 1])
                            last.then_inc(mult_a, 1)

                    def last_root(g, i, k, first):
                        layernorm_root(act, var_b, rooted_b, g, v_b[:], rv_b[:])
                    skewed(act, [(0, root_of), (1, products), (0, turned_rows), (1, last_root)])

                @block.sync
                def _(sp):
                    def part(g, i, k, first):
                        sp.wait_ge(final_b, g + 1)
                        if isinstance(g, int) and g == NGROUPS - 1:
                            h0 = g * GROUP
                            sp.dma_start(out[h0 * P:(NB - 1) * P, :].rearrange("(h l) d -> l h d", l=P), outs[:, k, 0:GROUP - 1, :]).then_inc(out_stored[k], 16)
                            sp.dma_start(out[(NB - 1) * P:N_NODES, :], outs[0:N_NODES - (NB - 1) * P, k, GROUP - 1, :]).then_inc(out_stored[k], 16)
                        else:
                            sp.dma_start(rows_of(out[0:(NB - 1) * P, :])[:, bass.ds(g * GROUP, GROUP), :], outs[:, k, :, :]).then_inc(out_stored[k], 16)
                    for g in range(2):
                        part(g, 0, g, True)
                    with sp.Fori(1, NGROUPS // 2 - 1) as i:
                        for k in range(2):
                            part(2 * i + k, i, k, False)
                    for g in (NGROUPS - 2, NGROUPS - 1):
                        part(g, g // 2, g % 2, False)
                    sp.wait_ge(out_stored[0], 16 * (NGROUPS // 2))
                    sp.wait_ge(out_stored[1], 16 * (NGROUPS // 2 + 1))
        stat_ctx.close()


_INS = ["x", "src", "dst", "edge_type_9", "edge_weight", "L0_gnn_w1", "L0_gnn_b1", "L0_gnn_w2", "L0_gnn_b2", "L0_gnn_w3",
        "L0_gnn_b3", "L0_gnn_lw", "L0_gnn_lb", "L2_gnn_W", "L2_gnn_b", "L2_gnn_gamma", "L2_gnn_beta", "L3_gnn_weights",
        "L3_gnn_biases"]


def kernel(**inputs):
    import numpy as np
    import concourse.bacc as bacc
    from concourse.bass_utils import run_bass_kernel_spmd

    nc = bacc.Bacc("TRN2", target_bir_lowering=False, num_devices=1)
    arrays, args = {}, {}
    for name in _INS:
        a = np.ascontiguousarray(inputs[name])
        arrays[f"in_{name}"] = a
        args[name] = nc.dram_tensor(f"in_{name}", a.shape, mybir.dt.from_np(a.dtype), kind="ExternalInput").ap()
    out = nc.dram_tensor("out_0", (N_NODES, D), mybir.dt.float32, kind="ExternalOutput").ap()
    gnn_kernel(nc, args, out)
    r = run_bass_kernel_spmd(nc, [arrays], core_ids=[0])
    return r.results[0]["out_0"]
```

```python
import concourse.bass as bass
from concourse import mybir
from contextlib import ExitStack


P = 128
N_NODES, N_EDGES, D, R = 12500, 200000, 64, 9
NB = -(-N_NODES // P)
NPAD = NB * P
QT = 8
EB = QT * P
NQ = -(-N_EDGES // EB)
NT = NQ * QT
EPAD = NT * P
QH = NQ // 2
HALVES = 2
PAD_NODE = NPAD - 1
SLOTS = 4
SWEEP_SLOTS = 7
GROUP = 7
NGROUPS = NB // GROUP
LN_EPS = 1e-5
BN_EPS = 1e-5
COUNT_EPS = 1e-8
SLOPE = 0.3
assert NQ % (2 * SLOTS) in (0, SLOTS) and NQ % SLOTS == 0 and NB % (2 * GROUP) == 0


def gnn_kernel(nc, ins, out):
    f32, i32, bf16, f16 = mybir.dt.float32, mybir.dt.int32, mybir.dt.bfloat16, mybir.dt.float16
    ALU = mybir.AluOpType
    ACT = mybir.ActivationFunctionType
    AX = mybir.AxisListType
    root = ExitStack()
    semaphores_of = {}

    def sb(ctx, name, shape, dt=f32):
        return ctx.enter_context(nc.sbuf_tensor(name, shape, dt))

    def pb(ctx, name, shape, dt=f32):
        return ctx.enter_context(nc.psum_tensor(name, shape, dt))

    def sem(ctx, name):
        held = semaphores_of.get(id(ctx))
        if held is None:
            held = semaphores_of[id(ctx)] = []

            def release():
                nc.clear_and_free_semaphores(held)
                del semaphores_of[id(ctx)]
                with nc.Block():
                    pass
            ctx.callback(release)
        held.append(nc.alloc_semaphore(name))
        return held[-1]

    def dram(name, shape, dt=f32):
        return nc.dram_tensor(name, shape, dt).ap()

    table16 = dram("table16", (NPAD, 16))
    table16b = dram("table16b", (NPAD, 16))
    table32 = dram("table32", (NPAD, 32))
    table64 = dram("table64", (NPAD, D))
    table_q = dram("table_q", (NPAD, D))
    table_p = dram("table_p", (NPAD, D))
    windows = dram("windows", (NT + 1, 2 * P))
    prefix = {w: dram(f"prefix{w}", (EPAD, w)) for w in (25, 16, 32, 128, 64)}
    messages = dram("messages", (EPAD, D))
    node_at_edge = dram("node_at_edge", (EPAD + NPAD, D))

    with root:
        ident = sb(root, "ident", [P, P])
        anti = sb(root, "anti", [P, P])
        ones = sb(root, "ones", [P, P])
        upper = sb(root, "upper", [P, P])
        iota_row = sb(root, "iota_row", [P, P])
        iota_upper = sb(root, "iota_upper", [P, P])
        X = sb(root, "X", [P, NB, D])
        src_idx = sb(root, "src_idx", [P, NT + 2 * QT], i32)
        weight = sb(root, "weight", [P, NT])
        seg_end = sb(root, "seg_end", [P, NT])
        seg_end_first = sb(root, "seg_end_first", [P, NT])
        etype = sb(root, "etype", [P, NT])
        carry_on = sb(root, "carry_on", [P, NT])
        linked = sb(root, "linked", [P, 2 * QT])
        node_f = sb(root, "node_f", [P, NB])
        h16 = sb(root, "h16", [P, NB, 16])
        fix_row = sb(root, "fix_row", [P, 2 * QT], i32)
        first_dst = sb(root, "first_dst", [P, 2 * QT], i32)
        end_row = sb(root, "end_row", [P, NB], i32)
        start_row = sb(root, "start_row", [P, NB], i32)
        count = sb(root, "count", [P, NB])
        several = sb(root, "several", [P, NB])
        nonempty = sb(root, "nonempty", [P, NB])
        dinv = sb(root, "dinv", [P, NB])
        counts = sb(root, "counts", [P, NB, 2 * R])

        def chain_of(engine, s):
            n = [0]

            def link(instruction):
                n[0] += 1
                instruction.then_inc(s, 1)
                engine.wait_ge(s, n[0])
            return link

        turns = [sem(root, "turns_pe"), sem(root, "turns_pool")]

        def settled(engine):
            engine.sem_inc(turns[engine is nc.gpsimd], 1)

        def per_half(ap):
            return ap.rearrange("p (h q j) -> p h j q", h=HALVES, j=QT)

        w_first = sb(root, "w_first", [D + 1, 16 + D])
        w2a = sb(root, "w2a", [33, 32])
        w3a = sb(root, "w3a", [33, D])
        lw_low = sb(root, "lw_low", [D, D])
        b1row = sb(root, "b1row", [P, 16])
        w_qp = sb(root, "w_qp", [D, 2 * D])
        bn_b = sb(root, "bn_b", [1, D])
        gamma = sb(root, "gamma", [1, D])
        beta = sb(root, "beta", [1, D])
        w_rel = sb(root, "w_rel", [2 * D, 2 * R * D])
        bias_sgn = sb(root, "bias_sgn", [1, D])
        lhs65 = sb(root, "lhs65", [D + 1, 2, GROUP * P])
        lhs33 = sb(root, "lhs33", [33, 2, GROUP * P])
        zeroed_weights = [w_first[:], w2a[:], lhs33[:]]
        unit_rows = [lhs65[D:D + 1, :, :], lhs33[32:33, :, :]]

        def loads(w2_raw):
            lw = ins["L0_gnn_lw"]
            return [(w_first[0:D, 0:16], ins["L0_gnn_w1"]), (w_first[0:D, 16:16 + D], lw[0:D, :]),
                    (w_first[D:D + 1, 16:16 + D], ins["L0_gnn_lb"][None, :]),
                    (w2a[0:16, :], ins["L0_gnn_w2"]), (w2a[32:33, :], ins["L0_gnn_b2"][None, :]),
                    (w3a[0:32, :], ins["L0_gnn_w3"]), (w3a[32:33, :], ins["L0_gnn_b3"][None, :]),
                    (lw_low[:], lw[D:2 * D, :]),
                    (b1row[:], ins["L0_gnn_b1"][None, :].to_broadcast([P, 16])),
                    (w2_raw[:], ins["L2_gnn_W"].rearrange("o (a i) -> o a i", a=2)),
                    (bn_b[:], ins["L2_gnn_b"][None, :]), (gamma[:], ins["L2_gnn_gamma"][None, :]),
                    (beta[:], ins["L2_gnn_beta"][None, :]),
                    (w_rel[0:D, :].rearrange("i (r o) -> i r o", o=D), ins["L3_gnn_weights"][2].rearrange("r i o -> i r o")),
                    (w_rel[D:2 * D, :].rearrange("i (r o) -> i r o", o=D), ins["L3_gnn_weights"][2].rearrange("r i o -> i r o"))]

        def skewed(engine, parts, first_at=2, total=NGROUPS, unrolled=2):
            lag = max(n for n, _ in parts)
            begin = unrolled * -(-(lag + first_at) // unrolled)

            def step(s, i, k):
                for n, f in parts:
                    g = s - n
                    if not isinstance(s, int):
                        f(g, i + (k - n) // unrolled, (k - n) % unrolled, False)
                    elif 0 <= g < total:
                        f(g, g // unrolled, g % unrolled, g < first_at)
            for s in range(begin):
                step(s, s // unrolled, s % unrolled)
            with engine.Fori(begin // unrolled, total // unrolled) as i:
                for k in range(unrolled):
                    step(i * unrolled + k, i, k)
            for s in range(total, total + lag):
                step(s, s // unrolled, s % unrolled)

        def together(engine, lag, f, first_at=2):
            begin = 2 * ((lag + first_at + 1) // 2)

            def step(s, i, k):
                groups = []
                for n in range(lag + 1):
                    g = s - n
                    if not isinstance(s, int):
                        groups.append((g, i + (k - n) // 2, (k - n) % 2, False))
                    else:
                        groups.append((g, g // 2, g % 2, g < first_at) if 0 <= g < NGROUPS else None)
                f(*groups)
            for s in range(begin):
                step(s, s // 2, s % 2)
            with engine.Fori(begin // 2, NGROUPS // 2) as i:
                for k in range(2):
                    step(2 * i + k, i, k)
            for s in range(NGROUPS, NGROUPS + lag):
                step(s, s // 2, s % 2)

        V = nc.vector
        TT = nc.vector.tensor_tensor

        edges_ctx = ExitStack()
        iota_i = sb(edges_ctx, "iota_i", [P, P], i32)
        node_i = sb(edges_ctx, "node_i", [P, NB], i32)
        ew_f = sb(edges_ctx, "ew_f", [QH, HALVES, EB])
        src_f = sb(edges_ctx, "src_f", [QH, HALVES, EB])
        dst_f = sb(edges_ctx, "dst_f", [QH, HALVES, EB])
        typ_f = sb(edges_ctx, "typ_f", [QH, HALVES, EB])
        below = sb(edges_ctx, "below", [P, P])
        corner = sb(edges_ctx, "corner", [P, P])
        prev_f = sb(edges_ctx, "prev_f", [QH, HALVES])
        next_f = sb(edges_ctx, "next_f", [QH, HALVES])
        tau = sb(edges_ctx, "tau", [P, NB])
        tau_i = sb(edges_ctx, "tau_i", [P, NB], i32)
        qbase = sb(edges_ctx, "qbase", [QH, 2 * QT], i32)
        full = N_EDGES // EB - QH
        rest = N_EDGES - (QH + full) * EB
        inner = ExitStack()
        src_i = sb(inner, "src_i", [QH, HALVES, EB], i32)
        dst_i = sb(inner, "dst_i", [QH, HALVES, EB], i32)
        typ_i = sb(inner, "typ_i", [QH, HALVES, EB], i32)
        prev_i = sb(inner, "prev_i", [QH, HALVES], i32)
        next_i = sb(inner, "next_i", [QH, HALVES], i32)
        w2_raw = sb(inner, "w2_raw", [D, 2, D])
        head = sb(inner, "head", [QH, HALVES, EB])
        same = sb(inner, "q_same", [QH, HALVES, EB])
        running_w = sb(inner, "running_w", [QH, HALVES, EB])
        tile_end = sb(inner, "tile_end", [QH, 2 * QT], i32)
        tile_lo = sb(inner, "tile_lo", [QH, 2 * QT])
        tile_hi = sb(inner, "tile_hi", [QH, 2 * QT])
        bits = sb(inner, "bits", [QH, 2 * QT], i32)
        lo_hot = sb(inner, "lo_hot", [QH, 2 * QT, P])
        hi_hot = sb(inner, "hi_hot", [QH, 2 * QT, NB])
        tiles_at = sb(inner, "tiles_at", [P, NB])
        all_q = sb(inner, "all_q", [P, NB])
        run_q = sb(inner, "run_q", [P, NB])
        link_q = sb(inner, "link_q", [QH, HALVES])
        chain_q = sb(inner, "chain_q", [QH, HALVES])
        last_q = sb(inner, "last_q", [QH, HALVES])
        row_q = sb(inner, "row_q", [1, 2 * NQ])
        run_row = sb(inner, "run_row", [1, 1 + NQ])
        carry_in = sb(inner, "carry_in", [QH, HALVES])
        far = sb(inner, "far", [1, 2 * P])
        sgn = sb(inner, "sgn", [1, D])
        s_pad = sem(inner, "s_pad")
        s_set = sem(inner, "s_set")
        s_dst = sem(inner, "s_dst")
        s_ew = sem(inner, "s_ew")
        s_rest = sem(inner, "s_rest")
        s_wts = sem(inner, "s_wts")
        s_const = sem(inner, "s_const")
        s_dve = sem(inner, "s_dve")
        s_hot = sem(inner, "s_hot")
        s_tiles = sem(inner, "s_tiles")
        s_cum = sem(inner, "s_cum")
        s_rowq = sem(inner, "s_rowq")
        s_colq = sem(inner, "s_colq")
        s_scan = sem(inner, "s_scan")
        s_dstwin = sem(inner, "s_dstwin")
        s_prewin = sem(inner, "s_prewin")
        s_win = sem(inner, "s_win")
        s_wraw = sem(inner, "s_wraw")
        s_sgn = sem(inner, "s_sgn")
        hist = pb(inner, "tile_hist", [P, NB])
        incl = pb(inner, "incl", [P, NB])
        totals = pb(inner, "totals", [P, NB])
        psq = pb(inner, "psq", [1, 2 * NQ])
        psc = pb(inner, "psc", [QH, HALVES])
        psw = pb(inner, "psw", [D, 3, D])

        def edge_rows(a):
            return [(lambda t: t[:, 0, :], a[0:QH * EB].rearrange("(q e) -> q e", e=EB)),
                    (lambda t: t[0:full, 1, :], a[QH * EB:(QH + full) * EB].rearrange("(q e) -> q e", e=EB)),
                    (lambda t: t[full:full + 1, 1, 0:rest], a[(QH + full) * EB:N_EDGES].rearrange("(q e) -> q e", q=1))]

        CONSTANTS = 16

        with nc.Block() as block:
            @block.gpsimd
            def _(pool):
                link = chain_of(pool, s_const)
                G = nc.gpsimd
                link(G.iota(iota_i[:], pattern=[[1, P]], base=0, channel_multiplier=0))
                link(G.tensor_copy(iota_row[:], iota_i[:]))
                link(G.memset(ones[:], 1.0))
                link(G.memset(ident[:], 0.0))
                link(G.memset(anti[:], 0.0))
                link(G.affine_select(out=ident[:], in_=ident[:], compare_op=ALU.not_equal, fill=1.0,
                                     base=0, pattern=[[1, P]], channel_multiplier=-1))
                link(G.affine_select(out=upper[:], in_=ones[:], compare_op=ALU.is_ge, fill=0.0,
                                     base=0, pattern=[[1, P]], channel_multiplier=-1))
                link(G.affine_select(out=anti[:], in_=anti[:], compare_op=ALU.not_equal, fill=1.0,
                                     base=-(P - 1), pattern=[[1, P]], channel_multiplier=1))
                link(G.affine_select(out=iota_upper[:], in_=iota_row[:], compare_op=ALU.is_ge,
                                     fill=999.0, base=0, pattern=[[1, P]], channel_multiplier=-1))
                link(G.memset(below[:], 0.0))
                link(G.memset(corner[:], 0.0))
                link(G.affine_select(out=below[:], in_=below[:], compare_op=ALU.not_equal, fill=1.0,
                                     base=-1, pattern=[[1, P]], channel_multiplier=-1))
                link(G.affine_select(out=corner[:], in_=corner[:], compare_op=ALU.not_equal, fill=1.0,
                                     base=P - 1, pattern=[[P, P]], channel_multiplier=-1))
                link(G.iota(node_i[:], pattern=[[P, NB]], base=0, channel_multiplier=1))
                link(G.tensor_copy(node_f[:], node_i[:]))
                link(G.iota(qbase[:].rearrange("q (h j) -> q h j", h=HALVES), pattern=[[0, HALVES], [1, QT]],
                            base=0, channel_multiplier=EB))
                for t in zeroed_weights:
                    G.memset(t, 0.0).then_inc(s_set, 1)
                pool.wait_ge(s_set, len(zeroed_weights))
                for t in unit_rows:
                    G.memset(t, 1.0).then_inc(s_set, 1)

            @block.sync
            def _(sp):
                sp.wait_ge(s_pad, 1)
                for part, a in edge_rows(ins["dst"]):
                    sp.dma_start(part(dst_i), a).then_inc(s_dst, 16)
                sp.wait_ge(s_pad, 4)
                last = ins["dst"][0:(2 * QH - 1) * EB].rearrange("(q e) -> q e", e=EB)
                with nc.allow_non_contiguous_dma(reason="one index per batch"):
                    sp.dma_start(prev_i[1:QH, 0:1], last[0:QH - 1, EB - 1:EB]).then_inc(s_dst, 16)
                    sp.dma_start(prev_i[0:QH, 1:2], last[QH - 1:2 * QH - 1, EB - 1:EB]).then_inc(s_dst, 16)
                    sp.dma_start(next_i[0:QH, 0:1], last[1:QH + 1, 0:1]).then_inc(s_dst, 16)
                    sp.dma_start(next_i[0:QH - 2, 1:2], last[QH + 1:2 * QH - 1, 0:1]).then_inc(s_dst, 16)
                    sp.dma_start(next_i[QH - 2:QH - 1, 1:2], ins["dst"][(2 * QH - 1) * EB:(2 * QH - 1) * EB + 1][None, :]).then_inc(s_dst, 16)
                sp.wait_ge(s_pad, 5)
                for part, a in edge_rows(ins["edge_weight"]):
                    sp.dma_start(part(ew_f), a).then_inc(s_ew, 16)
                sp.wait_ge(s_dstwin, 1)
                def windows_out(src, col):
                    for h in range(HALVES):
                        rows = windows[h * QH * QT:(h + 1) * QH * QT, :].rearrange("(q j) c -> q j c", j=QT)
                        rows1 = windows[h * QH * QT + 1:(h + 1) * QH * QT + 1, :].rearrange("(q j) c -> q j c", j=QT)
                        v = src[:, h, :].rearrange("q (j e) -> q j e", e=P)
                        sp.dma_start(rows[:, :, col + 1:col + P], v[:, :, 0:P - 1]).then_inc(s_win, 16)
                        sp.dma_start(rows1[:, :, col:col + 1], v[:, :, P - 1:P]).then_inc(s_win, 16)
                with nc.allow_non_contiguous_dma(reason="a column of the windows"):
                    windows_out(dst_f, 0)
                    sp.dma_start(windows[0:1, 0:1], far[0:1, 0:1]).then_inc(s_win, 16)
                    sp.dma_start(windows[0:1, P:P + 1], far[0:1, P:P + 1]).then_inc(s_win, 16)
                    sp.dma_start(windows[NT:NT + 1, 1:P], far[0:1, 1:P]).then_inc(s_win, 16)
                    sp.dma_start(windows[NT:NT + 1, P + 1:2 * P], far[0:1, P + 1:2 * P]).then_inc(s_win, 16)
                    sp.wait_ge(s_prewin, 1)
                    windows_out(running_w, P)
                sp.wait_ge(s_win, 16 * 12)

            @block.scalar
            def _(act):
                act.wait_ge(s_dst, 16 * 8)
                act.wait_ge(s_pad, 2)
                act.dma_start(X[:, 0:NB - 1, :], ins["x"][0:(NB - 1) * P, :].rearrange("(h l) d -> l h d", l=P)).then_inc(s_rest, 16)
                act.dma_start(X[0:N_NODES - (NB - 1) * P, NB - 1, :], ins["x"][(NB - 1) * P:N_NODES, :]).then_inc(s_rest, 16)
                act.wait_ge(s_pad, 7)
                for t, name in ((src_i, "src"), (typ_i, "edge_type_9")):
                    for part, a in edge_rows(ins[name]):
                        act.dma_start(part(t), a).then_inc(s_rest, 16)
                act.wait_ge(s_set, len(zeroed_weights) + len(unit_rows))
                for a, b in loads(w2_raw):
                    act.dma_start(a, b).then_inc(s_wts, 16)
                act.wait_ge(s_rest, 16 * 8)
                act.wait_ge(s_wts, 16 * len(loads(w2_raw)))
                nc.scalar.copy(src_f[:], src_i[:])
                nc.scalar.copy(typ_f[:], typ_i[:])

            @block.tensor
            def _(pe):
                pe.wait_ge(s_hot, 1)
                for t in range(2 * QT):
                    last = nc.tensor.matmul(hist[:], lo_hot[:, t, :], hi_hot[:, t, :], start=t == 0, stop=t == 2 * QT - 1)
                last.then_inc(s_tiles, 1)
                pe.wait_ge(s_const, CONSTANTS)
                pe.wait_ge(s_rowq, 1)
                for n, v in enumerate((last_q, chain_q)):
                    for h in range(HALVES):
                        last = nc.tensor.matmul(psq[0:1, n * NQ + h * QH:n * NQ + (h + 1) * QH], v[:, h:h + 1], ident[0:QH, 0:QH],
                                                start=True, stop=True)
                last.then_inc(s_colq, 1)
                pe.wait_ge(s_scan, 1)
                for h in range(HALVES):
                    last = nc.tensor.matmul(psc[:, h:h + 1], run_row[0:1, h * QH:(h + 1) * QH], ones[0:1, 0:1], start=True, stop=True)
                last.then_inc(s_colq, 1)
                pe.wait_ge(s_cum, 1)
                nc.tensor.matmul(incl[:], upper[:], tiles_at[:], start=True, stop=True)
                nc.tensor.matmul(totals[:], ones[:], tiles_at[:], start=True, stop=True).then_inc(s_tiles, 1)
                pe.wait_ge(s_wts, 16 * len(loads(w2_raw)))
                pe.wait_ge(s_sgn, 1)
                nc.tensor.transpose(psw[:, 0, :], w2_raw[:, 0, :], ident[0:D, 0:D])
                nc.tensor.transpose(psw[:, 1, :], w2_raw[:, 1, :], ident[0:D, 0:D])
                nc.tensor.matmul(psw[:, 2, :], ones[0:1, 0:D], sgn[:], start=True, stop=True).then_inc(s_wraw, 1)

            @block.vector
            def _(dve):
                link = chain_of(dve, s_dve)
                V.memset(dst_i[:], PAD_NODE).then_inc(s_pad, 1)
                V.memset(X[:, NB - 1, :], 0.0).then_inc(s_pad, 1)
                V.memset(prev_i[:], -1).then_inc(s_pad, 1)
                V.memset(next_i[:], PAD_NODE).then_inc(s_pad, 1)
                V.memset(ew_f[:], 0.0).then_inc(s_pad, 1)
                V.memset(src_i[:], PAD_NODE).then_inc(s_pad, 1)
                V.memset(typ_i[:], 0).then_inc(s_pad, 1)
                V.memset(src_idx[:, NT:], PAD_NODE).then_inc(s_pad, 1)
                link(V.memset(far[0:1, 1:P], 99999.0))
                link(V.memset(far[0:1, P:2 * P], 0.0))
                link(V.memset(far[0:1, 0:1], -1.0))
                dve.wait_ge(s_dst, 16 * 8)
                link(V.tensor_copy(next_f[:], next_i[:]))
                link(V.tensor_copy(prev_f[:], prev_i[:]))
                V.tensor_copy(dst_f[:], dst_i[:]).then_inc(s_dstwin, 1)
                dve.wait_ge(s_dstwin, 1)
                ends = dst_i[:].rearrange("q h (j e) -> q (h j) e", e=P)[:, :, P - 1]
                link(V.tensor_single_scalar(bits[:], ends, 7, ALU.logical_shift_right))
                link(V.tensor_copy(tile_hi[:], bits[:]))
                link(V.tensor_single_scalar(bits[:], ends, P - 1, ALU.bitwise_and))
                link(V.tensor_copy(tile_lo[:], bits[:]))
                dve.wait_ge(s_const, 2)
                link(TT(lo_hot[:], iota_row[0:QH, None, :].to_broadcast([QH, 2 * QT, P]),
                        tile_lo[:, :, None].to_broadcast([QH, 2 * QT, P]), ALU.is_equal))
                TT(hi_hot[:], iota_row[0:QH, None, 0:NB].to_broadcast([QH, 2 * QT, NB]),
                   tile_hi[:, :, None].to_broadcast([QH, 2 * QT, NB]), ALU.is_equal).then_inc(s_hot, 1)
                dve.wait_ge(s_hot, 1)
                link(V.memset(same[:, :, 0:1], 0.0))
                link(TT(same[:, :, 1:EB], dst_f[:, :, 1:EB], dst_f[:, :, 0:EB - 1], ALU.is_equal))
                dve.wait_ge(s_ew, 48)
                link(V.tensor_tensor_scan(running_w[:].rearrange("q h e -> q (h e)"), same[:].rearrange("q h e -> q (h e)"),
                                          ew_f[:].rearrange("q h e -> q (h e)"), 0.0, ALU.mult, ALU.add))
                link(TT(link_q[:], dst_f[:, :, 0], prev_f[:], ALU.is_equal))
                link(TT(chain_q[:], dst_f[:, :, 0], dst_f[:, :, EB - 1], ALU.is_equal))
                link(TT(chain_q[:], chain_q[:], link_q[:], ALU.mult))
                V.tensor_copy(last_q[:], running_w[:, :, EB - 1]).then_inc(s_rowq, 1)
                dve.wait_ge(s_colq, 1)
                link(V.tensor_copy(row_q[:], psq[:]))
                link(V.memset(run_row[:, 0:1], 0.0))
                V.tensor_tensor_scan(run_row[:, 1:1 + NQ], row_q[:, NQ:2 * NQ], row_q[:, 0:NQ], 0.0, ALU.mult, ALU.add).then_inc(s_scan, 1)
                for h in range(HALVES):
                    link(V.tensor_scalar(head[:, h, :], dst_f[:, h, :], dst_f[:, h, 0:1], None, ALU.is_equal))
                dve.wait_ge(s_tiles, 1)
                V.tensor_copy(tiles_at[:], hist[:]).then_inc(s_cum, 1)
                dve.wait_ge(s_colq, 2)
                link(TT(carry_in[:], psc[:], link_q[:], ALU.mult))
                for h in range(HALVES):
                    link(V.scalar_tensor_tensor(running_w[:, h, :], head[:, h, :], carry_in[:, h:h + 1], running_w[:, h, :],
                                                ALU.mult, ALU.add))
                link(TT(same[:, :, 0:EB - 1], dst_f[:, :, 1:EB], dst_f[:, :, 0:EB - 1], ALU.not_equal))
                link(TT(same[:, :, EB - 1], dst_f[:, :, EB - 1], next_f[:], ALU.not_equal))
                TT(running_w[:], running_w[:], same[:], ALU.mult).then_inc(s_prewin, 1)
                dve.wait_ge(s_tiles, 2)
                link(V.tensor_copy(all_q[:], totals[:]))
                link(V.memset(run_q[:], 1.0))
                link(V.tensor_tensor_scan(tau[:], run_q[:], all_q[:], 0.0, ALU.mult, ALU.add))
                link(TT(tau[:], tau[:], all_q[:], ALU.subtract))
                link(TT(tau[:], tau[:], incl[:], ALU.add))
                link(V.tensor_copy(tau_i[:], tau[:]))
                dve.wait_ge(s_wts, 16 * len(loads(w2_raw)))
                link(V.tensor_scalar(sgn[:], gamma[:], 0.0, 2.0, ALU.is_ge, ALU.mult))
                V.tensor_scalar_add(sgn[:], sgn[:], -1.0).then_inc(s_sgn, 1)
                dve.wait_ge(s_sgn, 1)
                dve.wait_ge(s_wraw, 1)
                link(TT(bias_sgn[:], bn_b[:], sgn[:], ALU.mult))
                link(V.tensor_copy(w_qp[:, D:2 * D], psw[:, 2, :]))
                link(TT(w_qp[:, 0:D], w_qp[:, D:2 * D], psw[:, 1, :], ALU.mult))
                link(TT(w_qp[:, D:2 * D], w_qp[:, D:2 * D], psw[:, 0, :], ALU.mult))
                link(TT(w_qp[:, D:2 * D], w_qp[:, D:2 * D], w_qp[:, 0:D], ALU.subtract))
                dve.wait_ge(s_const, CONSTANTS)
                link(TT(w_first[0:D, 16:16 + D], w_first[0:D, 16:16 + D], ident[0:D, 0:D], ALU.add))
        inner.close()

        c = ExitStack()
        same = sb(c, "same", [QH, 2 * QT, P])
        rev = sb(c, "rev", [QH, 2 * QT, P])
        eval_rev = sb(c, "eval_rev", [QH, P])
        end_rev = sb(c, "end_rev", [QH, 2 * QT * P])
        is_first = sb(c, "is_first", [QH, 2 * QT, P])
        dst_t = sb(c, "dst_t", [P, NT])
        first_t = sb(c, "first_t", [P, NT])
        end_rev_t = dst_t
        diag = is_first[:].rearrange("q t e -> q (t e)")[:, 0:2 * QT * QH].rearrange("q (t m) -> q t m", m=QH)
        carry_q = sb(c, "carry_q", [QH, 2 * QT])
        tmp_q = sb(c, "tmp_q", [QH, 2 * QT])
        qbase_f = sb(c, "qbase_f", [QH, 2 * QT])
        widx = sb(c, "widx", [P, 2, GROUP], i32)
        window = sb(c, "window", [P, 2, GROUP, 2 * P])
        cmp = sb(c, "cmp", [P, GROUP, P])
        upto = sb(c, "upto", [P, NB])
        deg = sb(c, "deg", [P, NB])
        xs = sb(c, "xs", [P, 2, GROUP, D])
        ps = pb(c, "ps", [P, 4, 512])
        pt = pb(c, "xw_pt", [D, 8 * P])
        po = pb(c, "xw_po", [P, 8, P])
        t_pe = sem(c, "t_pe")
        t_ev = sem(c, "t_ev")
        t_seg = sem(c, "t_seg")
        t_first = sem(c, "t_first")
        t_diag = sem(c, "t_diag")
        t_dve = sem(c, "t_dve")
        w_idx = sem(c, "w_idx")
        w_got = [sem(c, f"w_got{k}") for k in range(2)]
        w_taken = sem(c, "w_taken")
        w_chain = sem(c, "w_chain")
        x_in = sem(c, "x_in")
        x_turned = sem(c, "x_turned")
        x_evicted = sem(c, "x_evicted")
        x_done = sem(c, "x_done")
        x_out = sem(c, "x_out")
        HJ = [(h, j0) for h in range(HALVES) for j0 in (0, 4)]

        def view4(ap3, h, j0):
            return ap3[:, h, j0:j0 + 4, :]

        with nc.Block() as block:
            @block.tensor
            def _(pe):
                g = 0

                def group(fill):
                    nonlocal g
                    if g >= 4:
                        pe.wait_ge(t_ev, g - 3)
                    for j in range(4):
                        last = fill(j, g % 4)
                    last.then_inc(t_pe, 1)
                    g += 1

                def tr(src):
                    for h, j0 in HJ:
                        group(lambda j, b: nc.tensor.transpose(
                            ps[:, b, j * QH:(j + 1) * QH], src(h, j0 + j), ident[0:QH, 0:QH]))
                tr(lambda h, j: dst_f[:, h, j * P:(j + 1) * P])
                pe.wait_ge(t_ev, 4)
                for h, j0 in HJ:
                    group(lambda j, b: nc.tensor.matmul(
                        ps[0:QH, b, j * P:(j + 1) * P], per_half(dst_t[:])[:, h, j0 + j, :], anti[:],
                        start=True, stop=True))
                for a in (src_f, typ_f, ew_f):
                    tr(lambda h, j, a=a: a[:, h, j * P:(j + 1) * P])
                pe.wait_ge(t_first, 1)
                tr(lambda h, j: is_first[:, h * QT + j, :])
                pe.wait_ge(t_seg, 1)
                tr(lambda h, j: end_rev[:, (h * QT + j) * P:(h * QT + j + 1) * P])
                pe.wait_ge(t_ev, 28)
                for k in range(4):
                    pe.wait_ge(t_ev, g - 3)
                    nc.tensor.matmul(ps[:, g % 4, 0:NT // 4], anti[:], end_rev_t[:, k * (NT // 4):(k + 1) * (NT // 4)],
                                     start=True, stop=True).then_inc(t_pe, 1)
                    g += 1
                pe.wait_ge(t_diag, 1)
                for h, j0 in HJ:
                    group(lambda j, b: nc.tensor.matmul(
                        ps[:, b, j * QH:(j + 1) * QH], ones[0:QH, :], diag[:, h * QT + j0 + j, :],
                        start=True, stop=True))

                def turn(g, i, k, first):
                    pe.wait_ge(x_in, g + 1)
                    if not first:
                        pe.wait_ge(x_evicted, g)
                    settled(pe)
                    for b in range(GROUP):
                        last = nc.tensor.transpose(pt[:, b * P:(b + 1) * P], xs[:, k, b, :], ident[:])
                    last.then_inc(x_turned, 1)
                    pe.wait_ge(x_evicted, g + 1)
                    if not first:
                        pe.wait_ge(x_out, g)
                    for b in range(GROUP):
                        last = nc.tensor.matmul(po[:, b, 0:16 + D], lhs65[:, k, b * P:(b + 1) * P], w_first[:], start=True, stop=True)
                    last.then_inc(x_done, 1)
                skewed(pe, [(0, turn)], first_at=1)

            @block.scalar
            def _(act):
                g = 0

                def evict(out_ap, n, parts=P):
                    nonlocal g
                    act.wait_ge(t_pe, g + 1)
                    v = ps[0:parts, g % 4, 0:4 * n].rearrange("p (j q) -> p j q", j=4)
                    nc.scalar.copy(out_ap, v).then_inc(t_ev, 1)
                    g += 1
                for h, j0 in HJ:
                    evict(view4(per_half(dst_t[:]), h, j0), QH)
                for h, j0 in HJ:
                    evict(rev[:, h * QT + j0:h * QT + j0 + 4, :], P, QH)
                for a in (src_idx[:, 0:NT], etype[:], weight[:], first_t[:], end_rev_t[:]):
                    for h, j0 in HJ:
                        evict(view4(per_half(a), h, j0), QH)
                for k in range(4):
                    evict(seg_end[:, k * (NT // 4):(k + 1) * (NT // 4)].rearrange("p (j q) -> p j q", j=4), NT // 16)
                for h, j0 in HJ:
                    evict(view4(per_half(carry_on[:]), h, j0), QH)

                def step(g, i, k, first):
                    if not first:
                        act.wait_ge(x_turned, g - 1)
                    nc.scalar.copy(xs[:, k, :, :], X[:, bass.ds(g * GROUP, GROUP), :]).then_inc(x_in, 1)
                    act.wait_ge(x_turned, g + 1)
                    if not first:
                        act.wait_ge(x_done, g - 1)
                    nc.scalar.copy(lhs65[0:D, k, :], pt[:, 0:GROUP * P]).then_inc(x_evicted, 1)
                    act.wait_ge(x_done, g + 1)
                    nc.scalar.copy(h16[:, bass.ds(g * GROUP, GROUP), :], po[:, 0:GROUP, 0:16])
                    nc.scalar.copy(X[:, bass.ds(g * GROUP, GROUP), :], po[:, 0:GROUP, 16:16 + D]).then_inc(x_out, 1)
                skewed(act, [(0, step)])

            @block.gpsimd
            def _(pool):
                def step(g, i, k, first):
                    if not first:
                        pool.wait_ge(w_taken, g - 1)
                    nc.gpsimd.tensor_copy(widx[:, k, :], tau_i[:, bass.ds(g * GROUP, GROUP)]).then_inc(w_idx, 1)
                    pool.wait_ge(w_idx, g + 1)
                    settled(pool)
                    for u in range(GROUP):
                        nc.gpsimd.indirect_dma_start(window[:, k, u, :], None, windows,
                                                     bass.IndirectOffsetOnAxis(widx[:, k, u:u + 1], 0)).then_inc(w_got[k], 16)
                skewed(pool, [(0, step)])

            @block.vector
            def _(dve):
                link = chain_of(dve, t_dve)
                dstv = dst_f[:].rearrange("q h (j e) -> q (h j) e", e=P)
                link(TT(same[:, :, 1:P], dstv[:, :, 1:P], dstv[:, :, 0:P - 1], ALU.is_equal))
                link(V.memset(is_first[:, :, 0:1], 1.0))
                V.tensor_scalar(is_first[:, :, 1:P], same[:, :, 1:P], -1.0, 1.0, ALU.mult, ALU.add).then_inc(t_first, 1)
                lv = linked[0:QH, :].rearrange("q (h j) -> q h j", h=HALVES)
                df = dst_f[:].rearrange("q h (j e) -> q h j e", e=P)
                link(TT(lv[:, :, 1:QT], df[:, :, 1:QT, 0], df[:, :, 0:QT - 1, P - 1], ALU.is_equal))
                link(TT(lv[:, :, 0], df[:, :, 0, 0], prev_f[:], ALU.is_equal))
                link(V.tensor_copy(first_dst[0:QH, :].rearrange("q (h j) -> q h j", h=HALVES), df[:, :, :, 0]))
                link(V.tensor_scalar(eval_rev[:], iota_row[0:QH, :], -1.0, float(P - 1), ALU.mult, ALU.add))
                dve.wait_ge(t_first, 1)
                dve.wait_ge(t_ev, 8)
                link(V.memset(same[:, :, 0:1], 0.0))
                link(TT(same[:, :, 1:P], rev[:, :, 1:P], rev[:, :, 0:P - 1], ALU.is_equal))
                link(V.tensor_scalar(rev[:], same[:], -1.0, 1.0, ALU.mult, ALU.add))
                link(TT(rev[:], rev[:], eval_rev[:, None, :].to_broadcast([QH, 2 * QT, P]), ALU.mult))
                V.tensor_tensor_scan(end_rev[:], same[:].rearrange("q t e -> q (t e)"),
                                     rev[:].rearrange("q t e -> q (t e)"), 0.0, ALU.mult, ALU.add).then_inc(t_seg, 1)
                dve.wait_ge(t_seg, 1)
                ev = end_rev[:].rearrange("q (t e) -> q t e", e=P)[:, :, P - 1]
                link(V.tensor_single_scalar(tmp_q[:], ev, float(P - 1), ALU.is_equal))
                link(TT(carry_q[:], tmp_q[:], linked[0:QH, :], ALU.mult))
                dve.wait_ge(t_ev, 24)
                link(TT(diag, ident[0:QH, None, 0:QH].to_broadcast([QH, 2 * QT, QH]),
                        carry_q[:, :, None].to_broadcast([QH, 2 * QT, QH]), ALU.mult))
                V.tensor_copy(qbase_f[:], qbase[:]).then_inc(t_diag, 1)
                dve.wait_ge(t_diag, 1)
                link(V.tensor_scalar_add(qbase_f[:, QT:], qbase_f[:, QT:], float(QH * EB)))
                link(V.scalar_tensor_tensor(qbase_f[:], ev, float(QT), qbase_f[:], ALU.mult, ALU.add))
                link(V.tensor_copy(fix_row[0:QH, :], qbase_f[:]))
                dve.wait_ge(t_ev, 32)
                link(V.tensor_scalar_add(seg_end_first[:], seg_end[:], 1.0))
                link(TT(seg_end_first[:], seg_end_first[:], first_t[:], ALU.mult))
                link(V.tensor_scalar_add(seg_end_first[:], seg_end_first[:], -1.0))

                def step(g, i, k, first):
                    dve.wait_ge(w_got[k], (i + 1) * (16 * GROUP))
                    nodes = node_f[:, bass.ds(g * GROUP, GROUP)][:, :, None].to_broadcast([P, GROUP, P])
                    TT(cmp[:], window[:, k, :, 0:P], nodes, ALU.is_equal).then_inc(w_chain, 1)
                    dve.wait_ge(w_chain, g * 3 + 1)
                    TT(window[:, k, :, P:2 * P], cmp[:], window[:, k, :, P:2 * P], ALU.mult).then_inc(w_chain, 1)
                    TT(window[:, k, :, 0:P], window[:, k, :, 0:P], nodes, ALU.is_le).then_inc(w_chain, 1)
                    dve.wait_ge(w_chain, g * 3 + 3)
                    V.reduce_sum(upto[:, bass.ds(g * GROUP, GROUP)], window[:, k, :, 0:P], AX.X)
                    V.reduce_sum(deg[:, bass.ds(g * GROUP, GROUP)], window[:, k, :, P:2 * P], AX.X).then_inc(w_taken, 1)
                    dve.wait_ge(w_taken, g + 1)
                skewed(dve, [(0, step)])

        shifted = po[:, 0, 0:NB]
        end_buf = sb(c, "end_buf", [P, 1 + NB])
        end_f = end_buf[:, 1:1 + NB]
        tmp = sb(c, "tmp", [P, NB])
        tmp2 = sb(c, "tmp2", [P, NB])
        pos = sb(c, "pos", [P, NB])
        ti = sb(c, "ti", [P, NB], i32)
        tj = sb(c, "tj", [P, NB], i32)
        tk = sb(c, "tk", [P, NB], i32)
        d_ch = sem(c, "d_ch")
        d_end = sem(c, "d_end")
        d_pe = sem(c, "d_pe")
        d_deg = sem(c, "d_deg")
        d_sqrt = sem(c, "d_sqrt")
        d_h = sem(c, "d_h")
        d_out = sem(c, "d_out")
        with nc.Block() as block:
            @block.tensor
            def _(pe):
                pe.wait_ge(d_end, 1)
                nc.tensor.matmul(shifted, below[:], end_f, start=True, stop=False)
                nc.tensor.matmul(shifted, corner[:], end_buf[:, 0:NB], start=False, stop=True).then_inc(d_pe, 1)

            @block.scalar
            def _(act):
                act.wait_ge(d_deg, 1)
                nc.scalar.sqrt(tmp2[:], tmp[:]).then_inc(d_sqrt, 1)

            @block.sync
            def _(sp):
                sp.wait_ge(d_h, 1)
                sp.dma_start(table16.rearrange("(h l) d -> l h d", l=P), h16[:]).then_inc(d_out, 16)
                sp.wait_ge(d_out, 16)

            @block.vector
            def _(dve):
                link = chain_of(dve, d_ch)
                link(V.tensor_scalar_add(dinv[:], deg[:], 1.0))
                link(V.tensor_single_scalar(pos[:], dinv[:], 0.0, ALU.is_gt))
                V.tensor_scalar_max(tmp[:], dinv[:], 1e-30).then_inc(d_deg, 1)
                link(V.memset(end_buf[:, 0:1], 0.0))
                link(V.scalar_tensor_tensor(end_f, tau[:], float(P), upto[:], ALU.mult, ALU.add))
                V.tensor_scalar_add(end_f, end_f, -1.0).then_inc(d_end, 1)
                dve.wait_ge(d_end, 1)
                dve.wait_ge(d_sqrt, 1)
                link(V.reciprocal(dinv[:], tmp2[:]))
                link(TT(dinv[:], dinv[:], pos[:], ALU.mult))
                TT(h16[:], h16[:], dinv[:, :, None].to_broadcast([P, NB, 16]), ALU.mult).then_inc(d_h, 1)
                dve.wait_ge(d_pe, 1)
                link(TT(count[:], end_f, shifted, ALU.subtract))
                link(V.tensor_single_scalar(nonempty[:], count[:], 0.0, ALU.is_gt))
                link(V.tensor_single_scalar(several[:], count[:], 1.0, ALU.is_gt))
                dve.wait_ge(d_h, 1)

                def to_row(edge_f, row):
                    link(V.tensor_copy(ti[:], edge_f))
                    link(V.tensor_scalar(tj[:], ti[:], 10, 10, ALU.logical_shift_right, ALU.logical_shift_left))
                    link(V.tensor_scalar(tk[:], ti[:], P - 1, 3, ALU.bitwise_and, ALU.logical_shift_left))
                    link(TT(tj[:], tj[:], tk[:], ALU.bitwise_or))
                    link(V.tensor_scalar(tk[:], ti[:], 7, QT - 1, ALU.logical_shift_right, ALU.bitwise_and))
                    link(TT(row, tj[:], tk[:], ALU.bitwise_or))
                link(V.tensor_scalar(tmp[:], end_f, -1.0, 0.0, ALU.add, ALU.max))
                to_row(tmp[:], end_row[:])
                link(V.tensor_scalar_min(tmp[:], shifted[:], float(EPAD - 1)))
                to_row(tmp[:], start_row[:])
                link(V.tensor_copy(tmp[:], start_row[:]))
                link(V.tensor_scalar_add(tmp2[:], node_f[:], float(EPAD)))
                link(TT(tmp[:], tmp[:], tmp2[:], ALU.subtract))
                link(TT(tmp[:], tmp[:], nonempty[:], ALU.mult))
                link(TT(tmp[:], tmp[:], tmp2[:], ALU.add))
                link(V.tensor_copy(start_row[:], tmp[:]))
        c.close()
        edges_ctx.close()

        def rows_of(dram_ap):
            return dram_ap.rearrange("(h l) d -> l h d", l=P)

        def batches_of(dram_ap):
            return dram_ap.rearrange("(b e j) w -> b e (j w)", e=P, j=QT)

        def edge_pass(tag, table, gathered, width, weighted=False, with_types=False, squares=False,
                      histogram=None, zero_fill=None):
            with ExitStack() as c:
                idx = sb(c, tag + "idx", [P, SLOTS, QT], i32)
                segment_matrix = sb(c, tag + "seg", [P, SLOTS, QT, P])
                msg = sb(c, tag + "msg", [P, SLOTS, QT, width])
                summed = sb(c, tag + "sum", [P, SLOTS, QT * width])
                acc = [pb(c, tag + f"acc{k}", [P, QT * width]) for k in range(2)]
                gathered_rows = [sem(c, tag + f"gathered{k}") for k in range(SLOTS)]
                stored = [sem(c, tag + f"stored{k}") for k in range(SLOTS)]
                idx_ready = sem(c, tag + "idx_ready")
                matrix_ready = sem(c, tag + "matrix_ready")
                msg_ready = sem(c, tag + "msg_ready")
                product_done = sem(c, tag + "product_done")
                evicted = sem(c, tag + "evicted")
                hot_ready = sem(c, tag + "hot_ready")
                hot_used = sem(c, tag + "hot_used")
                zero_set = sem(c, tag + "zero_set")
                zeroed = sem(c, tag + "zeroed")
                out_b = batches_of(prefix[width])
                iters = NQ // SLOTS
                if histogram is not None:
                    key_lo, key_hi, iota_key = histogram["lo"], histogram["hi"], histogram["iota"]
                    hot_lo = sb(c, tag + "hot_lo", [P, 2, QT, P], bf16)
                    hot_hi = sb(c, tag + "hot_hi", [P, 2, QT, NB * R], bf16)
                    hacc = [pb(c, tag + f"hacc{k}", [P, NB * R // 2]) for k in range(2)]
                if zero_fill is not None:
                    zeros = sb(c, tag + "zeros", [P, QT * D])
                with nc.Block() as block:
                    @block.gpsimd
                    def _(pool):
                        def step(i, first):
                            for k in range(SLOTS):
                                pool.wait_ge(idx_ready, i * SLOTS + k + 1)
                                if not first:
                                    pool.wait_ge(product_done, (i - 1) * SLOTS + k + 1)
                                settled(pool)
                                for u in range(QT):
                                    nc.gpsimd.indirect_dma_start(
                                        msg[:, k, u, 0:gathered], None, table,
                                        bass.IndirectOffsetOnAxis(idx[:, k, u:u + 1], 0)).then_inc(gathered_rows[k], 16)
                        step(0, True)
                        with pool.Fori(1, iters) as i:
                            step(i, False)

                    @block.scalar
                    def _(act):
                        for k in range(2):
                            nc.scalar.copy(idx[:, k, :], src_idx[:, k * QT:(k + 1) * QT]).then_inc(idx_ready, 1)

                        def step(i, first):
                            for k in range(SLOTS):
                                ahead = (k + 2) % SLOTS
                                if not (first and k < 2):
                                    act.wait_ge(gathered_rows[ahead], ((i if k < 2 else i + 1)) * (16 * QT))
                                nc.scalar.copy(idx[:, ahead, :], src_idx[:, bass.ds((i * SLOTS + k + 2) * QT, QT)]).then_inc(idx_ready, 1)
                                if squares:
                                    act.wait_ge(gathered_rows[k], (i + 1) * (16 * QT))
                                    nc.scalar.square(msg[:, k, :, gathered:2 * gathered], msg[:, k, :, 0:gathered]).then_inc(msg_ready, 1)
                                act.wait_ge(product_done, i * SLOTS + k + 1)
                                if not first:
                                    act.wait_ge(stored[k], i * 16)
                                for a in range(0, QT * width, 512):
                                    z = min(a + 512, QT * width)
                                    last = nc.scalar.copy(summed[:, k, a:z], acc[k % 2][:, a:z])
                                last.then_inc(evicted, 1)
                        step(0, True)
                        with act.Fori(1, iters) as i:
                            step(i, False)

                    @block.sync
                    def _(sp):
                        if zero_fill is not None:
                            sp.wait_ge(zero_set, 1)
                        with sp.Fori(0, iters) as i:
                            for k in range(SLOTS):
                                sp.wait_ge(evicted, i * SLOTS + k + 1)
                                sp.dma_start(out_b[i * SLOTS + k], summed[:, k, :]).then_inc(stored[k], 16)
                                if zero_fill is not None:
                                    sp.dma_start(zero_fill[i * SLOTS + k], zeros[:]).then_inc(zeroed, 16)
                        for k in range(SLOTS):
                            sp.wait_ge(stored[k], iters * 16)
                        if zero_fill is not None:
                            sp.wait_ge(zeroed, NQ * 16)

                    @block.vector
                    def _(dve):
                        if zero_fill is not None:
                            nc.vector.memset(zeros[:], 0.0).then_inc(zero_set, 1)

                        def step(i, first):
                            for k in range(SLOTS):
                                if not first:
                                    dve.wait_ge(product_done, (i - 1) * SLOTS + k + 1)
                                for u in range(QT):
                                    t = i * (SLOTS * QT) + k * QT + u
                                    end = seg_end[:, bass.ds(t, 1)]
                                    if weighted:
                                        last = nc.vector.tensor_scalar(segment_matrix[:, k, u, :], iota_upper[:], end,
                                                                       weight[:, bass.ds(t, 1)], ALU.is_le, ALU.mult)
                                    else:
                                        last = nc.vector.tensor_scalar(segment_matrix[:, k, u, :], iota_upper[:], end,
                                                                       None, ALU.is_le)
                                last.then_inc(matrix_ready, 1)
                                if with_types:
                                    t0 = i * (SLOTS * QT) + k * QT
                                    nc.vector.tensor_tensor(
                                        msg[:, k, :, gathered:gathered + R],
                                        iota_row[:, None, 0:R].to_broadcast([P, QT, R]),
                                        etype[:, bass.ds(t0, QT)][:, :, None].to_broadcast([P, QT, R]), ALU.is_equal)
                                    dve.wait_ge(gathered_rows[k], (i + 1) * (16 * QT))
                                    nc.vector.tensor_tensor(
                                        msg[:, k, :, 0:gathered], msg[:, k, :, 0:gathered],
                                        weight[:, bass.ds(t0, QT)][:, :, None].to_broadcast([P, QT, gathered]),
                                        ALU.mult).then_inc(msg_ready, 1)
                                if histogram is not None:
                                    s = k % 2
                                    if not (first and k < 2):
                                        dve.wait_ge(hot_used, i * SLOTS + k - 1)
                                    for u in range(QT):
                                        t = i * (SLOTS * QT) + k * QT + u
                                        nc.vector.tensor_scalar(hot_lo[:, s, u, :], iota_key[:, 0:P], key_lo[:, bass.ds(t, 1)], None, ALU.is_equal)
                                        last = nc.vector.tensor_scalar(hot_hi[:, s, u, :], iota_key[:], key_hi[:, bass.ds(t, 1)], None, ALU.is_equal)
                                    last.then_inc(hot_ready, 1)
                        step(0, True)
                        with dve.Fori(1, iters) as i:
                            step(i, False)

                    @block.tensor
                    def _(pe):
                        def step(i, first, final):
                            for k in range(SLOTS):
                                if histogram is not None:
                                    s = k % 2
                                    pe.wait_ge(hot_ready, i * SLOTS + k + 1)
                                    half = NB * R // 2
                                    for u in range(QT):
                                        for a in range(2):
                                            last = nc.tensor.matmul(hacc[a][:], hot_lo[:, s, u, :], hot_hi[:, s, u, a * half:(a + 1) * half],
                                                                    start=first and k == 0 and u == 0,
                                                                    stop=final and k == SLOTS - 1 and u == QT - 1)
                                    last.then_inc(hot_used, 1)
                                pe.wait_ge(matrix_ready, i * SLOTS + k + 1)
                                if with_types or squares:
                                    pe.wait_ge(msg_ready, i * SLOTS + k + 1)
                                pe.wait_ge(gathered_rows[k], (i + 1) * (16 * QT))
                                if not (first and k < 2):
                                    pe.wait_ge(evicted, i * SLOTS + k - 1)
                                for u in range(QT):
                                    last = nc.tensor.matmul(acc[k % 2][:, u * width:(u + 1) * width], segment_matrix[:, k, u, :],
                                                            msg[:, k, u, :], start=True, stop=True)
                                last.then_inc(product_done, 1)
                        step(0, True, False)
                        with pe.Fori(1, iters - 1) as i:
                            step(i, False, False)
                        step(iters - 1, False, True)
                if histogram is not None:
                    done = sem(c, tag + "hist_out")
                    with nc.Block() as block:
                        @block.vector
                        def _(dve):
                            half = NB // 2
                            for a in range(2):
                                nc.vector.tensor_copy(counts[:, a * half:(a + 1) * half, 0:R],
                                                      hacc[a][:].rearrange("p (n r) -> p n r", r=R)).then_inc(done, 1)

        def carry_stage(tag, width):
            pre = prefix[width]
            with ExitStack() as c:
                tile_last = sb(c, tag + "tile_last", [QH, HALVES, QT, width])
                totals_t = sb(c, tag + "totals_t", [width, NT])
                running = sb(c, tag + "running", [width, 1 + NT])
                carried = sb(c, tag + "carried", [QH, 2 * QT, width])
                ps4 = pb(c, tag + "ps4", [P, 4, 512])
                qs4 = pb(c, tag + "qs4", [P, 4, 512])
                last_loaded = sem(c, tag + "last_loaded")
                turned = sem(c, tag + "turned")
                turned_out = sem(c, tag + "turned_out")
                scanned = sem(c, tag + "scanned")
                back = sem(c, tag + "back")
                carried_ready = sem(c, tag + "carried_ready")
                rows_back = sem(c, tag + "rows_back")
                HJ = [(h, j0) for h in range(HALVES) for j0 in (0, 4)]
                with nc.Block() as block:
                    @block.sync
                    def _(sp):
                        v = pre.rearrange("(h q e j) w -> q h e (j w)", h=HALVES, q=QH, e=P)
                        for h in range(HALVES):
                            sp.dma_start(tile_last[:, h, :, :].rearrange("q j w -> q (j w)"), v[:, h, P - 1, :]).then_inc(last_loaded, 16)

                    @block.tensor
                    def _(pe):
                        pe.wait_ge(last_loaded, 32)
                        for g, (h, j0) in enumerate(HJ):
                            for j in range(4):
                                last = nc.tensor.transpose(ps4[0:width, g, j * QH:(j + 1) * QH], tile_last[:, h, j0 + j, :],
                                                           ident[0:QH, 0:QH])
                            last.then_inc(turned, 1)
                        pe.wait_ge(scanned, 2)
                        rv = per_half(running[:, 0:NT])
                        for g, (h, j0) in enumerate(HJ):
                            for j in range(4):
                                last = nc.tensor.transpose(qs4[0:QH, g, j * width:(j + 1) * width], rv[:, h, j0 + j, :],
                                                           ident[0:width, 0:width])
                            last.then_inc(back, 1)

                    @block.scalar
                    def _(act):
                        for g, (h, j0) in enumerate(HJ):
                            act.wait_ge(turned, g + 1)
                            nc.scalar.copy(per_half(totals_t[:])[:, h, j0:j0 + 4, :],
                                           ps4[0:width, g, 0:4 * QH].rearrange("p (j q) -> p j q", j=4)).then_inc(turned_out, 1)

                    @block.vector
                    def _(dve):
                        V.memset(running[:, 0:1], 0.0).then_inc(scanned, 1)
                        dve.wait_ge(turned_out, 4)
                        V.tensor_tensor_scan(running[:, 1:1 + NT], carry_on[0:width, :], totals_t[:], 0.0,
                                             ALU.mult, ALU.add).then_inc(scanned, 1)
                        for g in range(4):
                            dve.wait_ge(back, g + 1)
                            TT(carried[:, 4 * g:4 * g + 4, :], qs4[0:QH, g, 0:4 * width].rearrange("q (j w) -> q j w", j=4),
                               linked[0:QH, 4 * g:4 * g + 4][:, :, None].to_broadcast([QH, 4, width]), ALU.mult).then_inc(carried_ready, 1)

                    @block.gpsimd
                    def _(pool):
                        for t in range(2 * QT):
                            pool.wait_ge(carried_ready, t // 4 + 1)
                            nc.gpsimd.indirect_dma_start(pre, bass.IndirectOffsetOnAxis(fix_row[0:QH, t:t + 1], 0),
                                                         carried[:, t, :], None, compute_op=ALU.add).then_inc(rows_back, 16)
                        pool.wait_ge(rows_back, 16 * 2 * QT)

        def gather_part(pool, width, idx, rows, copied, got, taken):
            def part(g, i, k, first):
                if not first:
                    pool.wait_ge(taken, g - 1)
                nc.gpsimd.tensor_copy(idx[:, k, :], end_row[:, bass.ds(g * GROUP, GROUP)]).then_inc(copied, 1)
                pool.wait_ge(copied, g + 1)
                settled(pool)
                for u in range(GROUP):
                    nc.gpsimd.indirect_dma_start(rows[:, k, u, :], None, prefix[width],
                                                 bass.IndirectOffsetOnAxis(idx[:, k, u:u + 1], 0)).then_inc(got[k], 16)
            return part

        def of_group(v, g, width=None):
            a = v[:, bass.ds(g * GROUP, GROUP)]
            return a if width is None else a[:, :, None].to_broadcast([P, GROUP, width])

        def rows_of_group(v, g):
            return v[:, bass.ds(g * GROUP, GROUP), :]

        def every_block(v, width):
            return v[:, None, :].to_broadcast([P, GROUP, width])

        class Chain:

            def __init__(self, engine, s, length):
                self.engine, self.s, self.length = engine, s, length

            def group(self, g):
                self.base, self.n = g * self.length, 0

            def __call__(self, instruction):
                self.n += 1
                assert self.n <= self.length
                instruction.then_inc(self.s, 1)
                self.engine.wait_ge(self.s, self.base + self.n)

        def layernorm_center(ch, y, m):
            ch(V.reduce_sum(m, y, AX.X))
            ch(V.tensor_scalar_mul(m, m, 1.0 / D))
            ch(TT(y, y, m[:, :, None].to_broadcast([P, GROUP, D]), ALU.subtract))

        def layernorm_var(ch, s_var, y, sq, v):
            ch(TT(sq, y, y, ALU.mult))
            ch(V.reduce_sum(v, sq, AX.X))
            V.tensor_scalar(v, v, 1.0 / D, LN_EPS, ALU.mult, ALU.add).then_inc(s_var, 1)

        def layernorm_scale(dve, ch, s_root, g, y, m, root_v, dst, done):
            dve.wait_ge(s_root, g + 1)
            ch(V.reciprocal(m, root_v))
            TT(dst, y, m[:, :, None].to_broadcast([P, GROUP, D]), ALU.mult).then_inc(done, 1)

        def layernorm(dve, ch, s_var, s_root, g, y, sq, m, v, root_v, dst, done):
            layernorm_center(ch, y, m)
            layernorm_var(ch, s_var, y, sq, v)
            layernorm_scale(dve, ch, s_root, g, y, m, root_v, dst, done)

        LN_LINKS = 6

        def layernorm_root(act, s_var, s_root, g, v, root_v):
            act.wait_ge(s_var, g + 1)
            nc.scalar.sqrt(root_v, v).then_inc(s_root, 1)

        def turn_blocks(out_ps, src):
            for b in range(GROUP):
                last = nc.tensor.transpose(out_ps[:, b * P:(b + 1) * P], src[:, b, :], ident[:])
            return last

        def node_tools(c, tag, width):
            idx = sb(c, tag + "idx", [P, 2, GROUP], i32)
            rows = sb(c, tag + "rows", [P, 2, GROUP, width])
            copied = sem(c, tag + "copied")
            got = [sem(c, tag + f"got{k}") for k in range(2)]
            taken = sem(c, tag + "taken")
            return idx, rows, copied, got, taken

        edge_pass("p1", table16, 16, 25, with_types=True, zero_fill=batches_of(node_at_edge[0:EPAD, :]))
        carry_stage("c1", 25)
        with ExitStack() as c:
            idx, rows, copied, got, taken = node_tools(c, "n1", 25)
            y = sb(c, "n1y", [P, 2, GROUP, 16])
            chain = sem(c, "n1chain")
            stored = sem(c, "n1stored")
            with nc.Block() as block:
                @block.gpsimd
                def _(pool):
                    skewed(pool, [(0, gather_part(pool, 25, idx, rows, copied, got, taken))])

                @block.vector
                def _(dve):
                    ch = Chain(dve, chain, 5)

                    def part(g, i, k, first):
                        ch.group(g)
                        dve.wait_ge(got[k], (i + 1) * (16 * GROUP))
                        ya = y[:, k, :, :]
                        TT(rows_of_group(counts, g)[:, :, R:2 * R], rows[:, k, :, 16:25], of_group(nonempty, g, R), ALU.mult)
                        ch(TT(ya, rows[:, k, :, 0:16], of_group(nonempty, g, 16), ALU.mult))
                        ch(TT(ya, ya, rows_of_group(h16, g), ALU.add))
                        ch(TT(ya, ya, of_group(dinv, g, 16), ALU.mult))
                        ch(TT(ya, ya, every_block(b1row, 16), ALU.add))
                        ch(V.tensor_scalar_max(ya, ya, 0.0))
                        TT(rows_of_group(h16, g), ya, of_group(dinv, g, 16), ALU.mult).then_inc(taken, 1)
                    skewed(dve, [(0, part)])

                @block.sync
                def _(sp):
                    def part(g, i, k, first):
                        sp.wait_ge(taken, g + 1)
                        sp.dma_start(rows_of(table16b)[:, bass.ds(g * GROUP, GROUP), :], rows_of_group(h16, g)).then_inc(stored, 16)
                    skewed(sp, [(0, part)])
                    sp.wait_ge(stored, 16 * NGROUPS)
        with ExitStack() as c:
            key_lo = sb(c, "key_lo", [P, NT])
            key_hi = sb(c, "key_hi", [P, NT])
            ki = sb(c, "ki", [P, NT], i32)
            iota_ki = sb(c, "iota_ki", [P, NB * R], i32)
            iota_key = sb(c, "iota_key", [P, NB * R], f16)
            made = sem(c, "made_iota")
            keyed = sem(c, "keyed")
            with nc.Block() as block:
                @block.gpsimd
                def _(pool):
                    nc.gpsimd.iota(iota_ki[:], pattern=[[1, NB * R]], base=0, channel_multiplier=0).then_inc(made, 1)

                @block.vector
                def _(dve):
                    link = chain_of(dve, keyed)
                    link(V.tensor_single_scalar(ki[:], src_idx[:, 0:NT], 7, ALU.logical_shift_right))
                    link(V.tensor_copy(key_hi[:], ki[:]))
                    link(V.scalar_tensor_tensor(key_hi[:], key_hi[:], float(R), etype[:], ALU.mult, ALU.add))
                    link(V.tensor_single_scalar(ki[:], src_idx[:, 0:NT], P - 1, ALU.bitwise_and))
                    link(V.tensor_copy(key_lo[:], ki[:]))
                    dve.wait_ge(made, 1)
                    link(V.tensor_copy(iota_key[:], iota_ki[:]))
            edge_pass("p2", table16b, 16, 16, weighted=True,
                      histogram={"lo": key_lo, "hi": key_hi, "iota": iota_key})
        carry_stage("c2", 16)
        L0 = ExitStack()
        h32 = sb(L0, "h32", [P, NB, 32])
        with ExitStack() as c:
            idx, rows, copied, got, taken = node_tools(c, "n2", 16)
            y = sb(c, "n2y", [P, 2, GROUP, 16])
            z = sb(c, "n2z", [P, 2, GROUP, 32])
            pt = pb(c, "n2pt", [16, 8 * P])
            po = pb(c, "n2po", [P, GROUP, 32])
            chain, ready, turned, evicted, product, relued, final, stored = [
                sem(c, "n2" + n) for n in ("chain", "ready", "turned", "evicted", "product", "relued", "final", "stored")]
            with nc.Block() as block:
                @block.gpsimd
                def _(pool):
                    skewed(pool, [(0, gather_part(pool, 16, idx, rows, copied, got, taken))])

                @block.vector
                def _(dve):
                    ch = Chain(dve, chain, 1)

                    def front(g, i, k, first):
                        ch.group(g)
                        dve.wait_ge(got[k], (i + 1) * (16 * GROUP))
                        if not first:
                            dve.wait_ge(turned, g - 1)
                        ya = y[:, k, :, :]
                        TT(ya, rows[:, k, :, :], of_group(nonempty, g, 16), ALU.mult).then_inc(taken, 1)
                        dve.wait_ge(taken, g + 1)
                        ch(TT(ya, ya, rows_of_group(h16, g), ALU.add))
                        TT(ya, ya, of_group(dinv, g, 16), ALU.mult).then_inc(ready, 1)

                    def back(g, i, k, first):
                        dve.wait_ge(relued, g + 1)
                        TT(rows_of_group(h32, g), z[:, k, :, :], of_group(dinv, g, 32), ALU.mult).then_inc(final, 1)
                    skewed(dve, [(0, front), (1, back)])

                @block.tensor
                def _(pe):
                    def part(g, i, k, first):
                        pe.wait_ge(ready, g + 1)
                        if not first:
                            pe.wait_ge(evicted, g)
                        settled(pe)
                        turn_blocks(pt, y[:, k, :, :]).then_inc(turned, 1)
                        pe.wait_ge(evicted, g + 1)
                        if not first:
                            pe.wait_ge(relued, g)
                        for b in range(GROUP):
                            last = nc.tensor.matmul(po[:, b, :], lhs33[:, k, b * P:(b + 1) * P], w2a[:], start=True, stop=True)
                        last.then_inc(product, 1)
                    skewed(pe, [(0, part)], first_at=1)

                @block.scalar
                def _(act):
                    def part(g, i, k, first):
                        act.wait_ge(turned, g + 1)
                        if not first:
                            act.wait_ge(product, g - 1)
                        nc.scalar.copy(lhs33[0:16, k, :], pt[:, 0:GROUP * P]).then_inc(evicted, 1)
                        act.wait_ge(product, g + 1)
                        if not first:
                            act.wait_ge(final, g - 1)
                        nc.scalar.activation(z[:, k, :, :], po[:], ACT.Relu).then_inc(relued, 1)
                    skewed(act, [(0, part)])

                @block.sync
                def _(sp):
                    def part(g, i, k, first):
                        sp.wait_ge(final, g + 1)
                        sp.dma_start(rows_of(table32)[:, bass.ds(g * GROUP, GROUP), :], rows_of_group(h32, g)).then_inc(stored, 16)
                    skewed(sp, [(0, part)])
                    sp.wait_ge(stored, 16 * NGROUPS)
        edge_pass("p3", table32, 32, 32, weighted=True)
        carry_stage("c3", 32)
        with ExitStack() as c:
            idx, rows, copied, got, taken = node_tools(c, "n3", 32)
            y = sb(c, "n3y", [P, 2, GROUP, 32])
            x4 = sb(c, "n3x4", [P, 2, GROUP, D])
            x4t = sb(c, "n3x4t", [D, 2, GROUP * P])
            r = sb(c, "n3r", [P, GROUP, D])
            sq = sb(c, "n3sq", [P, GROUP, D])
            m = sb(c, "n3m", [P, GROUP])
            v = sb(c, "n3v", [P, GROUP])
            rv = sb(c, "n3rv", [P, GROUP])
            pt = pb(c, "n3pt", [32, 8 * P])
            pt2 = pb(c, "n3pt2", [D, 8 * P])
            po = pb(c, "n3po", [P, GROUP, D])
            po2 = pb(c, "n3po2", [P, GROUP, D])
            chain, chain2, ready, turned, evicted, product, relued, turned2, evicted2, product2, summed, var, rooted, final, stored = [
                sem(c, "n3" + n) for n in ("chain", "chain2", "ready", "turned", "evicted", "product", "relued", "turned2",
                                           "evicted2", "product2", "summed", "var", "rooted", "final", "stored")]
            with nc.Block() as block:
                @block.gpsimd
                def _(pool):
                    skewed(pool, [(0, gather_part(pool, 32, idx, rows, copied, got, taken))])

                @block.vector
                def _(dve):
                    ch = Chain(dve, chain, 1)
                    ch2 = Chain(dve, chain2, LN_LINKS)

                    def front(g, i, k, first):
                        ch.group(g)
                        dve.wait_ge(got[k], (i + 1) * (16 * GROUP))
                        if not first:
                            dve.wait_ge(turned, g - 1)
                        ya = y[:, k, :, :]
                        TT(ya, rows[:, k, :, :], of_group(nonempty, g, 32), ALU.mult).then_inc(taken, 1)
                        dve.wait_ge(taken, g + 1)
                        ch(TT(ya, ya, rows_of_group(h32, g), ALU.add))
                        TT(ya, ya, of_group(dinv, g, 32), ALU.mult).then_inc(ready, 1)

                    def back(g, i, k, first):
                        dve.wait_ge(product2, g + 1)
                        TT(r[:], po2[:], rows_of_group(X, g), ALU.add).then_inc(summed, 1)
                        dve.wait_ge(summed, g + 1)
                        ch2.group(g)
                        layernorm(dve, ch2, var, rooted, g, r[:], sq[:], m[:], v[:], rv[:], rows_of_group(X, g), final)
                        dve.wait_ge(final, g + 1)
                    skewed(dve, [(0, front), (2, back)])

                @block.tensor
                def _(pe):
                    def turn(g, i, k, first):
                        pe.wait_ge(ready, g + 1)
                        if not first:
                            pe.wait_ge(evicted, g)
                        settled(pe)
                        turn_blocks(pt, y[:, k, :, :]).then_inc(turned, 1)

                    def turn_x4(g, i, k, first):
                        pe.wait_ge(relued, g + 1)
                        if not first:
                            pe.wait_ge(evicted2, g)
                        settled(pe)
                        turn_blocks(pt2, x4[:, k, :, :]).then_inc(turned2, 1)

                    def third_layer(g, i, k, first):
                        pe.wait_ge(evicted, g + 1)
                        if not first:
                            pe.wait_ge(relued, g)
                        for b in range(GROUP):
                            last = nc.tensor.matmul(po[:, b, :], lhs33[:, k, b * P:(b + 1) * P], w3a[:], start=True, stop=True)
                        last.then_inc(product, 1)

                    def mixed(g, i, k, first):
                        pe.wait_ge(evicted2, g + 1)
                        if not first:
                            pe.wait_ge(summed, g)
                        for b in range(GROUP):
                            last = nc.tensor.matmul(po2[:, b, :], x4t[:, k, b * P:(b + 1) * P], lw_low[:], start=True, stop=True)
                        last.then_inc(product2, 1)
                    skewed(pe, [(0, turn), (1, turn_x4), (0, third_layer), (1, mixed)], first_at=1)

                @block.scalar
                def _(act):
                    def take_turned(g, i, k, first):
                        act.wait_ge(turned, g + 1)
                        if not first:
                            act.wait_ge(product, g - 1)
                        nc.scalar.copy(lhs33[0:32, k, :], pt[:, 0:GROUP * P]).then_inc(evicted, 1)

                    def take_x4_turned(g, i, k, first):
                        act.wait_ge(turned2, g + 1)
                        if not first:
                            act.wait_ge(product2, g - 1)
                        nc.scalar.copy(x4t[:, k, :], pt2[:, 0:GROUP * P]).then_inc(evicted2, 1)

                    def relu(g, i, k, first):
                        act.wait_ge(product, g + 1)
                        if not first:
                            act.wait_ge(turned2, g - 1)
                        nc.scalar.activation(x4[:, k, :, :], po[:], ACT.Relu).then_inc(relued, 1)

                    def root_of(g, i, k, first):
                        layernorm_root(act, var, rooted, g, v[:], rv[:])
                    skewed(act, [(0, take_turned), (1, take_x4_turned), (0, relu), (2, root_of)])

                @block.sync
                def _(sp):
                    def part(g, i, k, first):
                        sp.wait_ge(final, g + 1)
                        sp.dma_start(rows_of(table64)[:, bass.ds(g * GROUP, GROUP), :], rows_of_group(X, g)).then_inc(stored, 16)
                    skewed(sp, [(0, part)])
                    sp.wait_ge(stored, 16 * NGROUPS)
        L0.close()

        edge_pass("p4", table64, D, 2 * D, squares=True)
        carry_stage("c4", 2 * D)
        with ExitStack() as c:
            idx, rows, copied, got, taken = node_tools(c, "n4", 2 * D)
            inv = sb(c, "n4inv", [P, NB])
            t = sb(c, "n4t", [P, 2, GROUP, 2 * D])
            mean_sq = sb(c, "n4mean_sq", [P, GROUP, D])
            dev = sb(c, "n4dev", [P, 2, GROUP, D])
            sq = sb(c, "n4sq", [P, GROUP, D])
            m = sb(c, "n4m", [P, GROUP])
            v = sb(c, "n4v", [P, GROUP])
            rv = sb(c, "n4rv", [P, GROUP])
            xs = sb(c, "n4xs", [P, 2, GROUP, D])
            xt = sb(c, "n4xt", [D, 2, GROUP * P])
            qs = sb(c, "n4qs", [P, 2, GROUP, D])
            p_s = sb(c, "n4ps", [P, 2, GROUP, D])
            sidx = sb(c, "n4sidx", [P, 2, GROUP], i32)
            bias_b = sb(c, "n4bias", [P, D])
            heads = sb(c, "heads", [QH, HALVES, QT * D])
            pt = pb(c, "n4pt", [D, 8 * P])
            po_q = pb(c, "n4po_q", [P, 8, D])
            po_p = pb(c, "n4po_p", [P, 8, D])
            pbias = pb(c, "n4pbias", [P, D])
            chain, chain2, var0, dev_ready, var, rooted, final, turned, evicted, product, q_out, p_out, kept, copied2 = [
                sem(c, "n4" + n) for n in ("chain", "chain2", "var0", "dev_ready", "var", "rooted", "final", "turned", "evicted",
                                           "product", "q_out", "p_out", "kept", "copied2")]
            made, bias_in = sem(c, "n4made"), sem(c, "n4bias_in")
            q_stored = [sem(c, f"n4q_stored{k}") for k in range(2)]
            p_stored = [sem(c, f"n4p_stored{k}") for k in range(2)]
            scattered = [sem(c, f"n4scattered{k}") for k in range(2)]
            head_got = sem(c, "head_got")
            head_put = sem(c, "head_put")
            with nc.Block() as block:
                @block.gpsimd
                def _(pool):
                    def scatter(g, i, k, first):
                        if not first:
                            pool.wait_ge(scattered[k], i * (16 * GROUP))
                        nc.gpsimd.tensor_copy(sidx[:, k, :], start_row[:, bass.ds(g * GROUP, GROUP)]).then_inc(copied2, 1)
                        pool.wait_ge(copied2, g + 1)
                        pool.wait_ge(p_out, g + 1)
                        settled(pool)
                        for u in range(GROUP):
                            nc.gpsimd.indirect_dma_start(node_at_edge, bass.IndirectOffsetOnAxis(sidx[:, k, u:u + 1], 0),
                                                         p_s[:, k, u, :], None).then_inc(scattered[k], 16)
                    skewed(pool, [(0, gather_part(pool, 2 * D, idx, rows, copied, got, taken)), (3, scatter)])
                    for k in range(2):
                        pool.wait_ge(p_stored[k], 16 * (NGROUPS // 2))
                    for h in range(2 * QT):
                        nc.gpsimd.indirect_dma_start(heads[:, h // QT, (h % QT) * D:(h % QT + 1) * D], None, table_p,
                                                     bass.IndirectOffsetOnAxis(first_dst[0:QH, h:h + 1], 0)).then_inc(head_got, 16)

                @block.vector
                def _(dve):
                    V.tensor_scalar_max(inv[:], count[:], COUNT_EPS).then_inc(made, 1)
                    dve.wait_ge(made, 1)
                    V.reciprocal(inv[:], inv[:]).then_inc(made, 1)
                    dve.wait_ge(made, 2)
                    TT(inv[:], inv[:], nonempty[:], ALU.mult).then_inc(made, 1)
                    dve.wait_ge(made, 3)
                    dve.wait_ge(bias_in, 1)
                    V.tensor_copy(bias_b[:], pbias[:]).then_inc(made, 1)
                    dve.wait_ge(made, 4)
                    ch = Chain(dve, chain, 2)
                    ch2 = Chain(dve, chain2, LN_LINKS + 2)

                    def front(g, i, k, first):
                        ch.group(g)
                        dve.wait_ge(got[k], (i + 1) * (16 * GROUP))
                        ta = t[:, k, :, :]
                        TT(ta, rows[:, k, :, :], of_group(inv, g, 2 * D), ALU.mult).then_inc(taken, 1)
                        dve.wait_ge(taken, g + 1)
                        ch(TT(mean_sq[:], ta[:, :, 0:D], ta[:, :, 0:D], ALU.mult))
                        ch(TT(mean_sq[:], ta[:, :, D:2 * D], mean_sq[:], ALU.subtract))
                        V.tensor_scalar_max(dev[:, k, :, :], mean_sq[:], 0.0).then_inc(var0, 1)
                        dve.wait_ge(var0, g + 1)

                    def back(g, i, k, first):
                        ch2.group(g)
                        dve.wait_ge(dev_ready, g + 1)
                        if not first:
                            dve.wait_ge(turned, g - 1)
                            dve.wait_ge(kept, g - 1)
                        y = dev[:, k, :, :]
                        ch2(TT(y, y, of_group(several, g, D), ALU.mult))
                        ch2(TT(y, y, rows_of_group(X, g), ALU.add))
                        layernorm(dve, ch2, var, rooted, g, y, sq[:], m[:], v[:], rv[:], xs[:, k, :, :], final)

                    def take_p(g, i, k, first):
                        dve.wait_ge(product, g + 1)
                        if not first:
                            dve.wait_ge(p_stored[k], i * 16)
                            dve.wait_ge(scattered[k], i * (16 * GROUP))
                        TT(p_s[:, k, :, :], po_p[:, 0:GROUP, :], every_block(bias_b, D), ALU.add).then_inc(p_out, 1)
                    skewed(dve, [(0, front), (2, take_p), (1, back)])

                @block.tensor
                def _(pe):
                    nc.tensor.matmul(pbias[:], ones[0:1, :], bias_sgn[:], start=True, stop=True).then_inc(bias_in, 1)

                    def part(g, i, k, first):
                        pe.wait_ge(final, g + 1)
                        if not first:
                            pe.wait_ge(evicted, g)
                        settled(pe)
                        turn_blocks(pt, xs[:, k, :, :]).then_inc(turned, 1)
                        pe.wait_ge(evicted, g + 1)
                        if not first:
                            pe.wait_ge(q_out, g)
                            pe.wait_ge(p_out, g)
                        for b in range(GROUP):
                            nc.tensor.matmul(po_q[:, b, :], xt[:, k, b * P:(b + 1) * P], w_qp[:, 0:D], start=True, stop=True)
                            last = nc.tensor.matmul(po_p[:, b, :], xt[:, k, b * P:(b + 1) * P], w_qp[:, D:2 * D], start=True, stop=True)
                        last.then_inc(product, 1)
                    skewed(pe, [(0, part)], first_at=1)

                @block.scalar
                def _(act):
                    def front(g, i, k, first):
                        act.wait_ge(var0, g + 1)
                        nc.scalar.sqrt(dev[:, k, :, :], dev[:, k, :, :]).then_inc(dev_ready, 1)

                    def back(g, i, k, first):
                        layernorm_root(act, var, rooted, g, v[:], rv[:])
                        act.wait_ge(turned, g + 1)
                        if not first:
                            act.wait_ge(product, g - 1)
                        nc.scalar.copy(xt[:, k, :], pt[:, 0:GROUP * P]).then_inc(evicted, 1)
                        act.wait_ge(final, g + 1)
                        nc.scalar.copy(rows_of_group(X, g), xs[:, k, :, :]).then_inc(kept, 1)

                    def take_q(g, i, k, first):
                        act.wait_ge(product, g + 1)
                        if not first:
                            act.wait_ge(q_stored[k], i * 16)
                        nc.scalar.copy(qs[:, k, :, :], po_q[:, 0:GROUP, :]).then_inc(q_out, 1)
                    skewed(act, [(0, front), (2, take_q), (1, back)])

                @block.sync
                def _(sp):
                    def part(g, i, k, first):
                        sp.wait_ge(q_out, g + 1)
                        sp.dma_start(rows_of(table_q)[:, bass.ds(g * GROUP, GROUP), :], qs[:, k, :, :]).then_inc(q_stored[k], 16)
                        sp.wait_ge(p_out, g + 1)
                        sp.dma_start(rows_of(table_p)[:, bass.ds(g * GROUP, GROUP), :], p_s[:, k, :, :]).then_inc(p_stored[k], 16)
                    skewed(sp, [(0, part)])
                    for k in range(2):
                        sp.wait_ge(q_stored[k], 16 * (NGROUPS // 2))
                        sp.wait_ge(scattered[k], (NGROUPS // 2) * 16 * GROUP)
                    sp.wait_ge(head_got, 16 * 2 * QT)
                    hv = node_at_edge[0:EPAD, :].rearrange("(h q e j) w -> q h e (j w)", h=HALVES, q=QH, e=P)
                    for h in range(HALVES):
                        sp.dma_start(hv[:, h, 0, :], heads[:, h, :]).then_inc(head_put, 16)
                    sp.wait_ge(head_put, 32)

        stat_ctx = ExitStack()
        scale_b = sb(stat_ctx, "scale_b", [P, D])
        shift_b = sb(stat_ctx, "shift_b", [P, D])
        with ExitStack() as c:
            idx = sb(c, "e_idx", [P, SLOTS, QT], i32)
            spread = sb(c, "spread", [P, SLOTS, QT, P])
            msg = sb(c, "e_msg", [P, SLOTS, QT, D])
            at_edge = sb(c, "at_edge", [P, SLOTS, QT, D])
            hid = sb(c, "hid", [P, SLOTS, QT, D])
            hid_sq = sb(c, "hid_sq", [P, SLOTS, QT, D])
            acc = [pb(c, f"e_acc{k}", [P, QT * D]) for k in range(2)]
            moment = [pb(c, f"moment{k}", [1, QT * D]) for k in range(2)]
            got = [sem(c, f"e_got{k}") for k in range(SLOTS)]
            loaded = [sem(c, f"e_loaded{k}") for k in range(SLOTS)]
            stored = [sem(c, f"e_stored{k}") for k in range(SLOTS)]
            idx_ready = sem(c, "e_idx_ready")
            matrix_ready = sem(c, "e_matrix_ready")
            spread_done = sem(c, "e_spread_done")
            hid_ready = sem(c, "e_hid_ready")
            sq_ready = sem(c, "e_sq_ready")
            moments_done = sem(c, "e_moments_done")
            iters = NQ // SLOTS
            in_b = batches_of(node_at_edge[0:EPAD, :])
            out_b = batches_of(messages)
            last_tiles = [min(P, max(0, N_EDGES - ((NQ - 1) * EB + u * P))) for u in range(QT)]
            with nc.Block() as block:
                @block.gpsimd
                def _(pool):
                    def step(i, first):
                        for k in range(SLOTS):
                            pool.wait_ge(idx_ready, i * SLOTS + k + 1)
                            if not first:
                                pool.wait_ge(hid_ready, (i - 1) * SLOTS + k + 1)
                            settled(pool)
                            for u in range(QT):
                                nc.gpsimd.indirect_dma_start(msg[:, k, u, :], None, table_q,
                                                             bass.IndirectOffsetOnAxis(idx[:, k, u:u + 1], 0)).then_inc(got[k], 16)
                    step(0, True)
                    with pool.Fori(1, iters) as i:
                        step(i, False)

                @block.sync
                def _(sp):
                    for k in range(2):
                        sp.dma_start(at_edge[:, k, :, :].rearrange("p j d -> p (j d)"), in_b[k]).then_inc(loaded[k], 16)

                    def step(i, first, final):
                        for k in range(SLOTS):
                            ahead = (k + 2) % SLOTS
                            if not (final and k >= 2):
                                if not (first and k < 2):
                                    sp.wait_ge(spread_done, i * SLOTS + k - 1)
                                sp.dma_start(at_edge[:, ahead, :, :].rearrange("p j d -> p (j d)"), in_b[i * SLOTS + k + 2]).then_inc(loaded[ahead], 16)
                            sp.wait_ge(hid_ready, i * SLOTS + k + 1)
                            sp.dma_start(out_b[i * SLOTS + k], hid[:, k, :, :].rearrange("p j d -> p (j d)")).then_inc(stored[k], 16)
                    step(0, True, False)
                    with sp.Fori(1, iters - 1) as i:
                        step(i, False, False)
                    step(iters - 1, False, True)
                    for k in range(SLOTS):
                        sp.wait_ge(stored[k], iters * 16)

                @block.scalar
                def _(act):
                    for k in range(2):
                        nc.scalar.copy(idx[:, k, :], src_idx[:, k * QT:(k + 1) * QT]).then_inc(idx_ready, 1)

                    def step(i, first):
                        for k in range(SLOTS):
                            ahead = (k + 2) % SLOTS
                            if not (first and k < 2):
                                act.wait_ge(got[ahead], (i if k < 2 else i + 1) * (16 * QT))
                            nc.scalar.copy(idx[:, ahead, :], src_idx[:, bass.ds((i * SLOTS + k + 2) * QT, QT)]).then_inc(idx_ready, 1)
                            act.wait_ge(hid_ready, i * SLOTS + k + 1)
                            if not first:
                                act.wait_ge(moments_done, (i - 1) * SLOTS + k + 1)
                            nc.scalar.square(hid_sq[:, k, :, :], hid[:, k, :, :]).then_inc(sq_ready, 1)
                    step(0, True)
                    with act.Fori(1, iters) as i:
                        step(i, False)

                @block.vector
                def _(dve):
                    def step(i, first):
                        for k in range(SLOTS):
                            if not first:
                                dve.wait_ge(spread_done, (i - 1) * SLOTS + k + 1)
                            for u in range(QT):
                                t = i * (SLOTS * QT) + k * QT + u
                                last = nc.vector.tensor_scalar(spread[:, k, u, :], iota_upper[:], seg_end_first[:, bass.ds(t, 1)], None, ALU.is_le)
                            last.then_inc(matrix_ready, 1)
                            dve.wait_ge(spread_done, i * SLOTS + k + 1)
                            dve.wait_ge(got[k], (i + 1) * (16 * QT))
                            if not first:
                                dve.wait_ge(stored[k], i * 16)
                                dve.wait_ge(moments_done, (i - 1) * SLOTS + k + 1)
                            nc.vector.tensor_tensor(hid[:, k, :, :].rearrange("p j d -> p (j d)"), acc[k % 2][:],
                                                    msg[:, k, :, :].rearrange("p j d -> p (j d)"), ALU.add).then_inc(hid_ready, 1)
                    step(0, True)
                    with dve.Fori(1, iters) as i:
                        step(i, False)

                @block.tensor
                def _(pe):
                    def step(i, first, final):
                        for k in range(SLOTS):
                            pe.wait_ge(matrix_ready, i * SLOTS + k + 1)
                            pe.wait_ge(loaded[k], (i + 1) * 16)
                            if not (first and k < 2):
                                pe.wait_ge(hid_ready, i * SLOTS + k - 1)
                            for u in range(QT):
                                last = nc.tensor.matmul(acc[k % 2][:, u * D:(u + 1) * D], spread[:, k, u, :], at_edge[:, k, u, :], start=True, stop=True)
                            last.then_inc(spread_done, 1)
                            pe.wait_ge(sq_ready, i * SLOTS + k + 1)
                            begin = first and k == 0
                            if final and k == SLOTS - 1:
                                for m_ps, a in ((moment[0], hid), (moment[1], hid_sq)):
                                    for u in range(QT):
                                        n = last_tiles[u]
                                        if n:
                                            stop = u == QT - 1 or not last_tiles[u + 1]
                                            last = nc.tensor.matmul(m_ps[:, u * D:(u + 1) * D], ones[0:n, 0:1], a[0:n, k, u, :], start=False, stop=stop)
                            else:
                                for m_ps, a in ((moment[0], hid), (moment[1], hid_sq)):
                                    last = nc.tensor.matmul(m_ps[:], ones[:, 0:1], a[:, k, :, :].rearrange("p j d -> p (j d)"), start=begin, stop=False)
                            last.then_inc(moments_done, 1)
                    step(0, True, False)
                    with pe.Fori(1, iters - 1) as i:
                        step(i, False, False)
                    step(iters - 1, False, True)

            mu = sb(c, "mu", [1, D])
            va = sb(c, "va", [1, D])
            tq = sb(c, "tq", [1, D])
            bc = pb(c, "bc", [P, 2, D])
            tb = sb(c, "tb", [1, D])
            stat_step = sem(c, "stat_step")
            var_ready = sem(c, "bn_var_ready")
            root_ready = sem(c, "bn_root_ready")
            rows_ready = sem(c, "bn_rows_ready")
            spread_out = sem(c, "bn_spread_out")
            spread_kept = sem(c, "bn_spread_kept")
            with nc.Block() as block:
                @block.vector
                def _(dve):
                    link = chain_of(dve, stat_step)
                    link(V.reduce_sum(mu[:], moment[0][:].rearrange("p (j d) -> p d j", j=QT), AX.X))
                    link(V.reduce_sum(va[:], moment[1][:].rearrange("p (j d) -> p d j", j=QT), AX.X))
                    link(V.tensor_scalar_mul(mu[:], mu[:], 1.0 / N_EDGES))
                    link(TT(tq[:], mu[:], mu[:], ALU.mult))
                    link(V.scalar_tensor_tensor(va[:], va[:], 1.0 / N_EDGES, tq[:], ALU.mult, ALU.subtract))
                    V.tensor_scalar(va[:], va[:], 0.0, BN_EPS, ALU.max, ALU.add).then_inc(var_ready, 1)
                    dve.wait_ge(root_ready, 1)
                    link(V.reciprocal(tq[:], va[:]))
                    link(V.tensor_scalar_mul(va[:], gamma[:], -1.0))
                    link(TT(va[:], va[:], gamma[:], ALU.max))
                    link(TT(tq[:], tq[:], va[:], ALU.mult))
                    link(V.tensor_scalar_max(tq[:], tq[:], 1e-20))
                    link(V.reciprocal(va[:], tq[:]))
                    link(TT(tb[:], beta[:], va[:], ALU.mult))
                    TT(mu[:], tb[:], mu[:], ALU.subtract).then_inc(rows_ready, 1)
                    dve.wait_ge(spread_out, 1)
                    V.tensor_copy(scale_b[:], bc[:, 0, :]).then_inc(spread_kept, 1)
                    V.tensor_copy(shift_b[:], bc[:, 1, :]).then_inc(spread_kept, 1)

                @block.scalar
                def _(act):
                    act.wait_ge(var_ready, 1)
                    nc.scalar.sqrt(va[:], va[:]).then_inc(root_ready, 1)

                @block.tensor
                def _(pe):
                    pe.wait_ge(rows_ready, 1)
                    nc.tensor.matmul(bc[:, 0, :], ones[0:1, :], tq[:], start=True, stop=True)
                    nc.tensor.matmul(bc[:, 1, :], ones[0:1, :], mu[:], start=True, stop=True).then_inc(spread_out, 1)

        with ExitStack() as c:
            seg = sb(c, "f_seg", [P, SWEEP_SLOTS, QT, P], bf16)
            hid = sb(c, "f_hid", [P, SWEEP_SLOTS, QT * D])
            moved = sb(c, "f_moved", [P, SWEEP_SLOTS, QT * D])
            act_h = sb(c, "f_act", [P, SWEEP_SLOTS, QT * D])
            parts = [sb(c, f"f_part{m}", [P, SWEEP_SLOTS, QT * D], bf16) for m in range(3)]
            summed = sb(c, "f_sum", [P, SWEEP_SLOTS, QT * D])
            acc = [pb(c, f"f_acc{k}", [P, QT * D]) for k in range(SWEEP_SLOTS)]
            loaded = [sem(c, f"f_loaded{k}") for k in range(SWEEP_SLOTS)]
            stored = [sem(c, f"f_stored{k}") for k in range(SWEEP_SLOTS)]
            matrix_ready = sem(c, "f_matrix_ready")
            moved_ready = sem(c, "f_moved_ready")
            leaky_ready = sem(c, "f_leaky_ready")
            high_ready = sem(c, "f_high_ready")
            rest_ready = sem(c, "f_rest_ready")
            middle_ready = sem(c, "f_middle_ready")
            low_ready = sem(c, "f_low_ready")
            product_done = sem(c, "f_product_done")
            evicted = sem(c, "f_evicted")
            in_b = batches_of(messages)
            out_b = batches_of(prefix[D])

            def over_batches(engine, work):
                skewed(engine, work, first_at=SWEEP_SLOTS, total=NQ, unrolled=SWEEP_SLOTS)
            with nc.Block() as block:
                @block.sync
                def _(sp):
                    def load(n, i, k, first):
                        if not first:
                            sp.wait_ge(moved_ready, n - SWEEP_SLOTS + 1)
                        sp.dma_start(hid[:, k, :], in_b[n]).then_inc(loaded[k], 16)

                    def store(n, i, k, first):
                        sp.wait_ge(evicted, n + 1)
                        sp.dma_start(out_b[n], summed[:, k, :]).then_inc(stored[k], 16)
                    over_batches(sp, [(0, load), (SWEEP_SLOTS, store)])
                    for k in range(SWEEP_SLOTS):
                        sp.wait_ge(stored[k], (NQ // SWEEP_SLOTS) * 16)

                @block.gpsimd
                def _(pool):
                    def move(n, i, k, first):
                        pool.wait_ge(loaded[k], (i + 1) * 16)
                        if not first:
                            pool.wait_ge(low_ready, n - SWEEP_SLOTS + 1)
                        nc.gpsimd.tensor_tensor(moved[:, k, :].rearrange("p (j d) -> p j d", d=D), hid[:, k, :].rearrange("p (j d) -> p j d", d=D),
                                                shift_b[:, None, :].to_broadcast([P, QT, D]), ALU.add).then_inc(moved_ready, 1)

                    def rest(n, i, k, first):
                        pool.wait_ge(high_ready, n + 1)
                        nc.gpsimd.tensor_tensor(moved[:, k, :], act_h[:, k, :], parts[0][:, k, :], ALU.subtract).then_inc(rest_ready, 1)
                    over_batches(pool, [(0, move), (1, rest)])

                @block.scalar
                def _(act):
                    def high(n, i, k, first):
                        act.wait_ge(leaky_ready, n + 1)
                        if not first:
                            act.wait_ge(product_done, n - SWEEP_SLOTS + 1)
                        nc.scalar.copy(parts[0][:, k, :], act_h[:, k, :]).then_inc(high_ready, 1)

                    def middle(n, i, k, first):
                        act.wait_ge(rest_ready, n + 1)
                        if not first:
                            act.wait_ge(product_done, n - SWEEP_SLOTS + 1)
                        nc.scalar.copy(parts[1][:, k, :], moved[:, k, :]).then_inc(middle_ready, 1)

                    def take(n, i, k, first):
                        act.wait_ge(product_done, n + 1)
                        if not first:
                            act.wait_ge(stored[k], i * 16)
                        nc.scalar.copy(summed[:, k, :], acc[k][:]).then_inc(evicted, 1)
                    over_batches(act, [(0, high), (1, middle), (3, take)])

                @block.vector
                def _(dve):
                    def matrix(n, i, k, first):
                        if not first:
                            dve.wait_ge(product_done, n - SWEEP_SLOTS + 1)
                        TT(seg[:, k, :, :], iota_upper[:, None, :].to_broadcast([P, QT, P]),
                           seg_end[:, bass.ds(n * QT, QT)][:, :, None].to_broadcast([P, QT, P]), ALU.is_le).then_inc(matrix_ready, 1)

                    def leaky(n, i, k, first):
                        dve.wait_ge(moved_ready, n + 1)
                        if not first:
                            dve.wait_ge(rest_ready, n - SWEEP_SLOTS + 1)
                        V.scalar_tensor_tensor(act_h[:, k, :], moved[:, k, :], SLOPE, moved[:, k, :], ALU.mult, ALU.max).then_inc(leaky_ready, 1)

                    def low(n, i, k, first):
                        dve.wait_ge(middle_ready, n + 1)
                        if not first:
                            dve.wait_ge(product_done, n - SWEEP_SLOTS + 1)
                        TT(parts[2][:, k, :], moved[:, k, :], parts[1][:, k, :], ALU.subtract).then_inc(low_ready, 1)
                    over_batches(dve, [(0, leaky), (0, matrix), (2, low)])

                @block.tensor
                def _(pe):
                    def add_up(n, i, k, first):
                        pe.wait_ge(matrix_ready, n + 1)
                        pe.wait_ge(high_ready, n + 1)
                        pe.wait_ge(middle_ready, n + 1)
                        pe.wait_ge(low_ready, n + 1)
                        if not first:
                            pe.wait_ge(evicted, n - SWEEP_SLOTS + 1)
                        for u in range(QT):
                            for m in range(3):
                                last = nc.tensor.matmul(acc[k][:, u * D:(u + 1) * D], seg[:, k, u, :],
                                                        parts[m][:, k, u * D:(u + 1) * D], start=m == 0, stop=m == 2)
                        last.then_inc(product_done, 1)
                    over_batches(pe, [(0, add_up)])
        carry_stage("c5", D)

        with ExitStack() as c:
            idx, rows, copied, got, taken = node_tools(c, "n5", D)
            inv = sb(c, "n5inv", [P, NB])
            inv_rel = sb(c, "n5inv_rel", [P, NB])
            some = sb(c, "n5some", [P, NB])
            y = sb(c, "n5y", [P, GROUP, D])
            y2 = sb(c, "n5y2", [P, 2, GROUP, D])
            sq = sb(c, "n5sq", [P, GROUP, D])
            m = sb(c, "n5m", [P, GROUP])
            v = sb(c, "n5v", [P, GROUP])
            rv = sb(c, "n5rv", [P, GROUP])
            v_b = sb(c, "n5v_b", [P, GROUP])
            rv_b = sb(c, "n5rv_b", [P, GROUP])
            prod = sb(c, "n5prod", [P, 2, 2 * R, D])
            halved = sb(c, "n5halved", [P, 2, R, D])
            outs = sb(c, "n5outs", [P, 2, GROUP, D])
            group_counts = sb(c, "n5counts", [P, 2, GROUP, 2 * R])
            THIRD = 2 * R // 3
            pairs = [sb(c, f"n5pair{m}", [P, 2, GROUP, 2 * D], bf16) for m in range(2)]
            pairs_t = [sb(c, f"n5pair_t{m}", [2 * D, 2, GROUP * P], bf16) for m in range(2)]
            remainder = sb(c, "n5remainder", [P, GROUP, D])
            low_t = sb(c, "n5low_t", [D + 3, 2, GROUP * P], bf16)
            w_parts = [sb(c, f"n5w_part{m}", [2 * D, 2 * R * D], bf16) for m in range(3)]
            w_mixed = sb(c, "n5w_mixed", [2 * D, 2 * R * D], bf16)
            w_low = sb(c, "n5w_low", [D + 3, 2 * R * D], bf16)
            w_left = sb(c, "n5w_left", [2 * D, 2 * R * D])
            b_rel = sb(c, "b_rel", [D + 3, 2 * R * D])
            b_left = sb(c, "n5b_left", [D + 3, 2 * R * D])
            b_part = sb(c, "n5b_part", [D + 3, 2 * R * D], bf16)
            ident_b = sb(c, "n5ident_b", [P, P], bf16)
            pt = [pb(c, f"n5pt{m}", [2 * D, 8 * P], bf16) for m in range(2)]
            po = [pb(c, f"n5po{k}", [P, 3, 512]) for k in range(2)]
            chain, chain3, var, rooted, final, var_b, rooted_b, turned, evicted, product, mult_v, mult_a, added, relations = [
                sem(c, "n5" + n) for n in ("chain", "chain3", "var", "rooted", "final", "var_b", "rooted_b", "turned",
                                           "evicted", "product", "mult_v", "mult_a", "added", "relations")]
            made = sem(c, "n5made")
            bias_loaded = sem(c, "n5bias_loaded")
            w_split = sem(c, "n5w_split")
            high_split = sem(c, "n5high_split")
            left_ready = sem(c, "n5left_ready")
            middle_split = sem(c, "n5middle_split")
            low_split = sem(c, "n5low_split")
            counted = sem(c, "n5counted")
            final_b = sem(c, "n5final_b")
            out_stored = [sem(c, f"n5out_stored{k}") for k in range(2)]
            with nc.Block() as block:
                @block.gpsimd
                def _(pool):
                    def step(gather, normed, turning, related, last):
                        if gather:
                            g, i, k, first = gather
                            if not first:
                                pool.wait_ge(taken, g - 1)
                            nc.gpsimd.tensor_copy(idx[:, k, :], end_row[:, bass.ds(g * GROUP, GROUP)]).then_inc(copied, 1)
                            pool.wait_ge(copied, g + 1)
                        for b in range(GROUP):
                            if gather:
                                g, i, k, first = gather
                                settled(pool)
                                nc.gpsimd.indirect_dma_start(rows[:, k, b, :], None, prefix[D],
                                                             bass.IndirectOffsetOnAxis(idx[:, k, b:b + 1], 0)).then_inc(got[k], 16)
                            if related:
                                g, i, k, first = related
                                s = (k + b) % 2
                                n = g * GROUP + b
                                pool.wait_ge(mult_v, n + 1)
                                pool.wait_ge(mult_a, n + 1)
                                if not (isinstance(g, int) and g == 0 and b < 2):
                                    pool.wait_ge(relations, n - 1)
                                nc.gpsimd.tensor_tensor(halved[:, s, :, :], prod[:, s, 0:R, :], prod[:, s, R:2 * R, :], ALU.add).then_inc(added, 1)
                        if normed:
                            g, i, k, first = normed
                            pool.wait_ge(middle_split, g + 1)
                            if not first:
                                pool.wait_ge(turned, g - 1)
                            nc.gpsimd.tensor_tensor(pairs[1][:, k, :, :].rearrange("p b (a d) -> p b a d", a=2),
                                                    remainder[:, :, None, :].to_broadcast([P, GROUP, 2, D]),
                                                    pairs[0][:, k, :, D:2 * D][:, :, None, :].to_broadcast([P, GROUP, 2, D]),
                                                    ALU.subtract).then_inc(low_split, 1)
                    together(pool, 4, step)

                @block.vector
                def _(dve):
                    mk = chain_of(dve, made)
                    mk(V.tensor_scalar_max(inv[:], count[:], 1.0))
                    mk(V.reciprocal(inv[:], inv[:]))
                    mk(TT(inv[:], inv[:], nonempty[:], ALU.mult))
                    mk(V.reduce_sum(inv_rel[:], counts[:], AX.X))
                    mk(V.tensor_single_scalar(some[:], inv_rel[:], 0.0, ALU.is_gt))
                    mk(V.tensor_scalar_max(inv_rel[:], inv_rel[:], 1.0))
                    mk(V.reciprocal(inv_rel[:], inv_rel[:]))
                    mk(TT(inv_rel[:], inv_rel[:], some[:], ALU.mult))
                    ch = Chain(dve, chain, 2 + LN_LINKS)
                    ch3 = Chain(dve, chain3, 2 + LN_LINKS)
                    ws = chain_of(dve, w_split)
                    ws(V.tensor_copy(ident_b[:], ident[:]))
                    ws(V.memset(low_t[D:D + 3, :, :], 1.0))
                    ws(V.tensor_copy(w_parts[0][:], w_rel[:]))
                    ws(TT(w_left[:], w_rel[:], w_parts[0][:], ALU.subtract))
                    ws(V.tensor_copy(w_parts[1][:], w_left[:]))
                    ws(TT(w_parts[2][:], w_left[:], w_parts[1][:], ALU.subtract))
                    ws(V.tensor_copy(w_mixed[0:D, :], w_parts[0][0:D, :]))
                    ws(V.tensor_copy(w_mixed[D:2 * D, :], w_parts[1][D:2 * D, :]))
                    ws(V.tensor_copy(w_low[0:D, :], w_parts[2][0:D, :]))
                    dve.wait_ge(bias_loaded, 16)
                    b = slice(D, D + 3)
                    ws(V.tensor_copy(b_part[b, :], b_rel[b, :]))
                    ws(V.tensor_scalar(w_low[b, :], b_part[b, :], ident[b, D:D + 1], None, ALU.mult))
                    ws(TT(b_left[b, :], b_rel[b, :], b_part[b, :], ALU.subtract))
                    ws(V.tensor_copy(b_part[b, :], b_left[b, :]))
                    ws(V.scalar_tensor_tensor(w_low[b, :], b_part[b, :], ident[b, D + 1:D + 2], w_low[b, :], ALU.mult, ALU.add))
                    ws(TT(b_left[b, :], b_left[b, :], b_part[b, :], ALU.subtract))
                    ws(V.scalar_tensor_tensor(w_low[b, :], b_left[b, :], ident[b, D + 2:D + 3], w_low[b, :], ALU.mult, ALU.add))

                    def mean_part(g, i, k, first):
                        ch.group(g)
                        dve.wait_ge(got[k], (i + 1) * (16 * GROUP))
                        TT(y[:], rows[:, k, :, :], of_group(inv, g, D), ALU.mult).then_inc(taken, 1)
                        dve.wait_ge(taken, g + 1)
                        ch(TT(y[:], y[:], every_block(scale_b, D), ALU.mult))
                        ch(TT(y[:], y[:], rows_of_group(X, g), ALU.add))

                    def relation_mean(g, i, k, first):
                        ch3.group(g)
                        dve.wait_ge(relations, (g + 1) * GROUP)
                        ya = y2[:, k, :, :]
                        ch3(TT(ya, ya, of_group(inv_rel, g, D), ALU.mult))
                        ch3(TT(ya, ya, rows_of_group(X, g), ALU.add))

                    def reduce(g, k, b):
                        dve.wait_ge(added, g * GROUP + b + 1)
                        V.reduce_sum(y2[:, k, b, :], halved[:, (k + b) % 2, :, :].rearrange("p r o -> p o r"), AX.X).then_inc(relations, 1)

                    def step(gather, normed, turning, related, last):
                        for b in range(GROUP):
                            if related:
                                g, i, k, first = related
                                s = (k + b) % 2
                                n = g * GROUP + b
                                dve.wait_ge(product, n + 1)
                                if not (isinstance(g, int) and g == 0 and b < 2):
                                    dve.wait_ge(added, n - 1)
                                TT(prod[:, s, 0:2 * THIRD, :].rearrange("p (a r) o -> p a r o", a=2),
                                   po[s][:, 0:2, 0:THIRD * D].rearrange("p a (r o) -> p a r o", o=D),
                                   counts[:, bass.ds(n, 1), 0:2 * THIRD].rearrange("p z (a r) -> p (z a) r", a=2)[:, :, :, None].to_broadcast([P, 2, THIRD, D]),
                                   ALU.mult).then_inc(mult_v, 1)
                            if normed:
                                g, i, k, first = normed
                                if b == 0:
                                    mean_part(g, i, k, first)
                                if b == 1:
                                    layernorm_center(ch, y[:], m[:])
                                if b == 2:
                                    layernorm_var(ch, var, y[:], sq[:], v[:])
                            if last:
                                g, i, k, first = last
                                if b == 3:
                                    relation_mean(g, i, k, first)
                            if normed:
                                g, i, k, first = normed
                                if b == 3:
                                    layernorm_scale(dve, ch, rooted, g, y[:], m[:], rv[:], rows_of_group(X, g), final)
                                    dve.wait_ge(final, g + 1)
                            if last:
                                g, i, k, first = last
                                if b == 4:
                                    layernorm_center(ch3, y2[:, k, :, :], m[:])
                            if normed and b == 5:
                                g, i, k, first = normed
                                dve.wait_ge(high_split, g + 1)
                                if not (isinstance(g, int) and g == 0):
                                    dve.wait_ge(low_split, g)
                                TT(remainder[:], rows_of_group(X, g), pairs[0][:, k, :, 0:D], ALU.subtract).then_inc(left_ready, 1)
                            if last:
                                g, i, k, first = last
                                if b == 5:
                                    layernorm_var(ch3, var_b, y2[:, k, :, :], sq[:], v_b[:])
                                if b == 6:
                                    if not first:
                                        dve.wait_ge(out_stored[k], i * 16)
                                    layernorm_scale(dve, ch3, rooted_b, g, y2[:, k, :, :], m[:], rv_b[:], outs[:, k, :, :], final_b)
                                    dve.wait_ge(final_b, g + 1)
                            if related and b > 0:
                                reduce(related[0], related[2], b - 1)
                        if related:
                            reduce(related[0], related[2], GROUP - 1)
                    together(dve, 4, step)

                @block.tensor
                def _(pe):
                    def step(gather, normed, turning, related, last):
                        for b in range(GROUP):
                            if related:
                                g, i, k, first = related
                                s = (k + b) % 2
                                n = g * GROUP + b
                                if b == 0:
                                    pe.wait_ge(evicted, g + 1)
                                if not (isinstance(g, int) and g == 0 and b < 2):
                                    pe.wait_ge(mult_v, n - 1)
                                    pe.wait_ge(mult_a, n - 1)
                                nodes = slice(b * P, (b + 1) * P)
                                factors = [(pairs_t[0][:, k, nodes], w) for w in w_parts]
                                factors += [(pairs_t[1][:, k, nodes], w_mixed), (low_t[:, k, nodes], w_low)]
                                for m, (rows_t, w) in enumerate(factors):
                                    for a in range(3):
                                        done = nc.tensor.matmul(po[s][:, a, 0:THIRD * D], rows_t, w[:, a * THIRD * D:(a + 1) * THIRD * D],
                                                                start=m == 0, stop=m == len(factors) - 1)
                                done.then_inc(product, 1)
                            if turning and b == 1:
                                g, i, k, first = turning
                                pe.wait_ge(low_split, g + 1)
                                if not (isinstance(g, int) and g == 0):
                                    pe.wait_ge(evicted, g)
                                settled(pe)
                                for m in range(2):
                                    for u in range(GROUP):
                                        done = nc.tensor.transpose(pt[m][:, u * P:(u + 1) * P], pairs[m][:, k, u, :], ident_b[:])
                                done.then_inc(turned, 1)
                    pe.wait_ge(w_split, 16)
                    together(pe, 4, step)

                @block.scalar
                def _(act):
                    def step(gather, normed, turning, related, last):
                        for b in range(GROUP):
                            if related:
                                g, i, k, first = related
                                s = (k + b) % 2
                                n = g * GROUP + b
                                if b == 0:
                                    act.wait_ge(counted, g + 1)
                                act.wait_ge(product, n + 1)
                                if not (isinstance(g, int) and g == 0 and b < 2):
                                    act.wait_ge(added, n - 1)
                                for r in range(THIRD):
                                    done = nc.scalar.activation(prod[:, s, 2 * THIRD + r, :], po[s][:, 2, r * D:(r + 1) * D], ACT.Copy,
                                                                scale=group_counts[:, k, b, 2 * THIRD + r:2 * THIRD + r + 1])
                                done.then_inc(mult_a, 1)
                            if turning and b == 2:
                                g, i, k, first = turning
                                act.wait_ge(turned, g + 1)
                                if not first:
                                    act.wait_ge(product, (g - 1) * GROUP)
                                    act.wait_ge(mult_a, (g - 1) * GROUP)
                                nc.scalar.copy(pairs_t[0][:, k, :], pt[0][:, 0:GROUP * P])
                                nc.scalar.copy(pairs_t[1][:, k, :], pt[1][:, 0:GROUP * P])
                                nc.scalar.copy(low_t[0:D, k, :], pt[1][0:D, 0:GROUP * P]).then_inc(evicted, 1)
                                nc.scalar.copy(group_counts[:, k, :, :], rows_of_group(counts, g)).then_inc(counted, 1)
                            if normed and b == 2:
                                layernorm_root(act, var, rooted, normed[0], v[:], rv[:])
                            if normed and b == 4:
                                g, i, k, first = normed
                                act.wait_ge(final, g + 1)
                                if not first:
                                    act.wait_ge(turned, g - 1)
                                nc.scalar.copy(pairs[0][:, k, :, 0:D], rows_of_group(X, g)).then_inc(high_split, 1)
                            if normed and b == 6:
                                g, i, k, first = normed
                                act.wait_ge(left_ready, g + 1)
                                nc.scalar.copy(pairs[0][:, k, :, D:2 * D], remainder[:]).then_inc(middle_split, 1)
                            if last and b == 5:
                                layernorm_root(act, var_b, rooted_b, last[0], v_b[:], rv_b[:])
                    together(act, 4, step)

                @block.sync
                def _(sp):
                    sp.dma_start(b_rel[D:D + 3, :], ins["L3_gnn_biases"][2:3].rearrange("z r o -> z (r o)").to_broadcast([3, 2 * R * D])).then_inc(bias_loaded, 16)

                    def part(g, i, k, first):
                        sp.wait_ge(final_b, g + 1)
                        if isinstance(g, int) and g == NGROUPS - 1:
                            h0 = g * GROUP
                            sp.dma_start(out[h0 * P:(NB - 1) * P, :].rearrange("(h l) d -> l h d", l=P), outs[:, k, 0:GROUP - 1, :]).then_inc(out_stored[k], 16)
                            sp.dma_start(out[(NB - 1) * P:N_NODES, :], outs[0:N_NODES - (NB - 1) * P, k, GROUP - 1, :]).then_inc(out_stored[k], 16)
                        else:
                            sp.dma_start(rows_of(out[0:(NB - 1) * P, :])[:, bass.ds(g * GROUP, GROUP), :], outs[:, k, :, :]).then_inc(out_stored[k], 16)
                    for g in range(2):
                        part(g, 0, g, True)
                    with sp.Fori(1, NGROUPS // 2 - 1) as i:
                        for k in range(2):
                            part(2 * i + k, i, k, False)
                    for g in (NGROUPS - 2, NGROUPS - 1):
                        part(g, g // 2, g % 2, False)
                    sp.wait_ge(out_stored[0], 16 * (NGROUPS // 2))
                    sp.wait_ge(out_stored[1], 16 * (NGROUPS // 2 + 1))
        stat_ctx.close()


_INS = ["x", "src", "dst", "edge_type_9", "edge_weight", "L0_gnn_w1", "L0_gnn_b1", "L0_gnn_w2", "L0_gnn_b2", "L0_gnn_w3",
        "L0_gnn_b3", "L0_gnn_lw", "L0_gnn_lb", "L2_gnn_W", "L2_gnn_b", "L2_gnn_gamma", "L2_gnn_beta", "L3_gnn_weights",
        "L3_gnn_biases"]


def kernel(**inputs):
    import numpy as np
    import concourse.bacc as bacc
    from concourse.bass_utils import run_bass_kernel_spmd

    nc = bacc.Bacc("TRN2", target_bir_lowering=False, num_devices=1)
    arrays, args = {}, {}
    for name in _INS:
        a = np.ascontiguousarray(inputs[name])
        arrays[f"in_{name}"] = a
        args[name] = nc.dram_tensor(f"in_{name}", a.shape, mybir.dt.from_np(a.dtype), kind="ExternalInput").ap()
    out = nc.dram_tensor("out_0", (N_NODES, D), mybir.dt.float32, kind="ExternalOutput").ap()
    gnn_kernel(nc, args, out)
    r = run_bass_kernel_spmd(nc, [arrays], core_ids=[0])
    return r.results[0]["out_0"]
```
